# Optimizing a Trainium2 kernel written in Bass

```python
import numpy as np
import jax
import jax.numpy as jnp

def _softmax(x, axis=-1):
    return jax.nn.softmax(x, axis=axis)

def _gelu(x):
    return jax.nn.gelu(x, approximate=True)

def _silu(x):
    return jax.nn.silu(x)

def _sigmoid(x):
    return jax.nn.sigmoid(x)

def _layernorm(x, axis=-1, eps=1e-05):
    m = jnp.mean(x, axis=axis, keepdims=True)
    v = jnp.var(x, axis=axis, keepdims=True)
    return (x - m) / jnp.sqrt(v + eps)

def _scatter_add(tgt, idx, src, axis=0):
    return tgt.at[idx].add(src)

def _segment_sum(src, seg, n):
    return jax.ops.segment_sum(src, seg, n)
kernel_name = 'mk_xattn_ffn_d2_seqx_r8_e2f99d'

def setup_inputs(seed: int=0):
    np.random.seed(seed)
    _w = jnp.asarray

    def _rec_inputs():
        import jax
        import jax.numpy as jnp
        _rk = jax.random.key(seed)
        x = -0.0002928 + 1 * jax.random.normal(jax.random.fold_in(_rk, 1), (4, 256, 256), jnp.float32)
        _lenS = 256 - jax.random.randint(jax.random.fold_in(_rk, 7), (4,), 0, max(1, 256 // 4) + 1, jnp.int32)
        _lenS2 = 256 - jax.random.randint(jax.random.fold_in(_rk, 8), (4,), 0, max(1, 256 // 4) + 1, jnp.int32)
        _ctx_2048P = jax.random.normal(jax.random.fold_in(_rk, 11), (4, 16, 256), jnp.float32)
        _ctx_2048c = jax.random.dirichlet(jax.random.fold_in(_rk, 511), 0.3 * jnp.ones((16,), jnp.float32), (4, 256))
        _ctx_2048t = jnp.einsum('bsk,bkd->bsd', _ctx_2048c, _ctx_2048P)
        _ctx_2048t = _ctx_2048t * jax.lax.rsqrt(jnp.mean(jnp.square(_ctx_2048t)) + 1e-12) * 0.953939
        ctx_2048 = -1.39393e-06 + 0.999914 * (_ctx_2048t + 0.3 * jax.random.normal(jax.random.fold_in(_rk, 611), (4, 256, 256), jnp.float32))
        _validS = jnp.arange(256)[None, :] < _lenS[:, None]
        _validS2 = jnp.arange(256)[None, :] < _lenS2[:, None]
        _causal = jnp.tril(jnp.ones((256, 256), dtype=bool))
        mask_BxS2_if1 = jnp.where(jnp.ones((4, 256), dtype=bool), 1, 0).astype(jnp.int32)
        return (x, ctx_2048, mask_BxS2_if1)
    x, ctx_2048, mask_BxS2_if1 = _rec_inputs()

    def _L0_xattn_setup():
        import jax, jax.numpy as jnp
        import numpy as np
        D_MODEL = 256
        N_HEADS = 32
        N_GROUPS = 8
        HEAD_DIM = D_MODEL // N_HEADS
        BATCH, SEQ = (2, 128)
        NEG_INF = float('-inf')
        key = jax.random.key(seed)
        ks = jax.random.split(key, 9)
        s = 0.02
        return {'Q': jax.random.normal(ks[0], (BATCH, SEQ, D_MODEL), jnp.float32), 'K': jax.random.normal(ks[1], (BATCH, SEQ, D_MODEL), jnp.float32), 'V': jax.random.normal(ks[2], (BATCH, SEQ, D_MODEL), jnp.float32), 'attention_mask': jnp.ones((BATCH, SEQ), jnp.int32), 'w_q': jax.random.normal(ks[3], (D_MODEL, D_MODEL), jnp.float32) * s, 'w_k': jax.random.normal(ks[4], (HEAD_DIM * N_GROUPS, D_MODEL), jnp.float32) * s, 'w_v': jax.random.normal(ks[5], (HEAD_DIM * N_GROUPS, D_MODEL), jnp.float32) * s, 'w_o': jax.random.normal(ks[6], (D_MODEL, D_MODEL), jnp.float32) * s, 'b_o': jnp.zeros((D_MODEL,), jnp.float32)}
    _L0_xattn_all = _L0_xattn_setup()
    _L0_xattn_in = {k: v for k, v in _L0_xattn_all.items() if k in ('w_q', 'w_k', 'w_v', 'w_o', 'b_o')}
    del _L0_xattn_all

    def _L0_ffn_setup():
        import jax, jax.numpy as jnp
        import numpy as np
        D_MODEL = 256
        HIDDEN = 704
        BATCH, SEQ = (4, 256)

        def _activation_quant(x):
            scale = 127.0 / jnp.clip(jnp.max(jnp.abs(x), axis=-1, keepdims=True), 1e-05, None)
            xq = jnp.clip(jnp.round(x * scale), -128.0, 127.0) / scale
            return x + jax.lax.stop_gradient(xq - x)

        def _weight_quant(w):
            scale = 1.0 / jnp.clip(jnp.mean(jnp.abs(w)), 1e-05, None)
            wq = jnp.clip(jnp.round(w * scale), -1.0, 1.0) / scale
            return w + jax.lax.stop_gradient(wq - w)

        def _bitlinear(x, w):
            return jnp.einsum('bsi,oi->bso', _activation_quant(x), _weight_quant(w))
        key = jax.random.key(seed)
        kx, k1, k2, k3 = jax.random.split(key, 4)
        x = jax.random.normal(kx, (BATCH, SEQ, D_MODEL), dtype=jnp.float32)
        w1 = jax.random.normal(k1, (HIDDEN, D_MODEL), dtype=jnp.float32) * 0.02
        w2 = jax.random.normal(k2, (HIDDEN, D_MODEL), dtype=jnp.float32) * 0.02
        w3 = jax.random.normal(k3, (D_MODEL, HIDDEN), dtype=jnp.float32) * 0.02
        return {'x': x, 'w1': w1, 'w2': w2, 'w3': w3}
    _L0_ffn_all = _L0_ffn_setup()
    _L0_ffn_in = {k: v for k, v in _L0_ffn_all.items() if k in ('w1', 'w2', 'w3')}
    del _L0_ffn_all

    def _L1_xattn_setup():
        import jax, jax.numpy as jnp
        import numpy as np
        HIDDEN = 256
        NUM_HEADS = 16
        NUM_KV_HEADS = 4
        HEAD_DIM = 128
        ROPE_THETA = 10000.0
        EPS = 1e-06

        def rms_norm(x, w, eps=EPS):
            var = jnp.mean(jnp.square(x), axis=-1, keepdims=True)
            return x * jax.lax.rsqrt(var + eps) * w

        def rope_cache(L, head_dim, theta, dtype):
            inv_freq = 1.0 / theta ** (jnp.arange(0, head_dim, 2, dtype=jnp.float32) / head_dim)
            t = jnp.arange(L, dtype=jnp.float32)
            freqs = jnp.outer(t, inv_freq)
            emb = jnp.concatenate([freqs, freqs], -1)
            cos = jnp.cos(emb).astype(dtype)[None, :, None, :]
            sin = jnp.sin(emb).astype(dtype)[None, :, None, :]
            return (cos, sin)

        def rotate_half(x):
            x1, x2 = jnp.split(x, 2, axis=-1)
            return jnp.concatenate([-x2, x1], axis=-1)
        key = jax.random.key(seed)
        ks = jax.random.split(key, 10)
        B, L, T = (2, 256, 64)
        q_out = NUM_HEADS * HEAD_DIM
        kv_out = NUM_KV_HEADS * HEAD_DIM
        s = lambda fan_in: 1.0 / np.sqrt(fan_in)
        return {'x': jax.random.normal(ks[0], (B, L, HIDDEN), jnp.float32), 'h_ctx_kv': jax.random.normal(ks[1], (B, T, HIDDEN), jnp.float32), 'wq': jax.random.normal(ks[2], (HIDDEN, q_out), jnp.float32) * s(HIDDEN), 'wk': jax.random.normal(ks[3], (HIDDEN, kv_out), jnp.float32) * s(HIDDEN), 'wv': jax.random.normal(ks[4], (HIDDEN, kv_out), jnp.float32) * s(HIDDEN), 'wo': jax.random.normal(ks[5], (q_out, HIDDEN), jnp.float32) * s(q_out), 'wk_ctx': jax.random.normal(ks[6], (HIDDEN, kv_out), jnp.float32) * s(HIDDEN), 'wv_ctx': jax.random.normal(ks[7], (HIDDEN, kv_out), jnp.float32) * s(HIDDEN), 'q_norm_w': jnp.ones((HEAD_DIM,), jnp.float32), 'k_norm_w': jnp.ones((HEAD_DIM,), jnp.float32)}
    _L1_xattn_all = _L1_xattn_setup()
    _L1_xattn_in = {k: v for k, v in _L1_xattn_all.items() if k in ('wq', 'wk', 'wv', 'wo', 'wk_ctx', 'wv_ctx', 'q_norm_w', 'k_norm_w')}
    del _L1_xattn_all

    def _L1_ffn_setup():
        import jax, jax.numpy as jnp
        import numpy as np
        B, S, H, I, E, K, R = (4, 128, 256, 896, 8, 2, 64)
        SCALING = 16.0 / 64.0
        key = jax.random.key(seed)
        ks = jax.random.split(key, 14)
        rn = lambda k, shape, sc: jax.random.normal(k, shape, jnp.float32) * sc
        x = rn(ks[0], (B, S, H), 1.0)
        expert_wealth = jnp.full((E,), 100.0, jnp.float32)
        conf_W = rn(ks[1], (E, H), 0.02)
        conf_b = ((jnp.arange(E) - E / 2.0) * 0.1).astype(jnp.float32)
        base_gate = rn(ks[2], (H, I), H ** (-0.5))
        base_up = rn(ks[3], (H, I), H ** (-0.5))
        base_down = rn(ks[4], (I, H), I ** (-0.5))
        gate_A = rn(ks[5], (E, H, R), H ** (-0.5))
        gate_B = rn(ks[6], (E, R, I), 0.01)
        up_A = rn(ks[7], (E, H, R), H ** (-0.5))
        up_B = rn(ks[8], (E, R, I), 0.01)
        down_A = rn(ks[9], (E, I, R), I ** (-0.5))
        down_B = rn(ks[10], (E, R, H), 0.01)
        return {'hidden_states': x, 'expert_wealth': expert_wealth, 'conf_W': conf_W, 'conf_b': conf_b, 'base_gate': base_gate, 'base_up': base_up, 'base_down': base_down, 'gate_A': gate_A, 'gate_B': gate_B, 'up_A': up_A, 'up_B': up_B, 'down_A': down_A, 'down_B': down_B}
    _L1_ffn_all = _L1_ffn_setup()
    _L1_ffn_in = {k: v for k, v in _L1_ffn_all.items() if k in ('expert_wealth', 'conf_W', 'conf_b', 'base_gate', 'base_up', 'base_down', 'gate_A', 'gate_B', 'up_A', 'up_B', 'down_A', 'down_B')}
    del _L1_ffn_all
    return {'x': x, 'ctx_2048': ctx_2048, 'mask_BxS2_if1': mask_BxS2_if1, 'L0_xattn_w_q': _L0_xattn_in['w_q'], 'L0_xattn_w_k': _L0_xattn_in['w_k'], 'L0_xattn_w_v': _L0_xattn_in['w_v'], 'L0_xattn_w_o': _L0_xattn_in['w_o'], 'L0_xattn_b_o': _L0_xattn_in['b_o'], 'L0_ffn_w1': _L0_ffn_in['w1'], 'L0_ffn_w2': _L0_ffn_in['w2'], 'L0_ffn_w3': _L0_ffn_in['w3'], 'L1_xattn_wq': _L1_xattn_in['wq'], 'L1_xattn_wk': _L1_xattn_in['wk'], 'L1_xattn_wv': _L1_xattn_in['wv'], 'L1_xattn_wo': _L1_xattn_in['wo'], 'L1_xattn_wk_ctx': _L1_xattn_in['wk_ctx'], 'L1_xattn_wv_ctx': _L1_xattn_in['wv_ctx'], 'L1_xattn_q_norm_w': _L1_xattn_in['q_norm_w'], 'L1_xattn_k_norm_w': _L1_xattn_in['k_norm_w'], 'L1_ffn_expert_wealth': _L1_ffn_in['expert_wealth'], 'L1_ffn_conf_W': _L1_ffn_in['conf_W'], 'L1_ffn_conf_b': _L1_ffn_in['conf_b'], 'L1_ffn_base_gate': _L1_ffn_in['base_gate'], 'L1_ffn_base_up': _L1_ffn_in['base_up'], 'L1_ffn_base_down': _L1_ffn_in['base_down'], 'L1_ffn_gate_A': _L1_ffn_in['gate_A'], 'L1_ffn_gate_B': _L1_ffn_in['gate_B'], 'L1_ffn_up_A': _L1_ffn_in['up_A'], 'L1_ffn_up_B': _L1_ffn_in['up_B'], 'L1_ffn_down_A': _L1_ffn_in['down_A'], 'L1_ffn_down_B': _L1_ffn_in['down_B']}

def reference(x, ctx_2048, mask_BxS2_if1, L0_xattn_w_q, L0_xattn_w_k, L0_xattn_w_v, L0_xattn_w_o, L0_xattn_b_o, L0_ffn_w1, L0_ffn_w2, L0_ffn_w3, L1_xattn_wq, L1_xattn_wk, L1_xattn_wv, L1_xattn_wo, L1_xattn_wk_ctx, L1_xattn_wv_ctx, L1_xattn_q_norm_w, L1_xattn_k_norm_w, L1_ffn_expert_wealth, L1_ffn_conf_W, L1_ffn_conf_b, L1_ffn_base_gate, L1_ffn_base_up, L1_ffn_base_down, L1_ffn_gate_A, L1_ffn_gate_B, L1_ffn_up_A, L1_ffn_up_B, L1_ffn_down_A, L1_ffn_down_B):
    import jax
    import jax.numpy as jnp

    def _L0_xattn_ref(Q, K, V, attention_mask, w_q, w_k, w_v, w_o, b_o):
        import jax, jax.numpy as jnp
        import numpy as np
        D_MODEL = 256
        N_HEADS = 32
        N_GROUPS = 8
        HEAD_DIM = D_MODEL // N_HEADS
        BATCH, SEQ = (2, 128)
        NEG_INF = float('-inf')
        B, S, D = Q.shape
        G, HG, HD = (N_GROUPS, N_HEADS // N_GROUPS, HEAD_DIM)
        q = (Q @ w_q.T).reshape(B, S, G, HG, HD)
        k = (K @ w_k.T).reshape(B, S, G, HD)
        v = (V @ w_v.T).reshape(B, S, G, HD)
        scale = jnp.sqrt(jnp.float32(HD))
        scores = jnp.einsum('bnghd,bmgd->bnghm', q, k) / scale
        pad = (attention_mask == 0)[:, None, None, None, :]
        scores = jnp.where(pad, NEG_INF, scores)
        causal = jnp.tril(jnp.ones((S, S), bool))[None, :, None, None, :]
        scores = jnp.where(causal, scores, NEG_INF)
        attn = jax.nn.softmax(scores, axis=-1)
        out = jnp.einsum('bnghm,bmgd->bnghd', attn, v).reshape(B, S, D)
        return out @ w_o.T + b_o

    def _L0_ffn_ref(x, w1, w2, w3):
        import jax, jax.numpy as jnp
        import numpy as np
        D_MODEL = 256
        HIDDEN = 704
        BATCH, SEQ = (4, 256)

        def _activation_quant(x):
            scale = 127.0 / jnp.clip(jnp.max(jnp.abs(x), axis=-1, keepdims=True), 1e-05, None)
            xq = jnp.clip(jnp.round(x * scale), -128.0, 127.0) / scale
            return x + jax.lax.stop_gradient(xq - x)

        def _weight_quant(w):
            scale = 1.0 / jnp.clip(jnp.mean(jnp.abs(w)), 1e-05, None)
            wq = jnp.clip(jnp.round(w * scale), -1.0, 1.0) / scale
            return w + jax.lax.stop_gradient(wq - w)

        def _bitlinear(x, w):
            return jnp.einsum('bsi,oi->bso', _activation_quant(x), _weight_quant(w))
        h = jax.nn.silu(_bitlinear(x, w1)) * _bitlinear(x, w2)
        return _bitlinear(h, w3)

    def _L1_xattn_ref(x, h_ctx_kv, wq, wk, wv, wo, wk_ctx, wv_ctx, q_norm_w, k_norm_w):
        import jax, jax.numpy as jnp
        import numpy as np
        HIDDEN = 256
        NUM_HEADS = 16
        NUM_KV_HEADS = 4
        HEAD_DIM = 128
        ROPE_THETA = 10000.0
        EPS = 1e-06

        def rms_norm(x, w, eps=EPS):
            var = jnp.mean(jnp.square(x), axis=-1, keepdims=True)
            return x * jax.lax.rsqrt(var + eps) * w

        def rope_cache(L, head_dim, theta, dtype):
            inv_freq = 1.0 / theta ** (jnp.arange(0, head_dim, 2, dtype=jnp.float32) / head_dim)
            t = jnp.arange(L, dtype=jnp.float32)
            freqs = jnp.outer(t, inv_freq)
            emb = jnp.concatenate([freqs, freqs], -1)
            cos = jnp.cos(emb).astype(dtype)[None, :, None, :]
            sin = jnp.sin(emb).astype(dtype)[None, :, None, :]
            return (cos, sin)

        def rotate_half(x):
            x1, x2 = jnp.split(x, 2, axis=-1)
            return jnp.concatenate([-x2, x1], axis=-1)
        B, L, _ = x.shape
        T = h_ctx_kv.shape[1]
        rep = NUM_HEADS // NUM_KV_HEADS
        q = (x @ wq).reshape(B, L, NUM_HEADS, HEAD_DIM)
        k = (x @ wk).reshape(B, L, NUM_KV_HEADS, HEAD_DIM)
        v = (x @ wv).reshape(B, L, NUM_KV_HEADS, HEAD_DIM)
        q = rms_norm(q, q_norm_w)
        k = rms_norm(k, k_norm_w)
        k_ctx = (h_ctx_kv @ wk_ctx).reshape(B, T, NUM_KV_HEADS, HEAD_DIM)
        v_ctx = (h_ctx_kv @ wv_ctx).reshape(B, T, NUM_KV_HEADS, HEAD_DIM)
        k_ctx = rms_norm(k_ctx, k_norm_w)
        cos, sin = rope_cache(L, HEAD_DIM, ROPE_THETA, x.dtype)
        q = q * cos + rotate_half(q) * sin
        k = k * cos + rotate_half(k) * sin
        k_full = jnp.concatenate([k_ctx, k], axis=1)
        v_full = jnp.concatenate([v_ctx, v], axis=1)
        k_full = jnp.repeat(k_full, rep, axis=2)
        v_full = jnpp_repeat = jnp.repeat(v_full, rep, axis=2)
        i = jnp.arange(L)[:, None]
        j = jnp.arange(L)[None, :]
        causal = jnp.where(j > i, -jnp.inf, 0.0).astype(x.dtype)
        mask = jnp.concatenate([jnp.zeros((L, T), x.dtype), causal], axis=1)
        scale = 1.0 / np.sqrt(HEAD_DIM)
        scores = jnp.einsum('blhd,bmhd->bhlm', q, k_full) * scale + mask
        probs = jax.nn.softmax(scores, axis=-1)
        out = jnp.einsum('bhlm,bmhd->blhd', probs, v_full)
        out = out.reshape(B, L, NUM_HEADS * HEAD_DIM)
        return out @ wo

    def _L1_ffn_ref(hidden_states, expert_wealth, conf_W, conf_b, base_gate, base_up, base_down, gate_A, gate_B, up_A, up_B, down_A, down_B):
        import jax, jax.numpy as jnp
        import numpy as np
        B, S, H, I, E, K, R = (4, 128, 256, 896, 8, 2, 64)
        SCALING = 16.0 / 64.0
        x = hidden_states
        conf = jax.nn.sigmoid(jnp.einsum('bsh,eh->bse', x, conf_W) + conf_b)
        bids = conf * expert_wealth
        top_bids, sel = jax.lax.top_k(bids, K)
        routing = jax.nn.softmax(top_bids, axis=-1)
        base_g = jnp.einsum('bsh,hi->bsi', x, base_gate)
        base_u = jnp.einsum('bsh,hi->bsi', x, base_up)
        out = jnp.zeros_like(x)
        for e in range(E):
            g = base_g + x @ gate_A[e] @ gate_B[e] * SCALING
            u = base_u + x @ up_A[e] @ up_B[e] * SCALING
            h = jax.nn.silu(g) * u
            oe = h @ base_down + h @ down_A[e] @ down_B[e] * SCALING
            we = jnp.sum(routing * (sel == e), axis=-1)
            out = out + we[..., None] * oe
        return out
    x = x + _L0_xattn_ref(_layernorm(x, axis=-1), ctx_2048, ctx_2048, mask_BxS2_if1, L0_xattn_w_q, L0_xattn_w_k, L0_xattn_w_v, L0_xattn_w_o, L0_xattn_b_o)
    x = x + _L0_ffn_ref(_layernorm(x, axis=-1), L0_ffn_w1, L0_ffn_w2, L0_ffn_w3)
    x = x + _L1_xattn_ref(_layernorm(x, axis=-1), ctx_2048, L1_xattn_wq, L1_xattn_wk, L1_xattn_wv, L1_xattn_wo, L1_xattn_wk_ctx, L1_xattn_wv_ctx, L1_xattn_q_norm_w, L1_xattn_k_norm_w)
    x = x + _L1_ffn_ref(_layernorm(x, axis=-1), L1_ffn_expert_wealth, L1_ffn_conf_W, L1_ffn_conf_b, L1_ffn_base_gate, L1_ffn_base_up, L1_ffn_base_down, L1_ffn_gate_A, L1_ffn_gate_B, L1_ffn_up_A, L1_ffn_up_B, L1_ffn_down_A, L1_ffn_down_B)
    return x

_drawn_inputs = setup_inputs


def setup_inputs(seed=0):
    import zlib

    import numpy as np

    out = dict(_drawn_inputs(seed))
    spreads = {'L0_xattn_b_o': (0.0, 0.1),
     'L1_xattn_q_norm_w': (1.0, 0.2),
     'L1_xattn_k_norm_w': (1.0, 0.2),
     'L1_ffn_expert_wealth': (100.0, 0.6)}
    factors = {'L0_xattn_w_q': 8.0,
     'L0_xattn_w_k': 8.0,
     'L0_ffn_w1': 5.757,
     'L0_ffn_w2': 5.182,
     'L0_ffn_w3': 5.101,
     'L1_ffn_conf_W': 4.952,
     'L1_ffn_conf_b': 4.418,
     'L1_ffn_gate_A': 5.972,
     'L1_ffn_gate_B': 5.934,
     'L1_ffn_up_A': 6.069,
     'L1_ffn_up_B': 6.02,
     'L1_ffn_down_A': 6.133,
     'L1_ffn_down_B': 6.168}
    for name, (base, spread) in spreads.items():
        noise = np.random.default_rng([zlib.crc32(name.encode()), seed]).standard_normal(out[name].shape)
        drawn = base * np.exp(spread * noise) if base else spread * noise
        out[name] = jnp.asarray(drawn.astype(out[name].dtype))
    for name, factor in factors.items():
        out[name] = (out[name] * factor).astype(out[name].dtype)
    return out
```

```python
import numpy as np
import concourse.bass as bass
from concourse import mybir
from contextlib import ExitStack

F32 = mybir.dt.float32
BF16 = mybir.dt.bfloat16
I32 = mybir.dt.int32
ALU = mybir.AluOpType
ACT = mybir.ActivationFunctionType
AX = mybir.AxisListType
ds = bass.ds

P = 128
B, S, D = 4, 256, 256
NT = B * S // P
TB = S // P
KD = D // P
NEG = -1e30
MAGIC = 12582912.0

G0, HG0, HD0 = 8, 4, 8
HALF = G0 // 2
NPART = 3
Q_TERM = (0, 0, 1, 1, 0, 2)
K_TERM = (0, 1, 0, 1, 2, 0)
ROW_M, ROW_PAD = 48, 49
HID0 = 704
HT0 = 6

H1, KV1, HD1 = 16, 4, 128
REP1 = H1 // KV1
T1 = 256
CH = 512
E1, R1, HID1 = 8, 64, 896
MT1 = HID1 // P
ET1 = E1 * R1 // P
SCALING = 0.25


class Chain:

    def __init__(self, eng, sem, i, per):
        self.eng, self.sem, self.i, self.per, self.k = eng, sem, i, per, 0

    def add(self, ins):
        ins.then_inc(self.sem, 1)
        self.k += 1

    def wait(self):
        self.eng.wait_ge(self.sem, self.i * self.per + self.k)

    def link(self, ins):
        self.add(ins)
        self.wait()

    def pause(self):
        self.wait()
        self.eng.sem_inc(self.sem, 1)
        self.k += 1

    def done(self):
        assert self.k == self.per, f"{self.sem}: the body adds {self.k}"


class Program:
    def __init__(self, nc, args):
        self.nc, self.a = nc, args
        self.top = ExitStack()
        self.attention = ExitStack()

    def sb(self, name, shape, dt=F32, ctx=None):
        return (ctx or self.top).enter_context(self.nc.sbuf_tensor(name, shape, dt))

    def ps(self, name, shape, ctx, dt=F32):
        return ctx.enter_context(self.nc.psum_tensor(name, shape, dt))

    def sems(self, ctx, names):
        return [ctx.enter_context(self.nc.semaphore(n)) for n in names.split()]


def layernorm(v, x, stats, mv, xn, rs, ln_var, ln_sd, chain, ready, it):
    for t in range(TB):
        chain.add(v.bn_stats(stats[:, t, :], x(t)))
    chain.pause()
    for t in range(TB):
        last = v.bn_aggr(mv[:, t, :], stats[:, t, :])
        if t == TB - 1:
            last.then_inc(ln_var, 1)
        else:
            chain.add(last)
    v.wait_ge(ln_sd, it + 1)
    chain.link(v.reciprocal(rs[:, TB:2 * TB], rs[:, 0:TB]))
    for t in range(TB):
        ins = v.tensor_scalar(xn[:, t, :], x(t), mv[:, t, 0:1], rs[:, TB + t:TB + t + 1], ALU.subtract, ALU.mult)
        if t == TB - 1:
            ins.then_inc(ready, 1)
        else:
            chain.add(ins)


def split_weights(g, chunks, raw, s_in, s_out):
    def load(n):
        src, hi, lo, view = chunks[n]
        g.dma_start(view(raw[n % 2]), src).then_inc(s_in[n % 2], 16)
        g.dma_start(hi, src).then_inc(s_in[n % 2], 16)

    load(0)
    for n, (src, hi, lo, view) in enumerate(chunks):
        if n + 1 < len(chunks):
            if n >= 1:
                g.wait_ge(s_out, n)
            load(n + 1)
        g.wait_ge(s_in[n % 2], 32 * (n // 2 + 1))
        g.tensor_tensor(lo, view(raw[n % 2]), hi, ALU.subtract).then_inc(s_out, 1)
    g.wait_ge(s_out, len(chunks))


def setup(p):
    nc, a = p.nc, p.a
    p.X = p.sb("X", [P, NT, D])
    p.identf = p.sb("identf", [P, P])
    p.identb = p.sb("identb", [P, P], BF16)
    p.eps = p.sb("eps", [P, 3])
    p.ones1 = p.sb("ones1", [1, P])
    p.ln_stats = p.sb("ln_stats", [P, TB, 6])
    p.ln_mv = p.sb("ln_mv", [P, TB, 2])
    p.ln_rs = p.sb("ln_rs", [P, 2 * TB])
    p.xn = p.sb("xn", [P, TB, D])
    p.CTS = p.sb("CTS", [P, 2, KD, B * S], BF16, p.attention)
    p.WQ = p.sb("WQ", [P, 2, KD, H1 * HD1], BF16, p.attention)
    p.WKV = p.sb("WKV", [P, 2, KD, 2, 2 * KV1 * HD1], BF16, p.attention)
    p.WO = p.sb("WO", [P, 2, H1, D], BF16, p.attention)


def first_attention(p):
    nc, a = p.nc, p.a
    with ExitStack() as c:
        sb = lambda n, s, dt=F32: p.sb(n, s, dt, c)
        wq = sb("wq0", [P, KD, D])
        wo = sb("wo0", [P, KD, D])
        bo = sb("bo0", [1, D])
        Vaug = sb("Vaug", [P, NT, G0, 32])
        Qst = sb("Qst", [P, B, 2, 8, S], BF16)
        Kst = sb("Kst", [P, B, 2, 2, HALF, S], BF16)
        triA = sb("triA", [P, 2, S], BF16)
        triB = sb("triB", [P, 2, S], BF16)
        k_scr = nc.dram_tensor("k_scr", [B, NPART, HD0, 2 * HALF * S], BF16).ap()
        q_scr = nc.dram_tensor("q_scr", [B, NPART, 2, P, S], BF16).ap()
        bank = [p.ps(f"a{i}", [P, 512], c) for i in range(8)]

        with ExitStack() as c1:
            CT = p.sb("CT", [P, KD, B * S], F32, c1)
            wk = p.sb("wk0", [P, KD, G0 * HD0], F32, c1)
            wv = p.sb("wv0", [P, KD, G0 * HD0], F32, c1)
            mask_i = p.sb("mask_i", [P, NT], I32, c1)
            mask_r = p.sb("mask_r", [1, B * S], I32, c1)
            valid = p.sb("valid", [P, NT], F32, c1)
            pad_row = p.sb("pad_row", [1, B * S], BF16, c1)
            one_row = p.sb("one_row", [1, B * 16 * S // 4], BF16, c1)
            kp = p.sb("kp", [G0 * HD0, NPART, B * S], BF16, c1)
            kr = p.sb("kr", [G0 * HD0, 2, 512], F32, c1)
            (s_x, s_ct, s_w, s_small, s_cst, s_eng, s_v, s_vd, s_k, s_khi, s_kr, s_kdr, s_kfree, s_kout, s_kin, s_rows, s_zero,
             s_valid, s_va, s_dch, s_cts) = p.sems(c1, "x0 ct0 w0 small0 cst0 eng0 v0 vd0 k0 khi0 kr0 kdr0 kfree0 kout0 kin0 rows0 zero0 valid0 va0 dch0 cts0")
            with nc.Block() as block:
                @block.sync
                def _(sp):
                    sp.dma_start(CT[:, :, :], a["ctxT"].rearrange("(k p) n -> p k n", p=P)).then_inc(s_ct, 16)
                    sp.dma_start(wk[:, :, :], a["wk0T"].rearrange("(k p) n -> p k n", p=P)).then_inc(s_w, 16)
                    sp.dma_start(wv[:, :, :], a["wv0T"].rearrange("(k p) n -> p k n", p=P)).then_inc(s_w, 16)
                    sp.dma_start(mask_i[:, :], a["mask_tok"]).then_inc(s_w, 16)
                    sp.dma_start(mask_r[:, :], a["mask_row"]).then_inc(s_w, 16)
                    sp.dma_start(p.X[:, :, :], a["x"].rearrange("(t p) d -> p t d", p=P)).then_inc(s_x, 16)
                    sp.dma_start(wq[:, :, :], a["wq0T"].rearrange("(k p) n -> p k n", p=P)).then_inc(s_x, 16)
                    sp.dma_start(wo[:, :, :], a["wo0T"].rearrange("(k p) n -> p k n", p=P)).then_inc(s_x, 16)
                    sp.dma_start(bo[:, :], a["bo0"]).then_inc(s_x, 16)
                    sp.wait_ge(s_kr, 6)
                    for b in range(B):
                        sp.dma_start(k_scr[b].rearrange("a d (g t) -> (d g) a t", t=S), kp[:, :, b * S:(b + 1) * S]).then_inc(s_kout, 16)
                    sp.wait_ge(s_kout, 16 * B)
                    sp.wait_ge(s_zero, 2)
                    for e in range(2):
                        for t in range(6):
                            sp.dma_start(Kst[64 * e + 8 * t:64 * e + 8 * t + 8, :, e, :, :, :].rearrange("p b h j n -> p b (h j n)"),
                                         k_scr[:, K_TERM[t], :, :].rearrange("b d n -> d b n")).then_inc(s_kin, 16)
                    sp.wait_ge(s_kin, 16 * 12)
                    sp.wait_ge(s_x, 64)

                @block.scalar
                def _(act):
                    act.wait_ge(s_zero, 2)
                    act.wait_ge(s_valid, 2)
                    for e in range(2):
                        for b in range(B):
                            act.dma_start(Kst[64 * e + ROW_M:64 * e + ROW_M + 1, b, e, :, :, :],
                                          one_row[0:1, 0:2048].rearrange("p (h j n) -> p h j n", h=2, j=HALF)).then_inc(s_rows, 16)
                            act.dma_start(Qst[64 * e + ROW_PAD:64 * e + ROW_PAD + 1, b, :, :, :],
                                          one_row[0:1, 0:4096].rearrange("p (h j n) -> p h j n", h=2, j=8)).then_inc(s_rows, 16)
                            for h in range(2):
                                for j in range(HALF):
                                    act.dma_start(Kst[64 * e + ROW_PAD:64 * e + ROW_PAD + 1, b, e, h, j, :],
                                                  pad_row[0:1, b * S:(b + 1) * S]).then_inc(s_rows, 16)
                    for n in range(2):
                        act.wait_ge(s_k, n + 1)
                        act.activation(kp[:, 0, n * 512:(n + 1) * 512], bank[2 + n][0:64, :], ACT.Copy).then_inc(s_khi, 1)
                    act.wait_ge(s_rows, 16 * 2 * B * 10)

                @block.gpsimd
                def _(g):
                    g.memset(p.identf[:, :], 0.0).then_inc(s_eng, 1)
                    g.memset(p.identb[:, :], 0.0).then_inc(s_eng, 1)
                    g.memset(triA[:, :, :], 0.0).then_inc(s_eng, 1)
                    g.memset(triB[:, :, :], 0.0).then_inc(s_eng, 1)
                    g.wait_ge(s_eng, 4)
                    for m in (p.identf, p.identb):
                        g.affine_select(out=m[:, :], in_=m[:, :], compare_op=ALU.not_equal, fill=1.0, base=0,
                                        pattern=[[-1, P]], channel_multiplier=1).then_inc(s_eng, 1)
                    g.affine_select(out=triA[:, :, P:S], in_=triA[:, :, P:S], compare_op=ALU.is_ge, fill=NEG, base=0,
                                    pattern=[[0, 2], [-1, P]], channel_multiplier=1).then_inc(s_eng, 1)
                    g.affine_select(out=triB[:, :, 0:P], in_=triB[:, :, 0:P], compare_op=ALU.is_ge, fill=NEG, base=0,
                                    pattern=[[0, 2], [1, P]], channel_multiplier=-1).then_inc(s_eng, 1)
                    g.memset(p.eps[:, 0:1], 1e-5).then_inc(s_eng, 1)
                    g.memset(p.eps[:, 1:2], HD1 * 1e-6).then_inc(s_eng, 1)
                    g.memset(p.eps[:, 2:3], 1e-6).then_inc(s_eng, 1)
                    g.memset(p.ones1[:, :], 1.0).then_inc(s_eng, 1)

                @block.vector
                def _(v):
                    v.memset(Qst[:, :, :, :, :].rearrange("p b h j n -> p (b h j n)").bitcast(F32), 0.0).then_inc(s_zero, 1)
                    v.memset(Kst[:, :, :, :, :, :].rearrange("p b e h j n -> p (b e h j n)").bitcast(F32), 0.0).then_inc(s_zero, 1)
                    v.memset(one_row[:, :], 1.0).then_inc(s_valid, 1)
                    v.memset(Vaug[:, :, :, :], 0.0).then_inc(s_dch, 1)
                    v.wait_ge(s_w, 64)
                    v.tensor_scalar(pad_row[:, :], mask_r[:, :], 0.0, NEG, ALU.is_equal, ALU.mult).then_inc(s_valid, 1)
                    v.tensor_scalar(valid[:, :], mask_i[:, :], 0.0, None, ALU.not_equal).then_inc(s_dch, 1)
                    v.wait_ge(s_dch, 2)
                    v.wait_ge(s_v, 1)
                    v.tensor_tensor(Vaug[:, :, :, 0:8], bank[0][:, :].rearrange("p (t g d) -> p t g d", t=NT, g=G0),
                                    valid[:, :].rearrange("p (t a b) -> p t a b", a=1, b=1).broadcast_to([P, NT, G0, 8]),
                                    ALU.mult).then_inc(s_va, 1)
                    v.tensor_copy(Vaug[:, :, :, 8:9], valid[:, :].rearrange("p (t a b) -> p t a b", a=1, b=1).broadcast_to([P, NT, G0, 1])).then_inc(s_va, 1)
                    for n in range(2):
                        cols = slice(n * 512, (n + 1) * 512)
                        v.wait_ge(s_khi, n + 1)
                        v.tensor_tensor(kr[:, n, :], bank[2 + n][0:64, :], kp[:, 0, cols], ALU.subtract).then_inc(s_kr, 1)
                        v.wait_ge(s_kr, 3 * n + 1)
                        v.tensor_copy(kp[:, 1, cols], kr[:, n, :]).then_inc(s_kr, 1)
                        v.wait_ge(s_kr, 3 * n + 2)
                        v.tensor_tensor(kp[:, 2, cols], kr[:, n, :], kp[:, 1, cols], ALU.subtract).then_inc(s_kr, 1)
                    v.tensor_copy(p.CTS[:, 0, :, :], CT[:, :, :]).then_inc(s_cts, 1)
                    v.wait_ge(s_cts, 1)
                    v.tensor_tensor(p.CTS[:, 1, :, :], CT[:, :, :], p.CTS[:, 0, :, :], ALU.subtract).then_inc(s_cts, 1)

                @block.tensor
                def _(pe):
                    pe.wait_ge(s_ct, 16)
                    pe.wait_ge(s_w, 64)
                    for n in range(2):
                        for k in range(KD):
                            mm = pe.matmul(bank[2 + n][0:64, :], wk[:, k, :], CT[:, k, n * 512:(n + 1) * 512],
                                           start=(k == 0), stop=(k == KD - 1))
                        mm.then_inc(s_k, 1)
                    for t in range(NT):
                        for k in range(KD):
                            mm = pe.matmul(bank[0][:, t * 64:(t + 1) * 64], CT[:, k, t * P:(t + 1) * P], wv[:, k, :],
                                           start=(k == 0), stop=(k == KD - 1))
                    mm.then_inc(s_v, 1)

        with ExitStack() as c2:
            raw = p.sb("raw", [P, 2, 2048], F32, c2)
            xT = p.sb("xT", [P, KD, S], F32, c2)
            qp = p.sb("qp", [P, NPART, 2, S], BF16, c2)
            qr = p.sb("qr", [P, 2, S], F32, c2)
            (s_var, s_sd, s_xn, s_dch, s_tr, s_xT, s_q, s_qhi, s_qp, s_qr, s_qout, s_qin, s_in0, s_in1, s_split) = \
                p.sems(c2, "var1 sd1 xn1 dch1 tr1 xT1 q1 qhi1 qp1 qr1 qout1 qin1 in01 in11 split1")
            with nc.Block() as block:
                @block.gpsimd
                def _(g):
                    chunks = []
                    for k in range(KD):
                        rows = slice(k * P, (k + 1) * P)
                        chunks.append((a["wq1"][rows, :], p.WQ[:, 0, k, :], p.WQ[:, 1, k, :], lambda r: r))
                        chunks.append((a["wkv1"][rows, :], p.WKV[:, 0, k, :, :].rearrange("p w n -> p (w n)"),
                                       p.WKV[:, 1, k, :, :].rearrange("p w n -> p (w n)"), lambda r: r))
                    for m in range(0, H1, 8):
                        chunks.append((a["wo1"][m * P:(m + 8) * P, :].rearrange("(m p) n -> p m n", p=P),
                                       p.WO[:, 0, m:m + 8, :], p.WO[:, 1, m:m + 8, :], lambda r: r.rearrange("p (m n) -> p m n", m=8)))
                    split_weights(g, chunks, [raw[:, 0, :], raw[:, 1, :]], (s_in0, s_in1), s_split)

                @block.sync
                def _(sp):
                    with sp.Fori(0, B) as b:
                        sp.wait_ge(s_qp, b * 3 + 3)
                        sp.dma_start(q_scr[ds(b, 1), :, :, :, :].rearrange("o a h p t -> p (o a h) t"),
                                     qp[:, :, :, :].rearrange("p a h t -> p (a h) t")).then_inc(s_qout, 16)
                        sp.wait_ge(s_qout, b * 16 + 16)
                        for e in range(2):
                            for t in range(6):
                                r = 64 * e + 8 * t
                                sp.dma_start(Qst[r:r + 8, ds(b, 1), :, :, :].rearrange("p o h j n -> p (o h) (j n)"),
                                             q_scr[ds(b, 1), Q_TERM[t], :, 64 * e:64 * e + 64, :].rearrange("o h (d j) t -> d (o h) (j t)", d=8)).then_inc(s_qin, 16)
                    sp.wait_ge(s_qin, 192 * B)

                @block.scalar
                def _(act):
                    with act.Fori(0, B) as b:
                        act.wait_ge(s_var, b + 1)
                        act.activation(p.ln_rs[:, 0:TB], p.ln_mv[:, :, 1], ACT.Sqrt, bias=p.eps[:, 0:1]).then_inc(s_sd, 1)
                        act.wait_ge(s_tr, b + 1)
                        act.activation(xT[:, :, :], bank[0][:, :].rearrange("p (k n) -> p k n", k=KD), ACT.Copy).then_inc(s_xT, 1)
                        act.wait_ge(s_q, b + 1)
                        act.activation(qp[:, 0, :, :], bank[1][:, :].rearrange("p (h n) -> p h n", h=2), ACT.Copy,
                                       scale=HD0 ** -0.5).then_inc(s_qhi, 1)

                @block.vector
                def _(v):
                    with v.Fori(0, B) as b:
                        ch = Chain(v, s_dch, b, 6)
                        layernorm(v, lambda t: p.X[:, ds(2 * b + t, 1), :].rearrange("p o n -> p (o n)"),
                                  p.ln_stats, p.ln_mv, p.xn, p.ln_rs, s_var, s_sd, ch, s_xn, b)
                        ch.done()
                        v.wait_ge(s_qhi, b + 1)
                        psq = bank[1][:, :].rearrange("p (h n) -> p h n", h=2)
                        v.scalar_tensor_tensor(qr[:, :, :], psq, HD0 ** -0.5, qp[:, 0, :, :], ALU.mult, ALU.subtract).then_inc(s_qp, 1)
                        v.wait_ge(s_qp, b * 3 + 1)
                        v.tensor_copy(qp[:, 1, :, :], qr[:, :, :]).then_inc(s_qp, 1)
                        v.wait_ge(s_qp, b * 3 + 2)
                        v.tensor_tensor(qp[:, 2, :, :], qr[:, :, :], qp[:, 1, :, :], ALU.subtract).then_inc(s_qp, 1)
                        v.wait_ge(s_qin, b * 192 + 192)

                @block.tensor
                def _(pe):
                    with pe.Fori(0, B) as b:
                        pe.wait_ge(s_xn, b + 1)
                        for k in range(KD):
                            for t in range(TB):
                                mm = pe.transpose(bank[0][:, k * S + t * P:k * S + (t + 1) * P], p.xn[:, t, k * P:(k + 1) * P], p.identf[:, :])
                        mm.then_inc(s_tr, 1)
                        pe.wait_ge(s_xT, b + 1)
                        for h in range(2):
                            for k in range(KD):
                                mm = pe.matmul(bank[1][:, h * S:(h + 1) * S], wq[:, k, h * P:(h + 1) * P], xT[:, k, :],
                                               start=(k == 0), stop=(k == KD - 1))
                        mm.then_inc(s_q, 1)

        with ExitStack() as c3:
            NM = p.sb("NM", [P, 2, 2, 2, HALF, 2], F32, c3)
            nmT = p.sb("nmT", [64, P], BF16, c3)
            (s_a, s_fa, s_held, s_nt, s_nmT, s_ndma, s_nfree) = p.sems(c3, "a2 fa2 held2 nt2 nmT2 ndma2 nfree2")
            with nc.Block() as block:
                @block.sync
                def _(sp):
                    sp.sem_inc(s_nfree, 1)
                    with sp.Fori(0, B) as b:
                        sp.wait_ge(s_nmT, b + 1)
                        for e in range(2):
                            for qb in range(2):
                                r = 64 * e + ROW_M
                                sp.dma_start(Qst[r:r + 1, ds(b, 1), :, :, qb * P:(qb + 1) * P].rearrange("p o h j n -> p (o h j) n"),
                                             nmT[(2 * e + qb) * 16:(2 * e + qb) * 16 + 16, :]).then_inc(s_ndma, 16)
                        sp.wait_ge(s_ndma, b * 64 + 64)
                        sp.sem_inc(s_nfree, 1)

                @block.scalar
                def _(act):
                    with act.Fori(0, B) as b:
                        act.wait_ge(s_nt, b + 1)
                        act.wait_ge(s_nfree, b + 1)
                        act.activation(nmT[:, :], bank[6][0:64, 0:P], ACT.Copy).then_inc(s_nmT, 1)

                @block.vector
                def _(v):
                    v.sem_inc(s_fa, 2)
                    with v.Fori(0, B) as b:
                        for h in range(2):
                            for j in range(HALF):
                                n = h * HALF + j
                                o = 3 * (n % 2)
                                v.wait_ge(s_a, b * 8 + n + 1)
                                v.tensor_reduce(NM[:, :, 0, h, j, :].rearrange("p e q -> p q e"),
                                                bank[o][:, :].rearrange("p (q e n) -> p q e n", q=2, e=2), AX.X, ALU.max, negate=True)
                                for pp in range(2):
                                    last = v.tensor_reduce(NM[:, :, 1, h, j, pp], bank[o + 1 + pp][:, :].rearrange("p (e n) -> p e n", e=2),
                                                           AX.X, ALU.max, negate=True)
                                last.then_inc(s_fa, 1)

                @block.tensor
                def _(pe):
                    with pe.Fori(0, B) as b:
                        for h in range(2):
                            for j in range(HALF):
                                n = h * HALF + j
                                o = 3 * (n % 2)
                                pe.wait_ge(s_fa, b * 8 + n + 1)
                                pe.matmul(bank[o][:, :], p.identb[:, :], triA[:, 0:1, P:S].broadcast_to([P, 4, P]), start=True, stop=False)
                                for pp in range(2):
                                    q = Qst[:, ds(b, 1), h, 2 * j + pp, 0:P].rearrange("p o n -> p (o n)")
                                    pe.matmul(bank[o][:, pp * S:(pp + 1) * S], q, Kst[:, ds(b, 1), :, h, j, 0:P].rearrange("p o e n -> p (o e) n"),
                                              start=False, stop=(pp == 1))
                                for pp in range(2):
                                    pe.matmul(bank[o + 1 + pp][:, :], p.identb[:, :], triA[:, :, :].rearrange("p e n -> p (e n)"), start=True, stop=False)
                                    q = Qst[:, ds(b, 1), h, 2 * j + pp, P:S].rearrange("p o n -> p (o n)")
                                    mm = pe.matmul(bank[o + 1 + pp][:, :], q, Kst[:, ds(b, 1), :, h, j, :].rearrange("p o e n -> p (o e) n"),
                                                   start=False, stop=True)
                                mm.then_inc(s_a, 1)
                        pe.wait_ge(s_fa, b * 8 + 10)
                        pe.sem_inc(s_held, 1)
                        pe.transpose(bank[6][0:64, 0:P], NM[:, :, :, :, :, :].rearrange("p e q h j r -> p (e q h j r)"), p.identf[:, :]).then_inc(s_nt, 1)
                        pe.wait_ge(s_nmT, b + 1)

        with ExitStack() as c4:
            PT = p.sb("PT", [P, HALF, 1536], F32, c4)
            VS = p.sb("VS", [P, 2, 2, HALF, 32], F32, c4)
            OT = p.sb("OT", [P, 2, 1024], F32, c4)
            rinv = p.sb("rinv", [P, 2, 16], F32, c4)
            AO = p.sb("AO", [P, TB, D], F32, c4)
            AOT = p.sb("AOT", [P, KD, S], F32, c4)
            (s_s, s_e, s_pv, s_vs, s_ot, s_t, s_dch, s_ao, s_aot, s_aoT, s_y, s_xr) = \
                p.sems(c4, "s3 e3 pv3 vs3 ot3 t3 dch3 ao3 aot3 aoT3 y3 xr3")
            with nc.Block() as block:
                @block.scalar
                def _(act):
                    act.sem_inc(s_aot, 1)
                    with act.Fori(0, B) as b:
                        for h in range(2):
                            for j in range(HALF):
                                n = h * HALF + j
                                o = 3 * (n % 2)
                                act.wait_ge(s_s, b * 8 + n + 1)
                                act.wait_ge(s_pv, b * 2 + h + 1)
                                for i in range(3):
                                    ins = act.activation(PT[:, j, i * 512:(i + 1) * 512], bank[o + i][:, :], ACT.Exp)
                                ins.then_inc(s_e, 1)
                            act.wait_ge(s_pv, b * 2 + h + 2)
                            act.activation(OT[:, h, 0:512], bank[6][:, :], ACT.Copy)
                            act.activation(OT[:, h, 512:1024], bank[7][:, :], ACT.Copy).then_inc(s_ot, 1)
                        act.wait_ge(s_aoT, b + 1)
                        act.activation(AOT[:, :, :], bank[4][:, :].rearrange("p (k n) -> p k n", k=KD), ACT.Copy).then_inc(s_aot, 1)

                @block.vector
                def _(v):
                    with v.Fori(0, B) as b:
                        ch = Chain(v, s_dch, b, 4)
                        v.tensor_copy(VS[:, :, :, :, :].rearrange("p h k j d -> p k h (j d)"),
                                      Vaug[:, ds(2 * b, 2), :, :].rearrange("p k (h j) d -> p k h (j d)", h=2)).then_inc(s_vs, 1)
                        for h in range(2):
                            v.wait_ge(s_t, b * 2 + h + 1)
                            for qb in range(TB):
                                T = bank[qb][:, :].rearrange("p (m d) -> p m d", d=32)
                                ch.add(v.reciprocal(rinv[:, qb, :], T[:, :, 8]))
                                ch.wait()
                                v.tensor_tensor(AO[:, qb, h * P:(h + 1) * P].rearrange("p (m d) -> p m d", d=8), T[:, :, 0:8],
                                                rinv[:, qb, :].rearrange("p (m o) -> p m o", o=1).broadcast_to([P, 16, 8]), ALU.mult).then_inc(s_ao, 1)
                        for t in range(TB):
                            v.wait_ge(s_y, b * 2 + t + 1)
                            xt = p.X[:, ds(2 * b + t, 1), :].rearrange("p o n -> p (o n)")
                            v.tensor_tensor(xt, bank[5 + t][:, 0:D], xt, ALU.add).then_inc(s_xr, 1)

                @block.tensor
                def _(pe):
                    pe.sem_inc(s_pv, 1)
                    with pe.Fori(0, B) as b:
                        for h in range(2):
                            for j in range(HALF):
                                n = h * HALF + j
                                o = 3 * (n % 2)
                                if n >= 2:
                                    pe.wait_ge(s_e, b * 8 + n - 1)
                                if n in (HALF, HALF + 1):
                                    pe.wait_ge(s_ao, b * 4 + 2)
                                if n < 2:
                                    pe.wait_ge(s_aot, b + 1)
                                qs = Qst[:, ds(b, 1), h, 2 * j:2 * j + 2, :].rearrange("p o j n -> p (o j) n")
                                for e in range(2):
                                    pe.matmul(bank[o + e][:, :], p.identb[:, :], triB[:, :, :].rearrange("p e n -> p (e n)"), start=True, stop=False)
                                    pe.matmul(bank[o + e][:, :], Kst[:, ds(b, 1), e, h, j, 0:P].rearrange("p o n -> p (o n)"), qs, start=False, stop=True)
                                pe.matmul(bank[o + 2][:, :], p.identb[:, :], triB[:, 0:1, 0:P].broadcast_to([P, 4, P]), start=True, stop=False)
                                for e in range(2):
                                    mm = pe.matmul(bank[o + 2][:, e * S:(e + 1) * S], Kst[:, ds(b, 1), e, h, j, P:S].rearrange("p o n -> p (o n)"),
                                                   qs[:, :, P:S], start=False, stop=(e == 1))
                                mm.then_inc(s_s, 1)
                            pe.wait_ge(s_e, b * 8 + (h + 1) * HALF)
                            pe.wait_ge(s_vs, b + 1)
                            for e in range(2):
                                for j in range(HALF):
                                    pe.matmul(bank[6 + e][32 * j:32 * j + 32, :], VS[:, h, 0, j, :], PT[:, j, e * 512:(e + 1) * 512],
                                              start=True, stop=False)
                                for j in range(HALF):
                                    mm = pe.matmul(bank[6 + e][32 * j:32 * j + 32, :].rearrange("p (r q) -> p r q", r=2)[:, :, P:S], VS[:, h, 1, j, :],
                                                   PT[:, j, 1024 + e * S:1024 + (e + 1) * S], start=False, stop=True)
                            mm.then_inc(s_pv, 1)
                            pe.wait_ge(s_ot, b * 2 + h + 1)
                            for qb in range(TB):
                                for m in range(4):
                                    mm = pe.transpose(bank[qb][:, m * P:(m + 1) * P], OT[:, h, m * S + qb * P:m * S + (qb + 1) * P], p.identf[:, :])
                            mm.then_inc(s_t, 1)
                        pe.wait_ge(s_ao, b * 4 + 4)
                        for k in range(KD):
                            for t in range(TB):
                                mm = pe.transpose(bank[4][:, k * S + t * P:k * S + (t + 1) * P], AO[:, t, k * P:(k + 1) * P], p.identf[:, :])
                        mm.then_inc(s_aoT, 1)
                        pe.wait_ge(s_aot, b + 2)
                        for t in range(TB):
                            pe.matmul(bank[5 + t][:, 0:D], p.ones1[:, :], bo[:, :], start=True, stop=False)
                            for k in range(KD):
                                mm = pe.matmul(bank[5 + t][:, 0:D], AOT[:, k, t * P:(t + 1) * P], wo[:, k, :], start=False, stop=(k == KD - 1))
                            mm.then_inc(s_y, 1)
                        pe.wait_ge(s_xr, b * 2 + 2)


def first_ffn(p):
    nc, a = p.nc, p.a
    with ExitStack() as c:
        sb = lambda n, s, dt=F32: p.sb(n, s, dt, c)
        W12 = sb("W12", [P, KD, 2 * HID0], BF16)
        W3 = sb("W3", [P, HT0, D], BF16)
        mean = sb("mean", [P, 3])
        inv = sb("inv", [P, 3])
        with ExitStack() as c1:
            w12 = p.sb("w12", [P, KD, 2 * HID0], F32, c1)
            w3 = p.sb("w3", [P, HT0, D], F32, c1)
            asum = p.sb("asum", [P, 3], F32, c1)
            ones = p.sb("ones", [P, P], F32, c1)
            tot = p.ps("tot", [P, 512], c1)
            (s_w, s_d, s_sum, s_tot) = p.sems(c1, "w4 d4 sum4 tot4")
            with nc.Block() as block:
                @block.sync
                def _(sp):
                    sp.dma_start(w12[:, :, :], a["w12T"].rearrange("(k p) n -> p k n", p=P)).then_inc(s_w, 16)
                    sp.dma_start(w3[:, :, :], a["w3T"].rearrange("(k p) n -> p k n", p=P)).then_inc(s_w, 16)

                @block.vector
                def _(v):
                    ch = Chain(v, s_d, 0, 0)
                    ch.add(v.memset(ones[:, :], 1.0))
                    v.wait_ge(s_w, 32)
                    for m in range(2):
                        ch.add(v.tensor_reduce(asum[:, m:m + 1], w12[:, :, m * HID0:(m + 1) * HID0], AX.XY, ALU.add, apply_absolute_value=True))
                    ch.add(v.tensor_reduce(asum[:, 2:3], w3[:, :, :], AX.XY, ALU.add, apply_absolute_value=True))
                    ch.wait()
                    v.tensor_copy(inv[:, :], asum[:, :]).then_inc(s_sum, 1)
                    v.wait_ge(s_tot, 1)
                    ch.link(v.tensor_scalar(mean[:, :], tot[:, 0:3], 1.0 / (D * HID0), 1e-5, ALU.mult, ALU.max))
                    ch.link(v.reciprocal(inv[:, :], mean[:, :]))
                    for raw, out, m in ((w12[:, :, 0:HID0], W12[:, :, 0:HID0], 0), (w12[:, :, HID0:], W12[:, :, HID0:], 1), (w3[:, :, :], W3[:, :, :], 2)):
                        ch.link(v.tensor_scalar(raw, raw, inv[:, m:m + 1], 1.0, ALU.mult, ALU.min))
                        ch.link(v.tensor_scalar(raw, raw, -1.0, MAGIC, ALU.max, ALU.add))
                        ch.add(v.tensor_scalar(out, raw, MAGIC, None, ALU.subtract))

                @block.tensor
                def _(pe):
                    pe.wait_ge(s_sum, 1)
                    pe.matmul(tot[:, 0:3], ones[:, :], asum[:, :], start=True, stop=True).then_inc(s_tot, 1)

        am = sb("am", [P, TB])
        qs = sb("qs", [P, 2 * TB])
        sa = sb("sa", [P, 2, TB])
        q = sb("q", [P, TB, D])
        hq = sb("hq", [P, TB, D], BF16)
        hqT = sb("hqT", [P, KD, S], BF16)
        sil = sb("sil", [P, TB, HID0])
        h = sb("h", [P, TB, HID0])
        hm = sb("hm", [P, TB, 4])
        h2 = sb("h2", [P, TB, HID0], BF16)
        h2T = sb("h2T", [P, TB, HT0, P], BF16)
        G = [p.ps(f"G{t}", [P, 1024], c) for t in range(TB)]
        U = [p.ps(f"U{t}", [P, 1024], c) for t in range(TB)]
        (s_var, s_sd, s_xn, s_dch, s_hq, s_tr, s_hqT, s_a, s_sa, s_sil, s_h2, s_ht, s_h2T, s_y, s_x) = \
            p.sems(c, "var5 sd5 xn5 dch5 hq5 tr5 hqT5 a5 sa5 sil5 h25 ht5 h2T5 y5 x5")
        with nc.Block() as block:
            @block.scalar
            def _(act):
                with act.Fori(0, B) as b:
                    act.wait_ge(s_var, b + 1)
                    act.activation(p.ln_rs[:, 0:TB], p.ln_mv[:, :, 1], ACT.Sqrt, bias=p.eps[:, 0:1]).then_inc(s_sd, 1)
                    act.wait_ge(s_tr, b + 1)
                    act.activation(hqT[:, :, :], G[0][:, 0:256].bitcast(BF16).rearrange("p (k n) -> p k n", k=KD), ACT.Copy).then_inc(s_hqT, 1)
                    act.wait_ge(s_sa, b + 1)
                    for t in range(TB):
                        act.wait_ge(s_a, b * TB + t + 1)
                        act.activation(sil[:, t, :], G[t][:, 0:HID0], ACT.Silu, scale=sa[:, 0, t:t + 1]).then_inc(s_sil, 1)
                    for t in range(TB):
                        act.wait_ge(s_ht, b * TB + t + 1)
                        src = G[t][:, 0:HT0 * 64].bitcast(BF16).rearrange("p (k n) -> p k n", n=P)
                        act.activation(h2T[:, t, 0:HT0 - 1, :], src[:, 0:HT0 - 1, :], ACT.Copy)
                        act.activation(h2T[0:64, t, HT0 - 1, :], src[0:64, HT0 - 1, :], ACT.Copy).then_inc(s_h2T, 1)

            @block.vector
            def _(v):
                with v.Fori(0, B) as b:
                    ch = Chain(v, s_dch, b, 31)
                    xt = lambda t: p.X[:, ds(2 * b + t, 1), :].rearrange("p o n -> p (o n)")
                    layernorm(v, xt, p.ln_stats, p.ln_mv, p.xn, p.ln_rs, s_var, s_sd, ch, s_xn, b)
                    v.wait_ge(s_xn, b + 1)
                    ch.wait()
                    ch.link(v.tensor_reduce(am[:, :], p.xn[:, :, :], AX.X, ALU.max, apply_absolute_value=True))
                    ch.link(v.tensor_scalar(am[:, :], am[:, :], 1e-5, None, ALU.max))
                    ch.link(v.reciprocal(qs[:, 0:TB], am[:, :]))
                    ch.link(v.tensor_scalar(qs[:, 0:TB], qs[:, 0:TB], 127.0, None, ALU.mult))
                    ch.link(v.tensor_scalar(qs[:, TB:2 * TB], am[:, :], 1.0 / 127.0, None, ALU.mult))
                    for t in range(TB):
                        ch.add(v.tensor_scalar(q[:, t, :], p.xn[:, t, :], qs[:, t:t + 1], -128.0, ALU.mult, ALU.max))
                    ch.wait()
                    ch.link(v.tensor_scalar(q[:, :, :], q[:, :, :], 127.0, MAGIC, ALU.min, ALU.add))
                    v.tensor_scalar(hq[:, :, :], q[:, :, :], MAGIC, None, ALU.subtract).then_inc(s_hq, 1)
                    ch.add(v.tensor_scalar(sa[:, 0, :], qs[:, TB:2 * TB], mean[:, 0:1], None, ALU.mult))
                    v.tensor_scalar(sa[:, 1, :], qs[:, TB:2 * TB], mean[:, 1:2], None, ALU.mult).then_inc(s_sa, 1)
                    v.wait_ge(s_sa, b + 1)
                    for t in range(TB):
                        v.wait_ge(s_sil, b * TB + t + 1)
                        ch.link(v.scalar_tensor_tensor(h[:, t, :], U[t][:, 0:HID0], sa[:, 1, t:t + 1], sil[:, t, :], ALU.mult, ALU.mult))
                        ch.link(v.tensor_reduce(hm[:, t, 0:1], h[:, t, :], AX.X, ALU.max, apply_absolute_value=True))
                        ch.link(v.tensor_scalar(hm[:, t, 0:1], hm[:, t, 0:1], 1e-5, None, ALU.max))
                        ch.link(v.reciprocal(hm[:, t, 1:2], hm[:, t, 0:1]))
                        ch.link(v.tensor_scalar(hm[:, t, 2:3], hm[:, t, 1:2], 127.0, None, ALU.mult))
                        ch.add(v.tensor_scalar(hm[:, t, 3:4], hm[:, t, 0:1], 1.0 / 127.0, mean[:, 2:3], ALU.mult, ALU.mult))
                        ch.link(v.tensor_scalar(h[:, t, :], h[:, t, :], hm[:, t, 2:3], -128.0, ALU.mult, ALU.max))
                        ch.link(v.tensor_scalar(h[:, t, :], h[:, t, :], 127.0, MAGIC, ALU.min, ALU.add))
                        v.tensor_scalar(h2[:, t, :], h[:, t, :], MAGIC, None, ALU.subtract).then_inc(s_h2, 1)
                    for t in range(TB):
                        v.wait_ge(s_y, b * TB + t + 1)
                        v.scalar_tensor_tensor(xt(t), U[t][:, 0:D], hm[:, t, 3:4], xt(t), ALU.mult, ALU.add).then_inc(s_x, 1)
                    v.wait_ge(s_x, b * TB + TB)
                    ch.done()

            @block.tensor
            def _(pe):
                with pe.Fori(0, B) as b:
                    pe.wait_ge(s_hq, b + 1)
                    gb = G[0][:, 0:256].bitcast(BF16)
                    for k in range(KD):
                        for t in range(TB):
                            mm = pe.transpose(gb[:, k * S + t * P:k * S + (t + 1) * P], hq[:, t, k * P:(k + 1) * P], p.identb[:, :])
                    mm.then_inc(s_tr, 1)
                    pe.wait_ge(s_hqT, b + 1)
                    for t in range(TB):
                        for o, dst in ((0, G[t]), (HID0, U[t])):
                            for n0, n1 in ((0, 512), (512, HID0)):
                                for k in range(KD):
                                    mm = pe.matmul(dst[:, n0:n1], hqT[:, k, t * P:(t + 1) * P], W12[:, k, o + n0:o + n1],
                                                   start=(k == 0), stop=(k == KD - 1))
                        mm.then_inc(s_a, 1)
                    for t in range(TB):
                        pe.wait_ge(s_h2, b * TB + t + 1)
                        gb = G[t][:, 0:HT0 * 64].bitcast(BF16)
                        for k in range(HT0):
                            n = min(P, HID0 - k * P)
                            mm = pe.transpose(gb[0:n, k * P:(k + 1) * P], h2[:, t, k * P:k * P + n], p.identb[:, :])
                        mm.then_inc(s_ht, 1)
                        pe.wait_ge(s_h2T, b * TB + t + 1)
                        for k in range(HT0):
                            n = min(P, HID0 - k * P)
                            mm = pe.matmul(U[t][:, 0:D], h2T[0:n, t, k, :], W3[0:n, k, :], start=(k == 0), stop=(k == HT0 - 1))
                        mm.then_inc(s_y, 1)
                    pe.wait_ge(s_x, b * TB + TB)

LINKS_C = 80
LINKS_D = 31


def second_attention(p):
    nc, a = p.nc, p.a
    NH = H1 + 2 * KV1
    CHUNKS = ("k", "kc", "v", "vc", "q0", "q1", "q2", "q3")
    with ExitStack() as c:
        sb = lambda n, s, dt=F32: p.sb(n, s, dt, c)
        CQ = sb("CQ", [P, TB, HD1])
        SQ = sb("SQ", [P, TB, HD1])
        CK = sb("CK", [P, TB, HD1])
        SK = sb("SK", [P, TB, HD1])
        WR = sb("WR", [P, 2, HD1])
        hT = sb("hT", [P, 2, KD, S], BF16)
        R = sb("R", [P, 3, CH])
        R2 = sb("R2", [P, CH])
        junk = sb("junk", [P, 4, HD1])
        ssq = sb("ssq", [P, TB, NH])
        rms = sb("rms", [P, TB, NH])
        rk = sb("rk", [P, TB, NH])
        qT = sb("qT", [P, 2, H1, S], BF16)
        kT = sb("kT", [P, 2, KV1, T1 + S], BF16)
        V = sb("V", [P, 4, KV1 * HD1])
        nm = sb("nm", [P, 2, 4])
        bias = sb("bias", [P, 2, 4])
        sm = sb("sm", [P, 2, 4])
        rs = sb("rs", [P, 2, 4])
        Pr = sb("Pr", [P, 2, REP1, 512])
        PTs = sb("PTs", [P, 4, 512])
        OT = sb("OT1", [P, 2, H1, S], BF16)
        bank = [p.ps(f"c{i}", [P, 512], c) for i in range(8)]
        mask = sb("mask1", [P, P], BF16)

        with ExitStack() as c1:
            rope = p.sb("rope", [P, TB, 4, 64], F32, c1)
            qkw = p.sb("qkw", [1, 2 * HD1], F32, c1)
            (s_w, s_wr, s_r, s_t, s_m) = p.sems(c1, "w6 wr6 r6 t6 m6")
            with nc.Block() as block:
                @block.sync
                def _(sp):
                    sp.dma_start(rope[:, :, :, :], a["rope"]).then_inc(s_w, 16)
                    sp.dma_start(qkw[:, :], a["qkw"]).then_inc(s_w, 16)

                @block.gpsimd
                def _(g):
                    g.memset(mask[:, :], 0.0).then_inc(s_m, 1)
                    g.wait_ge(s_m, 1)
                    g.affine_select(out=mask[:, :], in_=mask[:, :], compare_op=ALU.is_ge, fill=NEG, base=0,
                                    pattern=[[-1, P]], channel_multiplier=1).then_inc(s_m, 1)

                @block.vector
                def _(v):
                    v.wait_ge(s_wr, 1)
                    v.tensor_copy(WR[:, :, :], bank[0][:, 0:2 * HD1].rearrange("p (w n) -> p w n", w=2)).then_inc(s_r, 1)
                    v.wait_ge(s_r, 1)
                    for w, C_, S_ in ((0, CQ, SQ), (1, CK, SK)):
                        for t in range(TB):
                            v.tensor_tensor(C_[:, t, :], rope[:, t, 0:2, :].rearrange("p a n -> p (a n)"), WR[:, w, :], ALU.mult).then_inc(s_t, 1)
                            v.tensor_tensor(S_[:, t, 0:64], rope[:, t, 2, :], WR[:, w, 64:128], ALU.mult).then_inc(s_t, 1)
                            v.tensor_tensor(S_[:, t, 64:128], rope[:, t, 3, :], WR[:, w, 0:64], ALU.mult).then_inc(s_t, 1)

                @block.tensor
                def _(pe):
                    pe.wait_ge(s_w, 32)
                    pe.matmul(bank[0][:, 0:2 * HD1], p.ones1[:, :], qkw[:, :], start=True, stop=True).then_inc(s_wr, 1)

        NU = KV1 * TB
        KTS = [2 + 1 + u % TB for u in range(NU)]
        EV = sum(KTS)
        FIRST = [sum(KTS[:u]) for u in range(NU)]
        (s_var, s_sd, s_xn, s_dch, s_tr, s_hhi, s_hlo, s_pj, s_sq, s_vev, s_pf, s_rt, s_ro, s_ri, s_rT, s_rhi, s_rlo,
         s_s, s_nb, s_e, s_p, s_kT, s_evA, s_evD, s_pvk, s_ohi, s_olo, s_y, s_x) = \
            p.sems(c, "var7 sd7 xn7 dch7 tr7 hhi7 hlo7 pj7 sq7 vev7 pf7 rt7 ro7 ri7 rT7 rhi7 rlo7 "
                      "s7 nb7 e7 p7 kT7 evA7 evD7 pvk7 ohi7 olo7 y7 x7")
        ROT = [ch for ch in CHUNKS if ch[0] != "v"]
        NR = len(ROT) * TB
        head0 = {"k": 0, "kc": KV1, "q0": 2 * KV1, "q1": 3 * KV1, "q2": 4 * KV1, "q3": 5 * KV1}
        steps = [(t, ch) for t in range(TB) for ch in CHUNKS]
        rsteps = [(t, ch) for t, ch in steps if ch[0] != "v"]

        def place(t, ch, part):
            if ch == "k":
                return kT[:, part, :, T1 + t * P:T1 + (t + 1) * P]
            if ch == "kc":
                return kT[:, part, :, t * P:(t + 1) * P]
            h = REP1 * int(ch[1])
            return qT[:, part, h:h + REP1, t * P:(t + 1) * P]

        with nc.Block() as block:
            @block.scalar
            def _(act):
                act.sem_inc(s_e, 2)
                act.sem_inc(s_evA, 1)
                with act.Fori(0, B) as b:
                    act.wait_ge(s_var, b + 1)
                    act.activation(p.ln_rs[:, 0:TB], p.ln_mv[:, :, 1], ACT.Sqrt, bias=p.eps[:, 0:1]).then_inc(s_sd, 1)
                    act.wait_ge(s_tr, b + 1)
                    act.activation(hT[:, 0, :, :], bank[0][:, :].rearrange("p (k n) -> p k n", k=KD), ACT.Copy).then_inc(s_hhi, 1)

                    def hi_of(n):
                        t, ch = rsteps[n]
                        act.wait_ge(s_rT, b * NR + n + 1)
                        act.activation(place(t, ch, 0), bank[5 + n % 2][:, :].rearrange("p (h n) -> p h n", h=4), ACT.Copy).then_inc(s_rhi, 1)

                    r = 0
                    for n, (t, ch) in enumerate(steps):
                        act.wait_ge(s_pj, b * len(steps) + n + 1)
                        bk = bank[1 + n % 4]
                        if ch[0] == "v":
                            act.activation(V[:, (2 if ch == "v" else 0) + t, :], bk[:, :], ACT.Copy).then_inc(s_vev, 1)
                            continue
                        h0 = head0[ch]
                        for h in range(4):
                            ins = act.activation(junk[:, h, :], bk[:, h * HD1:(h + 1) * HD1], ACT.Square, accum_out=ssq[:, t, h0 + h:h0 + h + 1])
                        ins.then_inc(s_sq, 1)
                        act.wait_ge(s_sq, b * NR + r + 1)
                        if ch[0] == "k":
                            act.activation(rms[:, t, h0:h0 + 4], ssq[:, t, h0:h0 + 4], ACT.Sqrt, bias=p.eps[:, 2:3], scale=1.0 / HD1).then_inc(s_rt, 1)
                        else:
                            act.activation(rms[:, t, h0:h0 + 4], ssq[:, t, h0:h0 + 4], ACT.Sqrt, bias=p.eps[:, 1:2]).then_inc(s_rt, 1)
                        r += 1
                        if r >= 3:
                            hi_of(r - 3)
                    hi_of(NR - 2)
                    hi_of(NR - 1)

                    def exps(u, s):
                        g, t = u // TB, u % TB
                        w = 2 * u + s
                        nk = KTS[u] * P
                        act.wait_ge(s_nb, b * 2 * NU + w + 1)
                        for i in range(2):
                            h = 2 * s + i
                            ins = act.activation(Pr[:, u % 2, h, 0:nk], bank[2 * s + i][:, 0:nk], ACT.Exp, bias=bias[:, u % 2, h:h + 1],
                                                 scale=rk[:, t, 2 * KV1 + REP1 * g + h:2 * KV1 + REP1 * g + h + 1], accum_out=sm[:, u % 2, h:h + 1])
                        ins.then_inc(s_e, 1)

                    def evac(u, k):
                        i = FIRST[u] + k
                        if k < KTS[u] and i % 2 == 0:
                            act.wait_ge(s_kT, b * EV + i + 1)
                            act.wait_ge(s_pvk, b * EV + i + 1)
                            act.activation(PTs[:, i % 4, :], bank[4 + i % 2][:, :], ACT.Copy).then_inc(s_evA, 1)

                    exps(0, 0)
                    exps(0, 1)
                    for u in range(NU):
                        if u + 1 < NU:
                            exps(u + 1, 0)
                        evac(u, 0)
                        evac(u, 1)
                        if u + 1 < NU:
                            exps(u + 1, 1)
                        evac(u, 2)
                        evac(u, 3)
                        g, t = u // TB, u % TB
                        act.wait_ge(s_pvk, b * EV + FIRST[u] + KTS[u] + 4)
                        act.activation(OT[:, 0, REP1 * g:REP1 * g + REP1, t * P:(t + 1) * P],
                                       bank[6 + u % 2][:, :].rearrange("p (h n) -> p h n", h=4), ACT.Copy).then_inc(s_ohi, 1)

            @block.vector
            def _(v):
                v.sem_inc(s_evD, 1)
                v.sem_inc(s_x, 1)
                with v.Fori(0, B) as b:
                    ch_ = Chain(v, s_dch, b, LINKS_C)
                    xt = lambda t: p.X[:, ds(2 * b + t, 1), :].rearrange("p o n -> p (o n)")
                    layernorm(v, xt, p.ln_stats, p.ln_mv, p.xn, p.ln_rs, s_var, s_sd, ch_, s_xn, b)
                    v.wait_ge(s_hhi, b + 1)
                    v.tensor_tensor(hT[:, 1, :, :], bank[0][:, :].rearrange("p (k n) -> p k n", k=KD), hT[:, 0, :, :], ALU.subtract).then_inc(s_hlo, 1)

                    def lo_of(n):
                        t, ch = rsteps[n]
                        v.wait_ge(s_rhi, b * NR + n + 1)
                        v.tensor_tensor(place(t, ch, 1), bank[5 + n % 2][:, :].rearrange("p (h n) -> p h n", h=4), place(t, ch, 0), ALU.subtract).then_inc(s_rlo, 1)

                    r = 0
                    for n, (t, ch) in enumerate(steps):
                        if ch[0] == "v":
                            continue
                        bk = bank[1 + n % 4][:, :].rearrange("p (h a n) -> p h a n", h=4, a=2)
                        bf = bank[1 + n % 4][:, :].rearrange("p (h n) -> p h n", h=4)
                        h0 = head0[ch]
                        Rf = R[:, r % 3, :].rearrange("p (h n) -> p h n", h=4)
                        R2h = R2[:, :].rearrange("p (h a n) -> p h a n", h=4, a=2)
                        v.wait_ge(s_sq, b * NR + r + 1)
                        full = lambda tab: tab.rearrange("p (o n) -> p o n", o=1).broadcast_to([P, 4, tab.shape[-1]])
                        if ch == "kc":
                            ch_.add(v.tensor_tensor(Rf, bf, full(WR[:, 1, :]), ALU.mult))
                        else:
                            C_, S_ = (CK, SK) if ch == "k" else (CQ, SQ)
                            ch_.add(v.tensor_tensor(Rf, bf, full(C_[:, t, :]), ALU.mult))
                            ch_.add(v.tensor_tensor(R2h[:, :, 0, :], bk[:, :, 1, :], full(S_[:, t, 0:64]), ALU.mult))
                            ch_.add(v.tensor_tensor(R2h[:, :, 1, :], bk[:, :, 0, :], full(S_[:, t, 64:128]), ALU.mult))
                        v.wait_ge(s_rt, b * NR + r + 1)
                        ins = v.reciprocal(rk[:, t, h0:h0 + 4], rms[:, t, h0:h0 + 4])
                        ins.then_inc(s_pf, 1)
                        ch_.wait()
                        if ch == "k":
                            ch_.link(v.tensor_tensor(R[:, r % 3, :], R[:, r % 3, :], R2[:, :], ALU.add))
                        if ch[0] == "k":
                            v.wait_ge(s_pf, b * NR + r + 1)
                            v.tensor_tensor(Rf, Rf, rk[:, t, h0:h0 + 4].rearrange("p (h o) -> p h o", o=1).broadcast_to([P, 4, HD1]), ALU.mult).then_inc(s_ro, 1)
                        else:
                            v.tensor_tensor(R[:, r % 3, :], R[:, r % 3, :], R2[:, :], ALU.add).then_inc(s_ro, 1)
                        r += 1
                        if r >= 3:
                            lo_of(r - 3)
                        v.wait_ge(s_ro, b * NR + r)
                    lo_of(NR - 2)
                    lo_of(NR - 1)

                    def maxima(u, s):
                        g, t = u // TB, u % TB
                        w = 2 * u + s
                        nk = KTS[u] * P
                        v.wait_ge(s_s, b * 2 * NU + w + 1)
                        for i in range(2):
                            ch_.add(v.tensor_reduce(nm[:, u % 2, 2 * s + i:2 * s + i + 1], bank[2 * s + i][:, 0:nk], AX.X, ALU.max, negate=True))
                        ch_.wait()
                        h = 2 * KV1 + REP1 * g + 2 * s
                        v.tensor_tensor(bias[:, u % 2, 2 * s:2 * s + 2], nm[:, u % 2, 2 * s:2 * s + 2], rk[:, t, h:h + 2], ALU.mult).then_inc(s_nb, 1)

                    def norms(u):
                        nk = KTS[u] * P
                        v.wait_ge(s_e, b * 2 * NU + 2 * u + 4)
                        ch_.link(v.reciprocal(rs[:, u % 2, :], sm[:, u % 2, :]))
                        for h in range(REP1):
                            v.tensor_scalar(Pr[:, u % 2, h, 0:nk], Pr[:, u % 2, h, 0:nk], rs[:, u % 2, h:h + 1], None, ALU.mult).then_inc(s_p, 1)

                    def evac(u, k):
                        i = FIRST[u] + k
                        if k < KTS[u] and i % 2 == 1:
                            v.wait_ge(s_kT, b * EV + i + 1)
                            v.wait_ge(s_pvk, b * EV + i + 1)
                            v.tensor_copy(PTs[:, i % 4, :], bank[4 + i % 2][:, :]).then_inc(s_evD, 1)

                    maxima(0, 0)
                    maxima(0, 1)
                    for u in range(NU):
                        g, t = u // TB, u % TB
                        norms(u)
                        if u + 1 < NU:
                            maxima(u + 1, 0)
                            evac(u, 0)
                            evac(u, 1)
                            maxima(u + 1, 1)
                        else:
                            evac(u, 0)
                            evac(u, 1)
                        evac(u, 2)
                        evac(u, 3)
                        v.wait_ge(s_ohi, b * NU + u + 1)
                        hd = slice(REP1 * g, REP1 * g + REP1)
                        v.tensor_tensor(OT[:, 1, hd, t * P:(t + 1) * P], bank[6 + u % 2][:, :].rearrange("p (h n) -> p h n", h=4),
                                        OT[:, 0, hd, t * P:(t + 1) * P], ALU.subtract).then_inc(s_olo, 1)
                    for t in range(TB):
                        v.wait_ge(s_y, b * TB + t + 1)
                        v.tensor_tensor(xt(t), bank[t][:, 0:D], xt(t), ALU.add).then_inc(s_x, 1)
                    v.wait_ge(s_x, b * TB + TB + 1)
                    ch_.done()

            @block.tensor
            def _(pe):
                pe.sem_inc(s_pvk, 4)
                with pe.Fori(0, B) as b:
                    pe.wait_ge(s_xn, b + 1)
                    for k in range(KD):
                        for t in range(TB):
                            mm = pe.transpose(bank[0][:, k * S + t * P:k * S + (t + 1) * P], p.xn[:, t, k * P:(k + 1) * P], p.identf[:, :])
                    mm.then_inc(s_tr, 1)

                    def turn(n):
                        pe.wait_ge(s_ro, b * NR + n + 1)
                        if n >= 2:
                            pe.wait_ge(s_rlo, b * NR + n - 1)
                        for h in range(4):
                            mm = pe.transpose(bank[5 + n % 2][:, h * P:(h + 1) * P], R[:, n % 3, h * HD1:(h + 1) * HD1], p.identf[:, :])
                        mm.then_inc(s_rT, 1)

                    r = nv = 0
                    used = {}
                    for n, (t, ch) in enumerate(steps):
                        if n == 0:
                            pe.wait_ge(s_hlo, b + 1)
                        if n % 4 in used:
                            sem, per, cnt = used[n % 4]
                            pe.wait_ge(sem, b * per + cnt)
                        if ch[-1] == "c":
                            act_ = lambda part, k: p.CTS[:, part, k, ds(b * S + t * P, P)]
                        else:
                            act_ = lambda part, k: hT[:, part, k, t * P:(t + 1) * P]
                        if ch[0] == "q":
                            w_ = lambda part, k: p.WQ[:, part, k, int(ch[1]) * CH:(int(ch[1]) + 1) * CH]
                        else:
                            w_ = lambda part, k: p.WKV[:, part, k, int(ch[-1] == "c"), (CH if ch[0] == "v" else 0):(2 * CH if ch[0] == "v" else CH)]
                        terms = [(x, w, k) for x, w in ((0, 0), (0, 1), (1, 0)) for k in range(KD)]
                        for i, (x, w, k) in enumerate(terms):
                            mm = pe.matmul(bank[1 + n % 4][:, :], act_(x, k), w_(w, k), start=(i == 0), stop=(i == len(terms) - 1))
                        mm.then_inc(s_pj, 1)
                        if ch[0] == "v":
                            nv += 1
                            used[n % 4] = (s_vev, 2 * TB, nv)
                        else:
                            r += 1
                            used[n % 4] = (s_pf, NR, r)
                            if r >= 3:
                                turn(r - 3)
                    turn(NR - 2)
                    turn(NR - 1)
                    pe.wait_ge(s_rlo, b * NR + NR)
                    pe.wait_ge(s_vev, b * 2 * TB + 2 * TB)

                    def scores(u):
                        g, t = u // TB, u % TB
                        nk = KTS[u] * P
                        for s in range(2):
                            w = 2 * u + s
                            pe.wait_ge(s_e, b * 2 * NU + w + 1)
                            for i in range(2):
                                h = REP1 * g + 2 * s + i
                                o = bank[2 * s + i]
                                for n, (x, y) in enumerate(((0, 0), (0, 1), (1, 0))):
                                    pe.matmul(o[:, 0:nk], qT[:, x, h, t * P:(t + 1) * P], kT[:, y, g, 0:nk], start=(n == 0), stop=False)
                                mm = pe.matmul(o[:, nk - P:nk], p.identb[:, :], mask[:, :], start=False, stop=True)
                            mm.then_inc(s_s, 1)

                    def spread(u, k):
                        i = FIRST[u] + k
                        if k == 0:
                            pe.wait_ge(s_p, b * 4 * NU + 4 * u + 4)
                        if i % 2 == 0:
                            pe.wait_ge(s_evA, b * (EV // 2) + i // 2 + 1)
                        else:
                            pe.wait_ge(s_evD, b * (EV // 2) + i // 2 + 1)
                        for h in range(REP1):
                            mm = pe.transpose(bank[4 + i % 2][:, h * P:(h + 1) * P], Pr[:, u % 2, h, k * P:(k + 1) * P], p.identf[:, :])
                        mm.then_inc(s_kT, 1)

                    def product(u, k):
                        i = FIRST[u] + k
                        if k == 0 and u >= 2:
                            pe.wait_ge(s_olo, b * NU + u - 1)
                        pe.wait_ge(s_evD if i % 2 else s_evA, b * (EV // 2) + i // 2 + 2)
                        g = u // TB
                        mm = pe.matmul(bank[6 + u % 2][:, :], V[:, k, g * HD1:(g + 1) * HD1], PTs[:, i % 4, :], start=(k == 0), stop=(k == KTS[u] - 1))
                        mm.then_inc(s_pvk, 1)

                    scores(0)
                    for u in range(NU):
                        if u + 1 < NU:
                            scores(u + 1)
                        spread(u, 0)
                        spread(u, 1)
                        for k in range(KTS[u]):
                            product(u, k)
                            if k + 2 < KTS[u]:
                                spread(u, k + 2)
                    pe.wait_ge(s_olo, b * NU + NU)
                    for t in range(TB):
                        n = 0
                        for x, w in ((0, 0), (0, 1), (1, 0)):
                            for h in range(H1):
                                mm = pe.matmul(bank[t][:, 0:D], OT[:, x, h, t * P:(t + 1) * P], p.WO[:, w, h, :], start=(n == 0), stop=(n == 3 * H1 - 1))
                                n += 1
                        mm.then_inc(s_y, 1)
                    pe.wait_ge(s_x, b * TB + TB + 1)


def second_ffn(p):
    nc, a = p.nc, p.a
    with ExitStack() as c:
        sb = lambda n, s, dt=F32: p.sb(n, s, dt, c)
        WA = sb("WA", [P, 2, KD, 2, E1 * R1], BF16)
        WG = sb("WG", [P, 2, KD, 2, HID1], BF16)
        WB = sb("WB", [P, 2, 2, ET1, HID1], BF16)
        WDA = sb("WDA", [P, 2, MT1, E1 * R1], BF16)
        WD = sb("WD", [P, 2, MT1, D], BF16)
        WDB = sb("WDB", [P, 2, ET1, D], BF16)
        raw = sb("rawD", [P, 2, 2048])
        confT = sb("confT", [P, KD, E1])
        confb = sb("confb", [1, E1])
        wealth = sb("wealth", [1, E1])
        worth = sb("worth", [P, E1])
        order = sb("order", [P, E1])
        pick = sb("pick", [18, ET1, 2, P], BF16)
        pickw = sb("pickw", [18, 2, P])
        hf = sb("hf", [P, KD, S])
        hT = sb("hTd", [P, 2, KD, S], BF16)
        conf = sb("conf", [P, TB, E1])
        eq = sb("eq", [P, TB, E1])
        best = sb("best", [P, 4, TB])
        RT = sb("RT", [P, TB, 18])
        RTf = sb("RTf", [18, S])
        RTb = sb("RTb", [18, S], BF16)
        MK = sb("MK", [P, ET1, 2, S], BF16)
        wrep = sb("wrep", [P, 2, S])
        z = sb("z", [P, 2, 2, ET1, S], BF16)
        zm = sb("zm", [P, 2, 2, ET1, 2 * S], BF16)
        BS = sb("BS", [P, 2, 2, S])
        gl = sb("gl", [P, 2, 2 * S])
        ul = sb("ul", [P, 2, 2 * S])
        sil = sb("silD", [P, 2, 2 * S])
        hw = sb("hw", [P, 2, 2, S])
        hs = sb("hs", [P, 2, S])
        HW = sb("HW", [P, 2, MT1, 2 * S], BF16)
        HS = sb("HS", [P, 2, MT1, S], BF16)
        yt = sb("yt", [P, ET1, 2, S])
        ys = sb("ys", [P, ET1, S])
        YS = sb("YS", [P, 2, ET1, S], BF16)
        bank = [p.ps(f"d{i}", [P, 512], c) for i in range(8)]
        (s_c, s_sel, s_wl, s_wt) = p.sems(c, "c8 sel8 wl8 wt8")
        with nc.Block() as block:
            @block.sync
            def _(sp):
                sp.dma_start(confT[:, :, :], a["confT"].rearrange("(k p) e -> p k e", p=P)).then_inc(s_c, 16)
                sp.dma_start(confb[:, :], a["confb"]).then_inc(s_c, 16)
                sp.dma_start(wealth[:, :], a["wealth"]).then_inc(s_c, 16)
                sp.wait_ge(s_c, 48)

            @block.gpsimd
            def _(g):
                g.memset(pick[:, :, :, :], 0.0).then_inc(s_sel, 1)
                g.memset(pickw[:, :, :], 0.0).then_inc(s_sel, 1)
                g.wait_ge(s_sel, 2)
                for s in range(2):
                    for t in range(ET1):
                        v = pick[:, t, s, :].rearrange("k (h n) -> k h n", h=2)
                        g.affine_select(out=v, in_=v, compare_op=ALU.not_equal, fill=SCALING, base=-(E1 * s + 2 * t),
                                        pattern=[[-1, 2], [0, R1]], channel_multiplier=1).then_inc(s_sel, 1)
                    g.affine_select(out=pickw[:, s, :], in_=pickw[:, s, :], compare_op=ALU.not_equal, fill=1.0, base=-(2 * E1 + s),
                                    pattern=[[0, P]], channel_multiplier=1).then_inc(s_sel, 1)

            @block.vector
            def _(v):
                for e in range(E1):
                    v.memset(order[:, e:e + 1], e - 99.0).then_inc(s_wt, 1)
                v.wait_ge(s_wl, 1)
                v.tensor_copy(worth[:, :], bank[0][:, 0:E1]).then_inc(s_wt, 1)

            @block.tensor
            def _(pe):
                pe.wait_ge(s_c, 48)
                pe.matmul(bank[0][:, 0:E1], p.ones1[:, :], wealth[:, :], start=True, stop=True).then_inc(s_wl, 1)

        (s_var, s_sd, s_xn, s_dch, s_tr, s_hf, s_hhi, s_hlo, s_lg, s_conf, s_diff, s_ex, s_rt, s_rtT, s_rtc, s_zp, s_zhi, s_zlo,
         s_mkp, s_mk, s_wp, s_wrep, s_zm, s_bs, s_bev, s_lo, s_gl, s_ul, s_sil, s_hw, s_hs, s_hwhi, s_hshi, s_hwlo, s_hslo,
         s_yp, s_ys, s_yhi, s_ylo, s_y, s_x, s_out, s_in0, s_in1, s_split) = \
            p.sems(c, "var9 sd9 xn9 dch9 tr9 hf9 hhi9 hlo9 lg9 conf9 diff9 ex9 rt9 rtT9 rtc9 zp9 zhi9 zlo9 mkp9 mk9 wp9 wrep9 zm9 "
                      "bs9 bev9 lo9 gl9 ul9 sil9 hw9 hs9 hwhi9 hshi9 hwlo9 hslo9 yp9 ys9 yhi9 ylo9 y9 x9 out9 in09 in19 split9")
        HAVE_A, HAVE_G, HAVE_B, HAVE_DA, HAVE_D, HAVE_DB = 1, 3, 7, 9, 10, 11
        TERMS = ((0, 0), (0, 1), (1, 0))

        with nc.Block() as block:
            @block.gpsimd
            def _(g):
                two = lambda n: lambda r: r[:, 0:2 * n].rearrange("p (a n) -> p a n", a=2)
                some = lambda m, n: lambda r: r[:, 0:m * n].rearrange("p (m n) -> p m n", m=m)
                rows = lambda t, m0, m: t[m0 * P:(m0 + m) * P, :].rearrange("(m p) n -> p m n", p=P)
                fl = lambda w: w.rearrange("p k a n -> p k (a n)")
                chunks = [(rows(a["gu_A"], 0, KD), fl(WA[:, 0]), fl(WA[:, 1]), some(KD, 1024))]
                for k in range(KD):
                    chunks.append((a["base_gu"][k * P:(k + 1) * P, :], WG[:, 0, k].rearrange("p a n -> p (a n)"),
                                   WG[:, 1, k].rearrange("p a n -> p (a n)"), lambda r: r[:, 0:2 * HID1]))
                for w in range(2):
                    for t in range(0, ET1, 2):
                        chunks.append((rows(a["gu_B"], w * ET1 + t, 2), WB[:, 0, w, t:t + 2, :], WB[:, 1, w, t:t + 2, :], two(HID1)))
                for m0, m in ((0, 4), (4, 3)):
                    chunks.append((rows(a["d_A"], m0, m), WDA[:, 0, m0:m0 + m, :], WDA[:, 1, m0:m0 + m, :], some(m, E1 * R1)))
                chunks.append((rows(a["base_d"], 0, MT1), WD[:, 0], WD[:, 1], some(MT1, D)))
                chunks.append((rows(a["d_B"], 0, ET1), WDB[:, 0], WDB[:, 1], some(ET1, D)))
                split_weights(g, chunks, [raw[:, 0, :], raw[:, 1, :]], (s_in0, s_in1), s_split)

            @block.sync
            def _(sp):
                with sp.Fori(0, B) as b:
                    sp.wait_ge(s_x, b * TB + TB)
                    sp.dma_start(a["out"].rearrange("(t p) d -> p t d", p=P)[:, ds(b * TB, TB), :], p.X[:, ds(b * TB, TB), :]).then_inc(s_out, 16)
                sp.wait_ge(s_out, 16 * B)

            @block.scalar
            def _(act):
                with act.Fori(0, B) as b:
                    act.wait_ge(s_var, b + 1)
                    act.activation(p.ln_rs[:, 0:TB], p.ln_mv[:, :, 1], ACT.Sqrt, bias=p.eps[:, 0:1]).then_inc(s_sd, 1)
                    act.wait_ge(s_tr, b + 1)
                    hp = bank[0][:, :].rearrange("p (k n) -> p k n", k=KD)
                    act.activation(hf[:, :, :], hp, ACT.Copy).then_inc(s_hf, 1)
                    act.activation(hT[:, 0, :, :], hp, ACT.Copy).then_inc(s_hhi, 1)
                    act.wait_ge(s_lg, b + 1)
                    act.activation(conf[:, :, :], bank[1][:, 0:TB * E1].rearrange("p (t e) -> p t e", t=TB), ACT.Sigmoid).then_inc(s_conf, 1)
                    for i in range(4):
                        act.wait_ge(s_zp, b * 4 + i + 1)
                        act.activation(z[:, 0, i // 2, 2 * (i % 2):2 * (i % 2) + 2, :], bank[2 + i][:, :].rearrange("p (t n) -> p t n", t=2),
                                       ACT.Copy).then_inc(s_zhi, 1)
                    act.wait_ge(s_diff, b + 1)
                    act.activation(best[:, 2, :], best[:, 2, :], ACT.Exp).then_inc(s_ex, 1)
                    act.wait_ge(s_rtT, b + 1)
                    act.activation(RTf[:, :], bank[0][0:18, 0:S], ACT.Copy).then_inc(s_rtc, 1)
                    act.activation(RTb[:, :], bank[0][0:18, 0:S], ACT.Copy).then_inc(s_rtc, 1)
                    for t in range(ET1):
                        act.wait_ge(s_mkp, b * ET1 + t + 1)
                        act.activation(MK[:, t, :, :], bank[2 + t][:, :].rearrange("p (s n) -> p s n", s=2), ACT.Copy).then_inc(s_mk, 1)
                    act.wait_ge(s_wp, b + 1)
                    act.activation(wrep[:, :, :], bank[1][:, :].rearrange("p (s n) -> p s n", s=2), ACT.Copy).then_inc(s_wrep, 1)

                    def base_out(m):
                        act.wait_ge(s_bs, b * MT1 + m + 1)
                        if m >= 2:
                            act.wait_ge(s_ul, b * MT1 + m - 1)
                        act.activation(BS[:, m % 2, :, :], bank[6 + m % 2][:, :].rearrange("p (w n) -> p w n", w=2), ACT.Copy).then_inc(s_bev, 1)

                    def high(m):
                        act.wait_ge(s_hw, b * MT1 + m + 1)
                        act.activation(HW[:, 0, m, :], hw[:, m % 2, :, :].rearrange("p s n -> p (s n)"), ACT.Copy).then_inc(s_hwhi, 1)
                        act.wait_ge(s_hs, b * MT1 + m + 1)
                        act.activation(HS[:, 0, m, :], hs[:, m % 2, :], ACT.Copy).then_inc(s_hshi, 1)

                    base_out(0)
                    for m in range(MT1):
                        if m + 1 < MT1:
                            base_out(m + 1)
                        act.wait_ge(s_gl, b * MT1 + m + 1)
                        act.activation(sil[:, m % 2, :], gl[:, m % 2, :], ACT.Silu).then_inc(s_sil, 1)
                        if m >= 1:
                            high(m - 1)
                    high(MT1 - 1)
                    for t in range(ET1):
                        act.wait_ge(s_ys, b * ET1 + t + 1)
                        act.activation(YS[:, 0, t, :], ys[:, t, :], ACT.Copy).then_inc(s_yhi, 1)

            @block.vector
            def _(v):
                with v.Fori(0, B) as b:
                    ch = Chain(v, s_dch, b, LINKS_D)
                    xt = lambda t: p.X[:, ds(2 * b + t, 1), :].rearrange("p o n -> p (o n)")
                    layernorm(v, xt, p.ln_stats, p.ln_mv, p.xn, p.ln_rs, s_var, s_sd, ch, s_xn, b)
                    v.wait_ge(s_hhi, b + 1)
                    v.tensor_tensor(hT[:, 1, :, :], bank[0][:, :].rearrange("p (k n) -> p k n", k=KD), hT[:, 0, :, :], ALU.subtract).then_inc(s_hlo, 1)

                    v.wait_ge(s_conf, b + 1)
                    row = lambda r: r.rearrange("p (o e) -> p o e", o=1).broadcast_to([P, TB, E1])
                    col = lambda r: r.rearrange("p (t o) -> p t o", o=1).broadcast_to([P, TB, E1])
                    ch.link(v.tensor_tensor(conf[:, :, :], conf[:, :, :], row(worth[:, :]), ALU.mult))
                    for s in range(2):
                        mask = RT[:, :, s * E1:(s + 1) * E1]
                        ch.link(v.tensor_reduce(best[:, s, :], conf[:, :, :], AX.X, ALU.max))
                        ch.link(v.tensor_tensor(eq[:, :, :], conf[:, :, :], col(best[:, s, :]), ALU.is_equal))
                        ch.link(v.tensor_tensor(eq[:, :, :], eq[:, :, :], row(order[:, :]), ALU.mult))
                        ch.link(v.tensor_reduce(best[:, 3, :], eq[:, :, :], AX.X, ALU.min))
                        ch.link(v.tensor_tensor(mask, row(order[:, :]), col(best[:, 3, :]), ALU.is_equal))
                        if s == 0:
                            ch.link(v.scalar_tensor_tensor(conf[:, :, :], mask, -1e38, conf[:, :, :], ALU.mult, ALU.add))
                    v.tensor_tensor(best[:, 2, :], best[:, 1, :], best[:, 0, :], ALU.subtract).then_inc(s_diff, 1)
                    v.wait_ge(s_ex, b + 1)
                    ch.link(v.tensor_scalar(best[:, 3, :], best[:, 2, :], 1.0, None, ALU.add))
                    ch.link(v.reciprocal(RT[:, :, 16], best[:, 3, :]))
                    v.tensor_tensor(RT[:, :, 17], RT[:, :, 16], best[:, 2, :], ALU.mult).then_inc(s_rt, 1)
                    for i in range(4):
                        v.wait_ge(s_zhi, b * 4 + i + 1)
                        tt = slice(2 * (i % 2), 2 * (i % 2) + 2)
                        v.tensor_tensor(z[:, 1, i // 2, tt, :], bank[2 + i][:, :].rearrange("p (t n) -> p t n", t=2), z[:, 0, i // 2, tt, :],
                                        ALU.subtract).then_inc(s_zlo, 1)
                    v.wait_ge(s_zlo, b * 4 + 4)
                    v.wait_ge(s_mk, b * ET1 + ET1)
                    for w in range(2):
                        for x in range(2):
                            v.tensor_tensor(zm[:, x, w, :, :].rearrange("p t (s n) -> p t s n", s=2),
                                            z[:, x, w, :, :].rearrange("p t (o n) -> p t o n", o=1).broadcast_to([P, ET1, 2, S]),
                                            MK[:, :, :, :], ALU.mult).then_inc(s_zm, 1)
                    v.wait_ge(s_wrep, b + 1)

                    def adds(m):
                        v.wait_ge(s_bev, b * MT1 + m + 1)
                        for w, dst, s_done in ((0, gl, s_gl), (1, ul, s_ul)):
                            v.wait_ge(s_lo, b * 2 * MT1 + 2 * m + w + 1)
                            v.tensor_tensor(dst[:, m % 2, :].rearrange("p (s n) -> p s n", s=2),
                                            bank[2 + 2 * (m % 2) + w][:, :].rearrange("p (s n) -> p s n", s=2),
                                            BS[:, m % 2, w:w + 1, :].broadcast_to([P, 2, S]), ALU.add).then_inc(s_done, 1)

                    def finish(m):
                        v.wait_ge(s_sil, b * MT1 + m + 1)
                        v.wait_ge(s_ul, b * MT1 + m + 1)
                        hm = hw[:, m % 2, :, :]
                        ch.link(v.tensor_tensor(hm.rearrange("p s n -> p (s n)"), sil[:, m % 2, :], ul[:, m % 2, :], ALU.mult))
                        v.tensor_tensor(hm, hm, wrep[:, :, :], ALU.mult).then_inc(s_hw, 1)
                        v.wait_ge(s_hw, b * MT1 + m + 1)
                        v.tensor_tensor(hs[:, m % 2, :], hm[:, 0, :], hm[:, 1, :], ALU.add).then_inc(s_hs, 1)
                        v.wait_ge(s_hwhi, b * MT1 + m + 1)
                        v.tensor_tensor(HW[:, 1, m, :], hm.rearrange("p s n -> p (s n)"), HW[:, 0, m, :], ALU.subtract).then_inc(s_hwlo, 1)
                        v.wait_ge(s_hshi, b * MT1 + m + 1)
                        v.tensor_tensor(HS[:, 1, m, :], hs[:, m % 2, :], HS[:, 0, m, :], ALU.subtract).then_inc(s_hslo, 1)
                        v.wait_ge(s_hslo, b * MT1 + m + 1)

                    for m in range(MT1):
                        adds(m)
                        if m >= 1:
                            finish(m - 1)
                    finish(MT1 - 1)
                    for t in range(ET1):
                        v.wait_ge(s_yp, b * ET1 + t + 1)
                        ch.link(v.tensor_tensor(yt[:, t, :, :], bank[2 + t][:, :].rearrange("p (s n) -> p s n", s=2), MK[:, t, :, :], ALU.mult))
                        v.tensor_tensor(ys[:, t, :], yt[:, t, 0, :], yt[:, t, 1, :], ALU.add).then_inc(s_ys, 1)
                        v.wait_ge(s_yhi, b * ET1 + t + 1)
                        v.tensor_tensor(YS[:, 1, t, :], ys[:, t, :], YS[:, 0, t, :], ALU.subtract).then_inc(s_ylo, 1)
                    for t in range(TB):
                        v.wait_ge(s_y, b * TB + t + 1)
                        v.tensor_tensor(xt(t), bank[t][:, 0:D], xt(t), ALU.add).then_inc(s_x, 1)
                    ch.done()

            @block.tensor
            def _(pe):
                def rank(b):
                    for i in range(4):
                        for j in range(2):
                            n = 2 * i + j
                            w, t = n // ET1, n % ET1
                            for q, (x, y, k) in enumerate([(x, y, k) for x, y in TERMS for k in range(KD)]):
                                mm = pe.matmul(bank[2 + i][:, j * S:(j + 1) * S], WA[:, x, k, w, t * P:(t + 1) * P], hT[:, y, k, :],
                                               start=(q == 0), stop=(q == 5))
                        mm.then_inc(s_zp, 1)

                def base(b, m):
                    if m >= 2:
                        pe.wait_ge(s_bev, b * MT1 + m - 1)
                    for w in range(2):
                        for q, (x, y, k) in enumerate([(x, y, k) for x, y in TERMS for k in range(KD)]):
                            mm = pe.matmul(bank[6 + m % 2][:, w * S:(w + 1) * S], WG[:, x, k, w, m * P:(m + 1) * P], hT[:, y, k, :],
                                           start=(q == 0), stop=(q == 5))
                    mm.then_inc(s_bs, 1)

                def experts(b, m):
                    for w in range(2):
                        if m >= 2:
                            pe.wait_ge((s_gl, s_ul)[w], b * MT1 + m - 1)
                        elif m == 0:
                            pe.wait_ge(s_zm, b * 4 + 2 * w + 2)
                        for q, (x, y, t) in enumerate([(x, y, t) for x, y in TERMS for t in range(ET1)]):
                            mm = pe.matmul(bank[2 + 2 * (m % 2) + w][:, :], WB[:, x, w, t, m * P:(m + 1) * P], zm[:, y, w, t, :],
                                           start=(q == 0), stop=(q == 3 * ET1 - 1))
                        mm.then_inc(s_lo, 1)

                with pe.Fori(0, B) as b:
                    pe.wait_ge(s_xn, b + 1)
                    for k in range(KD):
                        for t in range(TB):
                            mm = pe.transpose(bank[0][:, k * S + t * P:k * S + (t + 1) * P], p.xn[:, t, k * P:(k + 1) * P], p.identf[:, :])
                    mm.then_inc(s_tr, 1)
                    pe.wait_ge(s_hf, b + 1)
                    for t in range(TB):
                        o = bank[1][:, t * E1:(t + 1) * E1]
                        pe.matmul(o, p.ones1[:, :], confb[:, :], start=True, stop=False)
                        for k in range(KD):
                            mm = pe.matmul(o, hf[:, k, t * P:(t + 1) * P], confT[:, k, :], start=False, stop=(k == KD - 1))
                    mm.then_inc(s_lg, 1)
                    pe.wait_ge(s_hlo, b + 1)
                    pe.wait_ge(s_split, HAVE_A)
                    rank(b)
                    pe.wait_ge(s_split, HAVE_G)
                    base(b, 0)
                    base(b, 1)
                    pe.wait_ge(s_rt, b + 1)
                    for t in range(TB):
                        mm = pe.transpose(bank[0][0:18, t * P:(t + 1) * P], RT[:, t, :], p.identf[:, :])
                    mm.then_inc(s_rtT, 1)
                    pe.wait_ge(s_rtc, b * 2 + 2)
                    pe.wait_ge(s_zlo, b * 4 + 4)
                    for t in range(ET1):
                        for s in range(2):
                            mm = pe.matmul(bank[2 + t][:, s * S:(s + 1) * S], pick[:, t, s, :], RTb[:, :], start=True, stop=True)
                        mm.then_inc(s_mkp, 1)
                    for s in range(2):
                        mm = pe.matmul(bank[1][:, s * S:(s + 1) * S], pickw[:, s, :], RTf[:, :], start=True, stop=True)
                    mm.then_inc(s_wp, 1)
                    pe.wait_ge(s_split, HAVE_B)
                    for m in range(MT1):
                        experts(b, m)
                        if m + 2 < MT1:
                            base(b, m + 2)
                    pe.wait_ge(s_split, HAVE_D)
                    pe.wait_ge(s_wrep, b + 1)
                    for m in range(MT1):
                        pe.wait_ge(s_hslo, b * MT1 + m + 1)
                        for t in range(TB):
                            for q, (x, y) in enumerate(TERMS):
                                pe.matmul(bank[t][:, 0:D], HS[:, x, m, t * P:(t + 1) * P], WD[:, y, m, :], start=(m == 0 and q == 0), stop=False)
                    for t in range(ET1):
                        for m in range(MT1):
                            for q, (x, y) in enumerate(TERMS):
                                mm = pe.matmul(bank[2 + t][:, :], WDA[:, x, m, t * P:(t + 1) * P], HW[:, y, m, :],
                                               start=(m == 0 and q == 0), stop=(m == MT1 - 1 and q == 2))
                        mm.then_inc(s_yp, 1)
                    pe.wait_ge(s_split, HAVE_DB)
                    for t in range(TB):
                        for e in range(ET1):
                            pe.wait_ge(s_ylo, b * ET1 + e + 1)
                            for q, (x, y) in enumerate(TERMS):
                                mm = pe.matmul(bank[t][:, 0:D], YS[:, x, e, t * P:(t + 1) * P], WDB[:, y, e, :], start=False,
                                               stop=(e == ET1 - 1 and q == 2))
                        mm.then_inc(s_y, 1)
                    pe.wait_ge(s_x, b * TB + TB)


def build(nc, args):
    p = Program(nc, args)
    with p.top:
        with p.attention:
            setup(p)
            first_attention(p)
            first_ffn(p)
            second_attention(p)
        second_ffn(p)


def kernel(**inputs):
    import numpy as np
    import concourse.bacc as bacc
    from concourse import mybir
    from concourse.bass_utils import run_bass_kernel_spmd

    f = {k: np.ascontiguousarray(v) for k, v in inputs.items()}
    T = lambda v: np.ascontiguousarray(v.T)
    L = {}
    L["x"] = f["x"].reshape(1024, 256)
    L["ctxT"] = T(f["ctx_2048"].reshape(1024, 256))
    L["mask_tok"] = T(f["mask_BxS2_if1"].reshape(8, 128))
    L["mask_row"] = f["mask_BxS2_if1"].reshape(1, 1024)
    wq = f["L0_xattn_w_q"].reshape(2, 4, 2, 2, 8, 256)
    L["wq0T"] = T(wq.transpose(0, 3, 4, 1, 2, 5).reshape(256, 256))
    L["wk0T"] = T(f["L0_xattn_w_k"].reshape(2, 4, 8, 256).transpose(2, 0, 1, 3).reshape(64, 256))
    L["wv0T"] = T(f["L0_xattn_w_v"])
    L["wo0T"] = np.ascontiguousarray(T(f["L0_xattn_w_o"]).reshape(2, 4, 2, 2, 8, 256).transpose(0, 3, 2, 1, 4, 5).reshape(256, 256))
    L["bo0"] = f["L0_xattn_b_o"].reshape(1, 256)
    L["w12T"] = np.concatenate([T(f["L0_ffn_w1"]), T(f["L0_ffn_w2"])], 1)
    L["w3T"] = np.concatenate([T(f["L0_ffn_w3"]), np.zeros((64, 256), np.float32)], 0)
    L["wq1"] = f["L1_xattn_wq"]
    L["wkv1"] = np.concatenate([f["L1_xattn_wk"], f["L1_xattn_wv"], f["L1_xattn_wk_ctx"], f["L1_xattn_wv_ctx"]], 1)
    L["wo1"] = f["L1_xattn_wo"]
    L["qkw"] = np.concatenate([f["L1_xattn_q_norm_w"], f["L1_xattn_k_norm_w"]]).reshape(1, 256)
    inv = (1.0 / np.float32(10000.0) ** (np.arange(0, 128, 2, dtype=np.float32) / np.float32(128))).astype(np.float32)
    ang = np.outer(np.arange(256, dtype=np.float32), inv).astype(np.float32)
    rope = np.stack([np.cos(ang), np.cos(ang), -np.sin(ang), np.sin(ang)], 1).astype(np.float32)
    L["rope"] = np.ascontiguousarray(rope.reshape(2, 128, 4, 64).transpose(1, 0, 2, 3))
    L["confT"] = T(f["L1_ffn_conf_W"])
    L["confb"] = f["L1_ffn_conf_b"].reshape(1, 8)
    L["wealth"] = f["L1_ffn_expert_wealth"].reshape(1, 8)
    L["base_gu"] = np.concatenate([f["L1_ffn_base_gate"], f["L1_ffn_base_up"]], 1)
    A = lambda n: f[n].transpose(1, 0, 2).reshape(f[n].shape[1], 512)
    L["gu_A"] = np.concatenate([A("L1_ffn_gate_A"), A("L1_ffn_up_A")], 1)
    L["gu_B"] = np.concatenate([f["L1_ffn_gate_B"].reshape(512, 896), f["L1_ffn_up_B"].reshape(512, 896)], 0)
    L["d_A"] = A("L1_ffn_down_A")
    L["base_d"] = f["L1_ffn_base_down"]
    L["d_B"] = f["L1_ffn_down_B"].reshape(512, 256)

    nc = bacc.Bacc("TRN2", target_bir_lowering=False, num_devices=1)
    arrays, args = {}, {}
    for name, v in L.items():
        v = np.ascontiguousarray(v)
        arrays[name + "_in"] = v
        args[name] = nc.dram_tensor(name + "_in", v.shape, mybir.dt.from_np(v.dtype), kind="ExternalInput").ap()
    args["out"] = nc.dram_tensor("out", (1024, 256), mybir.dt.float32, kind="ExternalOutput").ap()
    build(nc, args)
    r = run_bass_kernel_spmd(nc, [arrays], core_ids=[0])
    return r.results[0]["out"].reshape(4, 256, 256)
```

```python
import numpy as np
import concourse.bass as bass
from concourse import mybir
from contextlib import ExitStack

F32 = mybir.dt.float32
BF16 = mybir.dt.bfloat16
I32 = mybir.dt.int32
ALU = mybir.AluOpType
ACT = mybir.ActivationFunctionType
AX = mybir.AxisListType
ds = bass.ds

P = 128
B, S, D = 4, 256, 256
NT = B * S // P
TB = S // P
KD = D // P
NEG = -1e30
MAGIC = 12582912.0

G0, HG0, HD0 = 8, 4, 8
HALF = G0 // 2
NPART = 3
Q_TERM = (0, 0, 1, 1, 0, 2)
K_TERM = (0, 1, 0, 1, 2, 0)
ONES2 = float(np.array([0x3F803F80], np.uint32).view(np.float32)[0])
ROW_M, ROW_PAD = 48, 49
HID0 = 704
HT0 = 6

H1, KV1, HD1 = 16, 4, 128
REP1 = H1 // KV1
T1 = 256
CH = 512
E1, R1, HID1 = 8, 64, 896
MT1 = HID1 // P
ET1 = E1 * R1 // P
SCALING = 0.25
ROOM = 57344


class Chain:

    def __init__(self, eng, sem, i, per, start=0):
        self.eng, self.sem, self.i, self.per, self.start, self.k = eng, sem, i, per, start, 0

    def add(self, ins):
        ins.then_inc(self.sem, 1)
        self.k += 1

    def wait(self):
        self.eng.wait_ge(self.sem, self.i * self.per + self.start + self.k)

    def link(self, ins):
        self.add(ins)
        self.wait()

    def pause(self):
        self.wait()
        self.eng.sem_inc(self.sem, 1)
        self.k += 1

    def done(self, n=None):
        assert self.k == (self.per if n is None else n), f"{self.sem}: the body adds {self.k}"


def rounds(eng, body):
    with eng.Fori(0, B - 1) as b:
        body(b, b + 1)
    body(B - 1, None)


class Program:
    def __init__(self, nc, args):
        self.nc, self.a = nc, args
        self.top = ExitStack()

    def sb(self, name, shape, dt=F32, ctx=None):
        return (ctx or self.top).enter_context(self.nc.sbuf_tensor(name, shape, dt))

    def carve(self, shape, dt=BF16):
        n = int(np.prod(shape)) // (2 if dt == BF16 else 1)
        v = self.room[:, self.used:self.used + n]
        self.used += n
        assert self.used * 4 <= ROOM
        if dt == BF16:
            v = v.bitcast(BF16)
        names = "abcd"[:len(shape)]
        return v.rearrange(f"p ({' '.join(names)}) -> p {' '.join(names)}", **dict(zip(names, shape)))

    def ps(self, name, shape, ctx, dt=F32):
        return ctx.enter_context(self.nc.psum_tensor(name, shape, dt))

    def sems(self, ctx, names):
        return [ctx.enter_context(self.nc.semaphore(n)) for n in names.split()]


def layernorm(v, x, stats, mv, xn, rs, ln_var, ln_sd, chain, ready, it):
    for t in range(TB):
        chain.add(v.bn_stats(stats[:, t, :], x(t)))
    chain.pause()
    for t in range(TB):
        last = v.bn_aggr(mv[:, t, :], stats[:, t, :])
        if t == TB - 1:
            last.then_inc(ln_var, 1)
        else:
            chain.add(last)
    v.wait_ge(ln_sd, it + 1)
    chain.link(v.reciprocal(rs[:, TB:2 * TB], rs[:, 0:TB]))
    for t in range(TB):
        ins = v.tensor_scalar(xn[:, t, :], x(t), mv[:, t, 0:1], rs[:, TB + t:TB + t + 1], ALU.subtract, ALU.mult)
        if t == TB - 1:
            ins.then_inc(ready, 1)
        else:
            chain.add(ins)


def split_weights(p, g, chunks, raw):
    def load(n):
        src, hi, lo, view = chunks[n - first]
        g.dma_start(view(raw[:, n % 2, :]), src).then_inc(p.weight_in[n % 2], 16)
        g.dma_start(hi, src).then_inc(p.weight_in[n % 2], 16)

    first, last = p.split, p.split + len(chunks)
    load(first)
    for n in range(first, last):
        src, hi, lo, view = chunks[n - first]
        if n + 1 < last:
            if n >= 1:
                g.wait_ge(p.weight_split, n)
            load(n + 1)
        g.wait_ge(p.weight_in[n % 2], 32 * (n // 2 + 1))
        g.tensor_tensor(lo, view(raw[:, n % 2, :]), hi, ALU.subtract).then_inc(p.weight_split, 1)
    g.wait_ge(p.weight_split, last)
    p.split = last


def setup(p):
    nc, a = p.nc, p.a
    p.X = p.sb("X", [P, NT, D])
    p.identf = p.sb("identf", [P, P])
    p.identb = p.sb("identb", [P, P], BF16)
    p.eps = p.sb("eps", [P, 3])
    p.ones1 = p.sb("ones1", [1, P])
    p.ln_stats = p.sb("ln_stats", [P, TB, 6])
    p.ln_mv = p.sb("ln_mv", [P, TB, 2])
    p.ln_rs = p.sb("ln_rs", [P, 2 * TB])
    p.xn = p.sb("xn", [P, TB, D])
    p.weight_in = p.sems(p.top, "weight_in0 weight_in1")
    (p.weight_split,) = p.sems(p.top, "weight_split")
    p.split = 0
    p.room = p.sb("room", [P, ROOM // 4])
    p.used = 0
    p.CTS = p.carve([2, KD, B * S])
    p.WQ = p.carve([2, KD, H1 * HD1])
    p.WKV = p.carve([2, KD, 2, 2 * KV1 * HD1])
    p.WO = p.carve([2, H1, D])


def raw_weights(p, c):
    w12, w3 = KD * 2 * HID0, HT0 * D
    p.raw = p.sb("raw", [P, w12 + w3], F32, c)
    p.w12 = p.raw[:, 0:w12].rearrange("p (k n) -> p k n", k=KD)
    p.w3 = p.raw[:, w12:w12 + w3].rearrange("p (k n) -> p k n", k=HT0)


def first_attention(p):
    nc, a = p.nc, p.a
    with ExitStack() as c:
        sb = lambda n, s, dt=F32: p.sb(n, s, dt, c)
        wq = sb("wq0", [P, KD, D])
        wo = sb("wo0", [P, KD, D])
        bo = sb("bo0", [1, D])
        Vaug = sb("Vaug", [P, NT, G0, 32])
        Qst = sb("Qst", [P, 2, 8, B, S], BF16)
        Kst = sb("Kst", [P, 2, 2, HALF, B, S], BF16)
        triA = sb("triA", [P, 2, S], BF16)
        triB = sb("triB", [P, 2, S], BF16)
        k_scr = nc.dram_tensor("k_scr", [NPART, G0 * HD0, B * S], BF16).ap()
        q_scr = nc.dram_tensor("q_scr", [NPART, 2, P, B * S], BF16).ap()
        bank = [p.ps(f"a{i}", [P, 512], c) for i in range(8)]

        with ExitStack() as c1:
            CT = p.sb("CT", [P, KD, B * S], F32, c1)
            wk = p.sb("wk0", [P, KD, G0 * HD0], F32, c1)
            wv = p.sb("wv0", [P, KD, G0 * HD0], F32, c1)
            mask_i = p.sb("mask_i", [P, NT], I32, c1)
            mask_r = p.sb("mask_r", [1, B * S], I32, c1)
            valid = p.sb("valid", [P, NT], F32, c1)
            pad_row = p.sb("pad_row", [1, B * S], BF16, c1)
            one_row = p.sb("one_row", [1, B * S], BF16, c1)
            kp = p.sb("kp", [G0 * HD0, NPART, B * S], BF16, c1)
            kr = p.sb("kr", [G0 * HD0, 2, 512], F32, c1)
            stats = p.sb("stats0", [P, NT, 6], F32, c1)
            mv = p.sb("mv0", [P, NT, 2], F32, c1)
            rstd = p.sb("rstd0", [P, 2, NT], F32, c1)
            xT = p.sb("xT", [P, KD, S], F32, c1)
            qp = p.sb("qp", [P, NPART, 2, B, S], BF16, c1)
            qr = p.sb("qr", [P, 2, S], F32, c1)
            (s_x, s_wq, s_wo, s_ct, s_wk, s_m, s_eng, s_v, s_k, s_khi, s_kr, s_kout, s_kin, s_rows, s_zero,
             s_valid, s_va, s_dch, s_cts, s_var, s_sd, s_rstd, s_xn, s_tr, s_xT, s_q, s_qhi, s_qr, s_qp, s_qout, s_qinA, s_qinB, s_qinC) = \
                p.sems(c1, "x0 wq0 wo0 ct0 wk0 m0 eng0 v0 k0 khi0 kr0 kout0 kin0 rows0 zero0 valid0 va0 dch0 cts0 "
                           "var0 sd0 rstd0 xn0 tr0 xT0 q0 qhi0 qr0 qp0 qout0 qinA0 qinB0 qinC0")

            def stack_q(eng, e, terms, sem):
                for t in terms:
                    r = 64 * e + 8 * t
                    eng.dma_start(Qst[r:r + 8, :, :, :, :].rearrange("p h j b n -> p h (j b n)"),
                                  q_scr[Q_TERM[t], :, 64 * e:64 * e + 64, :].rearrange("h (d j) m -> d h (j m)", j=8)).then_inc(sem, 16)

            with nc.Block() as block:
                @block.sync
                def _(sp):
                    sp.dma_start(CT[:, :, :], a["ctxT"].rearrange("(k p) n -> p k n", p=P)).then_inc(s_ct, 16)
                    sp.dma_start(wk[:, :, :], a["wk0T"].rearrange("(k p) n -> p k n", p=P)).then_inc(s_wk, 16)
                    sp.dma_start(wv[:, :, :], a["wv0T"].rearrange("(k p) n -> p k n", p=P)).then_inc(s_wk, 16)
                    sp.dma_start(mask_i[:, :], a["mask_tok"]).then_inc(s_m, 16)
                    sp.dma_start(mask_r[:, :], a["mask_row"]).then_inc(s_m, 16)
                    sp.wait_ge(s_kr, 6)
                    sp.dma_start(k_scr.rearrange("a p m -> p a m"), kp[:, :, :]).then_inc(s_kout, 16)
                    sp.wait_ge(s_kout, 16)
                    sp.wait_ge(s_zero, 2)
                    for e in range(2):
                        for t in range(6):
                            sp.dma_start(Kst[64 * e + 8 * t:64 * e + 8 * t + 8, e, :, :, :, :].rearrange("p h j b n -> p (h j b n)"),
                                         k_scr[K_TERM[t], :, :].rearrange("(d g) m -> d (g m)", d=HD0)).then_inc(s_kin, 16)
                    with sp.Fori(0, B) as b:
                        sp.wait_ge(s_qp, b * 2 + 2)
                        sp.dma_start(q_scr[:, :, :, ds(b * S, S)].rearrange("a h p t -> p (a h) t"),
                                     qp[:, :, :, ds(b, 1), :].rearrange("p a h o t -> p (a h) (o t)")).then_inc(s_qout, 16)
                    sp.wait_ge(s_qout, B * 16)
                    stack_q(sp, 0, range(6), s_qinA)
                    sp.wait_ge(s_kin, 16 * 12)
                    sp.wait_ge(s_qinA, 16 * 6)

                @block.scalar
                def _(act):
                    act.dma_start(p.X[:, :, :], a["x"].rearrange("(t p) d -> p t d", p=P)).then_inc(s_x, 16)
                    act.dma_start(wq[:, :, :], a["wq0T"].rearrange("(k p) n -> p k n", p=P)).then_inc(s_wq, 16)
                    act.dma_start(wo[:, :, :], a["wo0T"].rearrange("(k p) n -> p k n", p=P)).then_inc(s_wo, 16)
                    act.dma_start(bo[:, :], a["bo0"]).then_inc(s_wo, 16)
                    act.wait_ge(s_eng, 1)
                    act.wait_ge(s_var, 1)
                    act.activation(rstd[:, 0, :], mv[:, :, 1], ACT.Sqrt, bias=p.eps[:, 0:1]).then_inc(s_sd, 1)
                    for n in range(2):
                        act.wait_ge(s_k, n + 1)
                        act.activation(kp[:, 0, n * 512:(n + 1) * 512], bank[2 + n][0:64, :], ACT.Copy).then_inc(s_khi, 1)

                    def turned(b):
                        act.wait_ge(s_tr, b + 1)
                        act.activation(xT[:, :, :], bank[4][:, :].rearrange("p (k n) -> p k n", k=KD), ACT.Copy).then_inc(s_xT, 1)

                    def body(b, nxt):
                        act.wait_ge(s_q, b + 1)
                        act.activation(qp[:, 0, :, ds(b, 1), :].rearrange("p h o n -> p h (o n)"), bank[5][:, :].rearrange("p (h n) -> p h n", h=2),
                                       ACT.Copy, scale=HD0 ** -0.5).then_inc(s_qhi, 1)
                        if nxt is not None:
                            turned(nxt)

                    turned(0)
                    rounds(act, body)
                    act.wait_ge(s_qout, B * 16)
                    stack_q(act, 1, range(3, 6), s_qinC)
                    act.wait_ge(s_qinC, 16 * 3)
                    act.wait_ge(s_wo, 32)

                @block.gpsimd
                def _(g):
                    g.memset(p.eps[:, 0:1], 1e-5).then_inc(s_eng, 1)
                    g.memset(p.eps[:, 1:2], HD1 * 1e-6).then_inc(s_eng, 1)
                    g.memset(p.eps[:, 2:3], 1e-6).then_inc(s_eng, 1)
                    g.memset(p.ones1[:, :], 1.0).then_inc(s_eng, 1)
                    g.memset(p.identf[:, :], 0.0).then_inc(s_eng, 1)
                    g.memset(p.identb[:, :], 0.0).then_inc(s_eng, 1)
                    g.memset(triA[:, :, :], 0.0).then_inc(s_eng, 1)
                    g.memset(triB[:, :, :], 0.0).then_inc(s_eng, 1)
                    g.wait_ge(s_eng, 8)
                    for m in (p.identf, p.identb):
                        g.affine_select(out=m[:, :], in_=m[:, :], compare_op=ALU.not_equal, fill=1.0, base=0,
                                        pattern=[[-1, P]], channel_multiplier=1).then_inc(s_eng, 1)
                    g.affine_select(out=triA[:, :, P:S], in_=triA[:, :, P:S], compare_op=ALU.is_ge, fill=NEG, base=0,
                                    pattern=[[0, 2], [-1, P]], channel_multiplier=1).then_inc(s_eng, 1)
                    g.affine_select(out=triB[:, :, 0:P], in_=triB[:, :, 0:P], compare_op=ALU.is_ge, fill=NEG, base=0,
                                    pattern=[[0, 2], [1, P]], channel_multiplier=-1).then_inc(s_eng, 1)
                    g.memset(Kst[:, :, :, :, :, :].rearrange("p e h j b n -> p (e h j b n)").bitcast(F32), 0.0).then_inc(s_zero, 1)
                    g.wait_ge(s_zero, 2)
                    g.wait_ge(s_valid, 2)
                    for e in range(2):
                        for r, row in ((ROW_M, one_row), (ROW_PAD, pad_row)):
                            g.dma_start(Kst[64 * e + r:64 * e + r + 1, e, :, :, :, :].rearrange("p h j b n -> p (h j) (b n)"),
                                        row[:, :].rearrange("p (o m) -> p o m", o=1).broadcast_to([1, 8, B * S])).then_inc(s_rows, 16)
                    g.wait_ge(s_rows, 16 * 4)
                    g.wait_ge(s_qout, B * 16)
                    stack_q(g, 1, range(3), s_qinB)
                    g.wait_ge(s_qinB, 16 * 3)

                @block.vector
                def _(v):
                    v.memset(one_row[:, :], 1.0).then_inc(s_valid, 1)
                    v.memset(Qst[:, :, :, :, :].rearrange("p h j b n -> p (h j b n)").bitcast(F32), ONES2).then_inc(s_zero, 1)
                    v.wait_ge(s_x, 16)
                    for t in range(NT):
                        v.bn_stats(stats[:, t, :], p.X[:, t, :]).then_inc(s_dch, 1)
                    v.wait_ge(s_dch, NT)
                    for t in range(NT):
                        v.bn_aggr(mv[:, t, :], stats[:, t, :]).then_inc(s_var if t == NT - 1 else s_dch, 1)
                    v.memset(Vaug[:, :, :, :], 0.0).then_inc(s_dch, 1)
                    v.wait_ge(s_m, 32)
                    v.tensor_scalar(pad_row[:, :], mask_r[:, :], 0.0, NEG, ALU.is_equal, ALU.mult).then_inc(s_valid, 1)
                    v.tensor_scalar(valid[:, :], mask_i[:, :], 0.0, None, ALU.not_equal).then_inc(s_dch, 1)
                    v.wait_ge(s_sd, 1)
                    v.reciprocal(rstd[:, 1, :], rstd[:, 0, :]).then_inc(s_rstd, 1)
                    for n in range(2):
                        cols = slice(n * 512, (n + 1) * 512)
                        v.wait_ge(s_khi, n + 1)
                        v.tensor_tensor(kr[:, n, :], bank[2 + n][0:64, :], kp[:, 0, cols], ALU.subtract).then_inc(s_kr, 1)
                        v.wait_ge(s_kr, 3 * n + 1)
                        v.tensor_copy(kp[:, 1, cols], kr[:, n, :]).then_inc(s_kr, 1)
                        v.wait_ge(s_kr, 3 * n + 2)
                        v.tensor_tensor(kp[:, 2, cols], kr[:, n, :], kp[:, 1, cols], ALU.subtract).then_inc(s_kr, 1)
                    v.wait_ge(s_dch, 2 * NT + 1)
                    v.wait_ge(s_v, 1)
                    v.tensor_tensor(Vaug[:, :, :, 0:8], bank[0][:, :].rearrange("p (t g d) -> p t g d", t=NT, g=G0),
                                    valid[:, :].rearrange("p (t a b) -> p t a b", a=1, b=1).broadcast_to([P, NT, G0, 8]),
                                    ALU.mult).then_inc(s_va, 1)
                    v.tensor_copy(Vaug[:, :, :, 8:9], valid[:, :].rearrange("p (t a b) -> p t a b", a=1, b=1).broadcast_to([P, NT, G0, 1])).then_inc(s_va, 1)
                    v.wait_ge(s_rstd, 1)

                    def normed(b):
                        for t in range(TB):
                            one = lambda r: r[:, ds(2 * b + t, 1), :].rearrange("p o n -> p (o n)")
                            v.tensor_scalar(p.xn[:, t, :], one(p.X), mv[:, ds(2 * b + t, 1), 0:1].rearrange("p a o -> p (a o)"),
                                            rstd[:, 1, ds(2 * b + t, 1)], ALU.subtract, ALU.mult).then_inc(s_xn, 1)

                    def body(b, nxt):
                        if nxt is not None:
                            v.wait_ge(s_tr, b + 1)
                            normed(nxt)
                        v.wait_ge(s_qhi, b + 1)
                        psq = bank[5][:, :].rearrange("p (h n) -> p h n", h=2)
                        part = lambda i: qp[:, i, :, ds(b, 1), :].rearrange("p h o n -> p h (o n)")
                        v.scalar_tensor_tensor(qr[:, :, :], psq, HD0 ** -0.5, part(0), ALU.mult, ALU.subtract).then_inc(s_qr, 1)
                        v.wait_ge(s_qr, b + 2)
                        v.tensor_copy(part(1), qr[:, :, :]).then_inc(s_qp, 1)
                        v.wait_ge(s_qp, b * 2 + 1)
                        v.tensor_tensor(part(2), qr[:, :, :], part(1), ALU.subtract).then_inc(s_qp, 1)
                        v.wait_ge(s_qp, b * 2 + 2)

                    v.sem_inc(s_qr, 1)
                    normed(0)
                    rounds(v, body)
                    v.tensor_copy(p.CTS[:, 0, :, :], CT[:, :, :]).then_inc(s_cts, 1)
                    v.wait_ge(s_cts, 1)
                    v.tensor_tensor(p.CTS[:, 1, :, :], CT[:, :, :], p.CTS[:, 0, :, :], ALU.subtract).then_inc(s_cts, 1)

                @block.tensor
                def _(pe):
                    pe.wait_ge(s_ct, 16)
                    pe.wait_ge(s_wk, 32)
                    for n in range(2):
                        for k in range(KD):
                            mm = pe.matmul(bank[2 + n][0:64, :], wk[:, k, :], CT[:, k, n * 512:(n + 1) * 512],
                                           start=(k == 0), stop=(k == KD - 1))
                        mm.then_inc(s_k, 1)
                    for t in range(NT):
                        for k in range(KD):
                            mm = pe.matmul(bank[0][:, t * 64:(t + 1) * 64], CT[:, k, t * P:(t + 1) * P], wv[:, k, :],
                                           start=(k == 0), stop=(k == KD - 1))
                    mm.then_inc(s_v, 1)
                    pe.wait_ge(s_eng, 10)
                    pe.wait_ge(s_wq, 16)

                    def turn(b):
                        pe.wait_ge(s_xn, b * TB + TB)
                        for k in range(KD):
                            for t in range(TB):
                                mm = pe.transpose(bank[4][:, k * S + t * P:k * S + (t + 1) * P], p.xn[:, t, k * P:(k + 1) * P], p.identf[:, :])
                        mm.then_inc(s_tr, 1)

                    def body(b, nxt):
                        pe.wait_ge(s_xT, b + 1)
                        pe.wait_ge(s_qr, b + 1)
                        for h in range(2):
                            for k in range(KD):
                                mm = pe.matmul(bank[5][:, h * S:(h + 1) * S], wq[:, k, h * P:(h + 1) * P], xT[:, k, :],
                                               start=(k == 0), stop=(k == KD - 1))
                        mm.then_inc(s_q, 1)
                        if nxt is not None:
                            turn(nxt)

                    turn(0)
                    rounds(pe, body)

        with ExitStack() as c2:
            NM = p.sb("NM", [P, 2, 2, 2, HALF, 2], F32, c2)
            nmT = p.sb("nmT", [64, P], BF16, c2)
            PT = p.sb("PT", [P, HALF, 1536], F32, c2)
            VS = p.sb("VS", [P, 2, 2, HALF, 32], F32, c2)
            OT = p.sb("OT", [P, 2, 1024], F32, c2)
            rinv = p.sb("rinv", [P, 2, 16], F32, c2)
            AO = p.xn
            AOT = p.sb("AOT", [P, KD, S], F32, c2)
            (s_a, s_fa, s_held, s_nt, s_nmT, s_ndma, s_s, s_e, s_pv, s_vs, s_ot, s_t, s_dch, s_ao, s_aot, s_aoT, s_y, s_xr, s_w) = \
                p.sems(c2, "a2 fa2 held2 nt2 nmT2 ndma2 s3 e3 pv3 vs3 ot3 t3 dch3 ao3 aot3 aoT3 y3 xr3 w3")
            NG = 2 * HALF
            with nc.Block() as block:
                @block.gpsimd
                def _(g):
                    chunks = []
                    for k in range(KD):
                        rows = slice(k * P, (k + 1) * P)
                        chunks.append((a["wq1"][rows, :], p.WQ[:, 0, k, :], p.WQ[:, 1, k, :], lambda r: r))
                        chunks.append((a["wkv1"][rows, :], p.WKV[:, 0, k, :, :].rearrange("p w n -> p (w n)"),
                                       p.WKV[:, 1, k, :, :].rearrange("p w n -> p (w n)"), lambda r: r))
                    for m in range(0, H1, 8):
                        chunks.append((a["wo1"][m * P:(m + 8) * P, :].rearrange("(m p) n -> p m n", p=P),
                                       p.WO[:, 0, m:m + 8, :], p.WO[:, 1, m:m + 8, :], lambda r: r.rearrange("p (m n) -> p m n", m=8)))
                    split_weights(p, g, chunks, p.raw[:, 0:4096].rearrange("p (s n) -> p s n", s=2))
                    g.dma_start(p.w12, a["w12T"].rearrange("(k p) n -> p k n", p=P)).then_inc(s_w, 16)
                    g.dma_start(p.w3, a["w3T"].rearrange("(k p) n -> p k n", p=P)).then_inc(s_w, 16)
                    g.wait_ge(s_w, 32)

                @block.sync
                def _(sp):
                    with sp.Fori(0, B) as b:
                        sp.wait_ge(s_nmT, b + 1)
                        for e in range(2):
                            for qb in range(2):
                                r = 64 * e + ROW_M
                                sp.dma_start(Qst[r:r + 1, :, :, ds(b, 1), qb * P:(qb + 1) * P].rearrange("p h j o n -> p (h j o) n"),
                                             nmT[(2 * e + qb) * 16:(2 * e + qb) * 16 + 16, :]).then_inc(s_ndma, 16)
                    sp.wait_ge(s_ndma, B * 64)

                @block.scalar
                def _(act):
                    def maxima_out(b, first=False):
                        act.wait_ge(s_nt, b + 1)
                        if not first:
                            act.wait_ge(s_ndma, b * 64)
                        act.activation(nmT[:, :], bank[3][0:64, 0:P], ACT.Copy).then_inc(s_nmT, 1)

                    def body(b, nxt):
                        for n in range(NG):
                            h, j = n // HALF, n % HALF
                            act.wait_ge(s_pv, b * 2 + h + 1)
                            for i in range(3):
                                act.wait_ge(s_s, b * 3 * NG + 3 * n + i + 1)
                                act.activation(PT[:, j, i * 512:(i + 1) * 512], bank[i][:, :], ACT.Exp).then_inc(s_e, 1)
                            if j == HALF - 1:
                                act.wait_ge(s_pv, b * 2 + h + 2)
                                act.activation(OT[:, h, 0:512], bank[6][:, :], ACT.Copy)
                                act.activation(OT[:, h, 512:1024], bank[7][:, :], ACT.Copy).then_inc(s_ot, 1)
                        if nxt is not None:
                            maxima_out(nxt)
                        act.wait_ge(s_aoT, b + 1)
                        act.activation(AOT[:, :, :], bank[6][:, :].rearrange("p (k n) -> p k n", k=KD), ACT.Copy).then_inc(s_aot, 1)

                    maxima_out(0, first=True)
                    rounds(act, body)

                @block.vector
                def _(v):
                    def maxima(b, n):
                        h, j = n // HALF, n % HALF
                        for i in range(3):
                            v.wait_ge(s_a, b * 3 * NG + 3 * n + i + 1)
                            if i == 0:
                                v.tensor_reduce(NM[:, :, 0, h, j, :].rearrange("p e q -> p q e"),
                                                bank[3][:, :].rearrange("p (q e n) -> p q e n", q=2, e=2), AX.X, ALU.max, negate=True).then_inc(s_fa, 1)
                            else:
                                v.tensor_reduce(NM[:, :, 1, h, j, i - 1], bank[3 + i][:, :].rearrange("p (e n) -> p e n", e=2),
                                                AX.X, ALU.max, negate=True).then_inc(s_fa, 1)

                    def normalise(b, h, ch):
                        v.wait_ge(s_t, b * 2 + h + 1)
                        for qb in range(TB):
                            T = bank[6 + qb][:, :].rearrange("p (m d) -> p m d", d=32)
                            ch.link(v.reciprocal(rinv[:, qb, :], T[:, :, 8]))
                            v.tensor_tensor(AO[:, qb, h * P:(h + 1) * P].rearrange("p (m d) -> p m d", d=8), T[:, :, 0:8],
                                            rinv[:, qb, :].rearrange("p (m o) -> p m o", o=1).broadcast_to([P, 16, 8]), ALU.mult).then_inc(s_ao, 1)

                    def body(b, nxt):
                        ch = Chain(v, s_dch, b, 4)
                        v.tensor_copy(VS[:, :, :, :, :].rearrange("p h k j d -> p k h (j d)"),
                                      Vaug[:, ds(2 * b, 2), :, :].rearrange("p k (h j) d -> p k h (j d)", h=2)).then_inc(s_vs, 1)
                        for n in range(NG):
                            if nxt is not None:
                                maxima(nxt, n)
                            if n % HALF == HALF - 1:
                                normalise(b, n // HALF, ch)
                        v.wait_ge(s_y, b + 1)
                        x = p.X[:, ds(2 * b, TB), :]
                        v.tensor_tensor(x, bank[7][:, :].rearrange("p (t d) -> p t d", t=TB), x, ALU.add).then_inc(s_xr, 1)
                        ch.done()

                    for n in range(NG):
                        maxima(0, n)
                    v.sem_inc(s_xr, 1)
                    rounds(v, body)

                @block.tensor
                def _(pe):
                    def maxima(b, n):
                        h, j = n // HALF, n % HALF
                        if n >= 1:
                            pe.wait_ge(s_fa, b * 3 * NG + 3 * n - 2)
                        elif not isinstance(b, int):
                            pe.wait_ge(s_nmT, b)
                        pe.matmul(bank[3][:, :], p.identb[:, :], triA[:, 0:1, P:S].broadcast_to([P, 4, P]), start=True, stop=False)
                        for pp in range(2):
                            q = Qst[:, h, 2 * j + pp, ds(b, 1), 0:P].rearrange("p o n -> p (o n)")
                            mm = pe.matmul(bank[3][:, pp * S:(pp + 1) * S], q, Kst[:, :, h, j, ds(b, 1), 0:P].rearrange("p e o n -> p (e o) n"),
                                           start=False, stop=(pp == 1))
                        mm.then_inc(s_a, 1)
                        for pp in range(2):
                            if n >= 1:
                                pe.wait_ge(s_fa, b * 3 * NG + 3 * n - 1 + pp)
                            elif not isinstance(b, int):
                                pe.wait_ge(s_fa, b * 3 * NG)
                            o = bank[4 + pp]
                            q = Qst[:, h, 2 * j + pp, ds(b, 1), P:S].rearrange("p o n -> p (o n)")
                            pe.matmul(o[:, :], q, Kst[:, :, h, j, ds(b, 1), :].rearrange("p e o n -> p (e o) n"), start=True, stop=False)
                            pe.matmul(o[:, :].rearrange("p (e n) -> p e n", e=2)[:, :, P:S], p.identb[:, :], triA[:, :, P:S],
                                      start=False, stop=True).then_inc(s_a, 1)

                    def turn_maxima(b):
                        pe.wait_ge(s_fa, b * 3 * NG + 3 * NG)
                        pe.sem_inc(s_held, 1)
                        pe.transpose(bank[3][0:64, 0:P], NM[:, :, :, :, :, :].rearrange("p e q h j r -> p (e q h j r)"), p.identf[:, :]).then_inc(s_nt, 1)

                    def scores(b, n):
                        h, j = n // HALF, n % HALF
                        qs = Qst[:, h, 2 * j:2 * j + 2, ds(b, 1), :].rearrange("p j o n -> p (j o) n")
                        for e in range(2):
                            if n >= 1:
                                pe.wait_ge(s_e, b * 3 * NG + 3 * n - 2 + e)
                            pe.matmul(bank[e][:, :], Kst[:, e, h, j, ds(b, 1), 0:P].rearrange("p o n -> p (o n)"), qs, start=True, stop=False)
                            pe.matmul(bank[e][:, :].rearrange("p (j n) -> p j n", j=2)[:, :, 0:P], p.identb[:, :], triB[:, :, 0:P],
                                      start=False, stop=True).then_inc(s_s, 1)
                        if n >= 1:
                            pe.wait_ge(s_e, b * 3 * NG + 3 * n)
                        pe.matmul(bank[2][:, :], p.identb[:, :], triB[:, 0:1, 0:P].broadcast_to([P, 4, P]), start=True, stop=False)
                        for e in range(2):
                            mm = pe.matmul(bank[2][:, e * S:(e + 1) * S], Kst[:, e, h, j, ds(b, 1), P:S].rearrange("p o n -> p (o n)"),
                                           qs[:, :, P:S], start=False, stop=(e == 1))
                        mm.then_inc(s_s, 1)

                    def products(b, h):
                        pe.wait_ge(s_e, b * 3 * NG + (h + 1) * 3 * HALF)
                        pe.wait_ge(s_vs, b + 1)
                        if h == 1:
                            pe.wait_ge(s_ao, b * 4 + 2)
                        else:
                            pe.wait_ge(s_xr, b + 1)
                        for e in range(2):
                            for j in range(HALF):
                                pe.matmul(bank[6 + e][32 * j:32 * j + 32, :], VS[:, h, 0, j, :], PT[:, j, e * 512:(e + 1) * 512],
                                          start=True, stop=False)
                            for j in range(HALF):
                                mm = pe.matmul(bank[6 + e][32 * j:32 * j + 32, :].rearrange("p (r q) -> p r q", r=2)[:, :, P:S], VS[:, h, 1, j, :],
                                               PT[:, j, 1024 + e * S:1024 + (e + 1) * S], start=False, stop=True)
                        mm.then_inc(s_pv, 1)

                    def turn(b, h):
                        pe.wait_ge(s_ot, b * 2 + h + 1)
                        for qb in range(TB):
                            for m in range(4):
                                mm = pe.transpose(bank[6 + qb][:, m * P:(m + 1) * P], OT[:, h, m * S + qb * P:m * S + (qb + 1) * P], p.identf[:, :])
                        mm.then_inc(s_t, 1)

                    def output(b):
                        pe.wait_ge(s_ao, b * 4 + 4)
                        for k in range(KD):
                            for t in range(TB):
                                mm = pe.transpose(bank[6][:, k * S + t * P:k * S + (t + 1) * P], AO[:, t, k * P:(k + 1) * P], p.identf[:, :])
                        mm.then_inc(s_aoT, 1)
                        pe.wait_ge(s_aot, b + 1)
                        for t in range(TB):
                            o = bank[7][:, t * D:(t + 1) * D]
                            pe.matmul(o, p.ones1[:, :], bo[:, :], start=True, stop=False)
                            for k in range(KD):
                                mm = pe.matmul(o, AOT[:, k, t * P:(t + 1) * P], wo[:, k, :], start=False, stop=(k == KD - 1))
                        mm.then_inc(s_y, 1)

                    def body(b, nxt):
                        pe.wait_ge(s_ndma, b * 64 + 64)
                        fill = iter(range(NG))

                        def between():
                            if nxt is not None:
                                maxima(nxt, next(fill))

                        for h in range(2):
                            for j in range(HALF):
                                if (h, j) != (1, 0):
                                    scores(b, h * HALF + j)
                                if j >= 1:
                                    between()
                            products(b, h)
                            if h == 0:
                                scores(b, HALF)
                            between()
                            turn(b, h)
                        if nxt is not None:
                            turn_maxima(nxt)
                        output(b)

                    for n in range(NG):
                        maxima(0, n)
                    turn_maxima(0)
                    pe.sem_inc(s_pv, 1)
                    rounds(pe, body)


LINKS_B0, LINKS_B = 14, 25


def first_ffn(p):
    nc, a = p.nc, p.a
    with ExitStack() as c:
        sb = lambda n, s, dt=F32: p.sb(n, s, dt, c)
        W12 = sb("W12", [P, KD, 2 * HID0], BF16)
        W3 = sb("W3", [P, HT0, D], BF16)
        mean = sb("mean", [P, 3])
        inv = sb("inv", [P, 3])
        w12, w3 = p.w12, p.w3
        with ExitStack() as c1:
            asum = p.sb("asum", [P, 3], F32, c1)
            ones = p.sb("ones", [P, P], F32, c1)
            tot = p.ps("tot", [P, 512], c1)
            (s_d, s_sum, s_tot, s_mean) = p.sems(c1, "d4 sum4 tot4 mean4")

            def ternary(eng, raw, out, m, link):
                link(eng.tensor_scalar(raw, raw, inv[:, m:m + 1], 1.0, ALU.mult, ALU.min))
                link(eng.tensor_scalar(raw, raw, -1.0, MAGIC, ALU.max, ALU.add))
                return eng.tensor_scalar(out, raw, MAGIC, None, ALU.subtract)

            with nc.Block() as block:
                @block.vector
                def _(v):
                    ch = Chain(v, s_d, 0, 0)
                    ch.add(v.memset(ones[:, :], 1.0))
                    for m in range(2):
                        ch.add(v.tensor_reduce(asum[:, m:m + 1], w12[:, :, m * HID0:(m + 1) * HID0], AX.XY, ALU.add, apply_absolute_value=True))
                    ch.add(v.tensor_reduce(asum[:, 2:3], w3[:, :, :], AX.XY, ALU.add, apply_absolute_value=True))
                    ch.wait()
                    v.tensor_copy(inv[:, :], asum[:, :]).then_inc(s_sum, 1)
                    v.wait_ge(s_tot, 1)
                    ch.link(v.tensor_scalar(mean[:, :], tot[:, 0:3], 1.0 / (D * HID0), 1e-5, ALU.mult, ALU.max))
                    v.reciprocal(inv[:, :], mean[:, :]).then_inc(s_mean, 1)
                    v.wait_ge(s_mean, 1)
                    for m in range(2):
                        cols = slice(m * HID0, (m + 1) * HID0)
                        ch.add(ternary(v, w12[:, :, cols], W12[:, :, cols], m, ch.link))

                @block.tensor
                def _(pe):
                    pe.wait_ge(s_sum, 1)
                    pe.matmul(tot[:, 0:3], ones[:, :], asum[:, :], start=True, stop=True).then_inc(s_tot, 1)

        am = sb("am", [P, TB])
        qs = sb("qs", [P, 2 * TB])
        sa = sb("sa", [P, 2 * TB])
        q = sb("q", [P, TB, D])
        hq = sb("hq", [P, TB, D], BF16)
        hqT = sb("hqT", [P, KD, S], BF16)
        sil = sb("sil", [P, TB, HID0])
        h = sb("h", [P, TB, HID0])
        hm = sb("hm", [P, 4, TB])
        h2 = sb("h2", [P, TB, HID0], BF16)
        h2T = sb("h2T", [P, TB, HT0, P], BF16)
        G = [p.ps(f"G{t}", [P, 1024], c) for t in range(TB)]
        U = [p.ps(f"U{t}", [P, 1024], c) for t in range(TB)]
        (s_var, s_sd, s_xn, s_dch, s_hq, s_tr, s_hqT, s_a, s_sa, s_sil, s_h2, s_ht, s_h2T, s_y, s_x, s_tern) = \
            p.sems(c, "var5 sd5 xn5 dch5 hq5 tr5 hqT5 a5 sa5 sil5 h25 ht5 h2T5 y5 x5 tern5")
        with nc.Block() as block:
            @block.gpsimd
            def _(g):
                ch = Chain(g, s_tern, 0, 0)
                ch.link(ternary(g, w3, W3[:, :, :], 2, ch.link))

            @block.scalar
            def _(act):
                def front(b):
                    act.wait_ge(s_var, b + 1)
                    act.activation(p.ln_rs[:, 0:TB], p.ln_mv[:, :, 1], ACT.Sqrt, bias=p.eps[:, 0:1]).then_inc(s_sd, 1)

                def turned(b):
                    act.wait_ge(s_tr, b + 1)
                    act.activation(hqT[:, :, :], G[1][:, 0:256].bitcast(BF16).rearrange("p (k n) -> p k n", k=KD), ACT.Copy).then_inc(s_hqT, 1)

                def body(b, nxt):
                    if nxt is not None:
                        front(nxt)
                    act.wait_ge(s_sa, b + 1)
                    for t in range(TB):
                        act.wait_ge(s_a, b * TB + t + 1)
                        act.activation(sil[:, t, :], G[t][:, 0:HID0], ACT.Silu, scale=sa[:, 2 * t:2 * t + 1]).then_inc(s_sil, 1)
                    if nxt is not None:
                        turned(nxt)
                    for t in range(TB):
                        act.wait_ge(s_ht, b * TB + t + 1)
                        src = G[t][:, 0:HT0 * 64].bitcast(BF16).rearrange("p (k n) -> p k n", n=P)
                        act.activation(h2T[:, t, 0:HT0 - 1, :], src[:, 0:HT0 - 1, :], ACT.Copy)
                        act.activation(h2T[0:64, t, HT0 - 1, :], src[0:64, HT0 - 1, :], ACT.Copy).then_inc(s_h2T, 1)

                front(0)
                turned(0)
                rounds(act, body)

            @block.vector
            def _(v):
                xt = lambda b, t: p.X[:, ds(2 * b + t, 1), :].rearrange("p o n -> p (o n)")

                def front(b, ch):
                    layernorm(v, lambda t: xt(b, t), p.ln_stats, p.ln_mv, p.xn, p.ln_rs, s_var, s_sd, ch, s_xn, b)
                    v.wait_ge(s_xn, b + 1)
                    ch.wait()
                    ch.link(v.tensor_reduce(am[:, :], p.xn[:, :, :], AX.X, ALU.max, apply_absolute_value=True))
                    ch.link(v.tensor_scalar(am[:, :], am[:, :], 1e-5, None, ALU.max))
                    ch.link(v.reciprocal(qs[:, 0:TB], am[:, :]))
                    ch.link(v.tensor_scalar(qs[:, 0:TB], qs[:, 0:TB], 127.0, None, ALU.mult))
                    ch.link(v.tensor_scalar(qs[:, TB:2 * TB], am[:, :], 1.0 / 127.0, None, ALU.mult))
                    for t in range(TB):
                        ch.add(v.tensor_scalar(q[:, t, :], p.xn[:, t, :], qs[:, t:t + 1], -128.0, ALU.mult, ALU.max))
                    ch.wait()
                    ch.link(v.tensor_scalar(q[:, :, :], q[:, :, :], 127.0, MAGIC, ALU.min, ALU.add))
                    v.tensor_scalar(hq[:, :, :], q[:, :, :], MAGIC, None, ALU.subtract).then_inc(s_hq, 1)

                def scales(b, ch):
                    ch.add(v.tensor_scalar(sa[:, 0:2 * TB:2], qs[:, TB:2 * TB], mean[:, 0:1], None, ALU.mult))
                    v.tensor_scalar(sa[:, 1:2 * TB:2], qs[:, TB:2 * TB], mean[:, 1:2], None, ALU.mult).then_inc(s_sa, 1)
                    v.wait_ge(s_sa, b + 1)

                def body(b, nxt):
                    ch = Chain(v, s_dch, b, LINKS_B, LINKS_B0)
                    scales(b, ch)
                    if nxt is not None:
                        front(nxt, ch)
                    for t in range(TB):
                        v.wait_ge(s_sil, b * TB + t + 1)
                        ch.add(v.scalar_tensor_tensor(h[:, t, :], U[t][:, 0:HID0], sa[:, 2 * t + 1:2 * t + 2], sil[:, t, :], ALU.mult, ALU.mult))
                    ch.wait()
                    ch.link(v.tensor_reduce(hm[:, 0, :], h[:, :, :], AX.X, ALU.max, apply_absolute_value=True))
                    ch.link(v.tensor_scalar(hm[:, 0, :], hm[:, 0, :], 1e-5, None, ALU.max))
                    ch.link(v.reciprocal(hm[:, 1, :], hm[:, 0, :]))
                    ch.add(v.tensor_scalar(hm[:, 2, :], hm[:, 1, :], 127.0, None, ALU.mult))
                    ch.link(v.tensor_scalar(hm[:, 3, :], hm[:, 0, :], 1.0 / 127.0, mean[:, 2:3], ALU.mult, ALU.mult))
                    for t in range(TB):
                        ch.add(v.tensor_scalar(h[:, t, :], h[:, t, :], hm[:, 2, t:t + 1], -128.0, ALU.mult, ALU.max))
                    ch.wait()
                    ch.link(v.tensor_scalar(h[:, :, :], h[:, :, :], 127.0, MAGIC, ALU.min, ALU.add))
                    for t in range(TB):
                        v.tensor_scalar(h2[:, t, :], h[:, t, :], MAGIC, None, ALU.subtract).then_inc(s_h2, 1)
                    for t in range(TB):
                        v.wait_ge(s_y, b * TB + t + 1)
                        v.scalar_tensor_tensor(xt(b, t), U[t][:, 0:D], hm[:, 3, t:t + 1], xt(b, t), ALU.mult, ALU.add).then_inc(s_x, 1)
                    if nxt is not None:
                        ch.done()

                v.sem_inc(s_x, 1)
                first = Chain(v, s_dch, 0, LINKS_B0)
                front(0, first)
                first.done()
                rounds(v, body)

            @block.tensor
            def _(pe):
                def turn(b):
                    pe.wait_ge(s_hq, b + 1)
                    gb = G[1][:, 0:256].bitcast(BF16)
                    for k in range(KD):
                        for t in range(TB):
                            mm = pe.transpose(gb[:, k * S + t * P:k * S + (t + 1) * P], hq[:, t, k * P:(k + 1) * P], p.identb[:, :])
                    mm.then_inc(s_tr, 1)

                def body(b, nxt):
                    pe.wait_ge(s_hqT, b + 1)
                    pe.wait_ge(s_x, b * TB + 1)
                    for t in range(TB):
                        for o, dst in ((0, G[t]), (HID0, U[t])):
                            for n0, n1 in ((0, 512), (512, HID0)):
                                for k in range(KD):
                                    mm = pe.matmul(dst[:, n0:n1], hqT[:, k, t * P:(t + 1) * P], W12[:, k, o + n0:o + n1],
                                                   start=(k == 0), stop=(k == KD - 1))
                        mm.then_inc(s_a, 1)
                    pe.wait_ge(s_sil, b * TB + TB)
                    if nxt is not None:
                        turn(nxt)
                        pe.wait_ge(s_hqT, nxt + 1)
                    pe.wait_ge(s_tern, 3)
                    for t in range(TB):
                        pe.wait_ge(s_h2, b * TB + t + 1)
                        gb = G[t][:, 0:HT0 * 64].bitcast(BF16)
                        for k in range(HT0):
                            n = min(P, HID0 - k * P)
                            mm = pe.transpose(gb[0:n, k * P:(k + 1) * P], h2[:, t, k * P:k * P + n], p.identb[:, :])
                        mm.then_inc(s_ht, 1)
                        pe.wait_ge(s_h2T, b * TB + t + 1)
                        for k in range(HT0):
                            n = min(P, HID0 - k * P)
                            mm = pe.matmul(U[t][:, 0:D], h2T[0:n, t, k, :], W3[0:n, k, :], start=(k == 0), stop=(k == HT0 - 1))
                        mm.then_inc(s_y, 1)

                turn(0)
                rounds(pe, body)


LINKS_C0, LINKS_C = 40, 88
LINKS_D0, LINKS_D = 20, 31


def second_attention(p):
    nc, a = p.nc, p.a
    NH = H1 + 2 * KV1
    CHUNKS = ("k", "kc", "v", "vc", "q0", "q1", "q2", "q3")
    with ExitStack() as c:
        sb = lambda n, s, dt=F32: p.sb(n, s, dt, c)
        CQ = sb("CQ", [P, TB, HD1])
        SQ = sb("SQ", [P, TB, HD1])
        CK = sb("CK", [P, TB, HD1])
        SK = sb("SK", [P, TB, HD1])
        WR = sb("WR", [P, 2, HD1])
        hT = sb("hT", [P, 2, KD, S], BF16)
        R = sb("R", [P, 3, CH])
        R2 = sb("R2", [P, CH])
        ssq = sb("ssq", [P, TB, NH])
        rms = sb("rms", [P, TB, NH])
        rk = sb("rk", [P, TB, NH])
        qT = sb("qT", [P, 2, H1, S], BF16)
        kT = sb("kT", [P, 2, KV1, T1 + S], BF16)
        V = sb("V", [P, 2, 4, KV1 * HD1], BF16)
        nm = sb("nm", [P, 2, 4])
        bias = sb("bias", [P, 2, 4])
        sm = sb("sm", [P, 2, 4])
        rs = sb("rs", [P, 2, 4])
        Pr = sb("Pr", [P, 2, REP1, 512])
        junk = Pr[:, 0, :, 0:HD1]
        raw = sb("rawC", [P, 2, HID1])
        PTs = sb("PTs", [P, 2, 4, 512], BF16)
        OT = sb("OT1", [P, 2, H1, S], BF16)
        bank = [p.ps(f"c{i}", [P, 512], c) for i in range(8)]
        mask = sb("mask1", [P, P], BF16)

        with ExitStack() as c1:
            rope = p.sb("rope", [P, TB, 4, 64], F32, c1)
            qkw = p.sb("qkw", [1, 2 * HD1], F32, c1)
            (s_w, s_wr, s_r, s_t, s_m) = p.sems(c1, "w6 wr6 r6 t6 m6")
            with nc.Block() as block:
                @block.sync
                def _(sp):
                    sp.dma_start(rope[:, :, :, :], a["rope"]).then_inc(s_w, 16)
                    sp.dma_start(qkw[:, :], a["qkw"]).then_inc(s_w, 16)

                @block.gpsimd
                def _(g):
                    g.memset(mask[:, :], 0.0).then_inc(s_m, 1)
                    g.wait_ge(s_m, 1)
                    g.affine_select(out=mask[:, :], in_=mask[:, :], compare_op=ALU.is_ge, fill=NEG, base=0,
                                    pattern=[[-1, P]], channel_multiplier=1).then_inc(s_m, 1)

                @block.vector
                def _(v):
                    v.wait_ge(s_wr, 1)
                    v.tensor_copy(WR[:, :, :], bank[0][:, 0:2 * HD1].rearrange("p (w n) -> p w n", w=2)).then_inc(s_r, 1)
                    v.wait_ge(s_r, 1)
                    for w, C_, S_ in ((0, CQ, SQ), (1, CK, SK)):
                        for t in range(TB):
                            v.tensor_tensor(C_[:, t, :], rope[:, t, 0:2, :].rearrange("p a n -> p (a n)"), WR[:, w, :], ALU.mult).then_inc(s_t, 1)
                            v.tensor_tensor(S_[:, t, 0:64], rope[:, t, 2, :], WR[:, w, 64:128], ALU.mult).then_inc(s_t, 1)
                            v.tensor_tensor(S_[:, t, 64:128], rope[:, t, 3, :], WR[:, w, 0:64], ALU.mult).then_inc(s_t, 1)

                @block.tensor
                def _(pe):
                    pe.wait_ge(s_w, 32)
                    pe.matmul(bank[0][:, 0:2 * HD1], p.ones1[:, :], qkw[:, :], start=True, stop=True).then_inc(s_wr, 1)

        NU = KV1 * TB
        KTS = [2 + 1 + u % TB for u in range(NU)]
        EV = sum(KTS)
        FIRST = [sum(KTS[:u]) for u in range(NU)]
        (s_var, s_sd, s_xn, s_dch, s_tr, s_hhi, s_hlo, s_pj, s_sq, s_vhi, s_vev, s_pf, s_rt, s_ro, s_ri, s_rT, s_rhi, s_rlo,
         s_s, s_nb, s_e, s_p, s_kT, s_evA, s_evD, s_pvk, s_ohi, s_olo, s_y, s_x) = \
            p.sems(c, "var7 sd7 xn7 dch7 tr7 hhi7 hlo7 pj7 sq7 vhi7 vev7 pf7 rt7 ro7 ri7 rT7 rhi7 rlo7 "
                      "s7 nb7 e7 p7 kT7 evA7 evD7 pvk7 ohi7 olo7 y7 x7")
        ROT = [ch for ch in CHUNKS if ch[0] != "v"]
        NR = len(ROT) * TB
        head0 = {"k": 0, "kc": KV1, "q0": 2 * KV1, "q1": 3 * KV1, "q2": 4 * KV1, "q3": 5 * KV1}
        steps = [(t, ch) for t in range(TB) for ch in CHUNKS]
        rsteps = [(t, ch) for t, ch in steps if ch[0] != "v"]

        def place(t, ch, part):
            if ch == "k":
                return kT[:, part, :, T1 + t * P:T1 + (t + 1) * P]
            if ch == "kc":
                return kT[:, part, :, t * P:(t + 1) * P]
            h = REP1 * int(ch[1])
            return qT[:, part, h:h + REP1, t * P:(t + 1) * P]

        with nc.Block() as block:
            @block.gpsimd
            def _(g):
                chunks = []
                for k in range(KD):
                    for w in range(2):
                        chunks.append((a["base_gu"][k * P:(k + 1) * P, w * HID1:(w + 1) * HID1], p.WG[:, 0, k, w, :], p.WG[:, 1, k, w, :],
                                       lambda r: r[:, 0:HID1]))
                for w in range(2):
                    for t in range(ET1):
                        r0 = (w * ET1 + t) * P
                        chunks.append((a["gu_B"][r0:r0 + P, :], p.WB[:, 0, w, t, :], p.WB[:, 1, w, t, :], lambda r: r[:, 0:HID1]))
                split_weights(p, g, chunks, raw)

            @block.scalar
            def _(act):
                def normed(b):
                    act.wait_ge(s_var, b + 1)
                    act.activation(p.ln_rs[:, 0:TB], p.ln_mv[:, :, 1], ACT.Sqrt, bias=p.eps[:, 0:1]).then_inc(s_sd, 1)

                def turned(b):
                    act.wait_ge(s_tr, b + 1)
                    act.activation(hT[:, 0, :, :], bank[0][:, :].rearrange("p (k n) -> p k n", k=KD), ACT.Copy).then_inc(s_hhi, 1)

                def project(b):
                    def hi_of(n):
                        t, ch = rsteps[n]
                        act.wait_ge(s_rT, b * NR + n + 1)
                        act.activation(place(t, ch, 0), bank[5 + n % 2][:, :].rearrange("p (h n) -> p h n", h=4), ACT.Copy).then_inc(s_rhi, 1)

                    r = 0
                    for n, (t, ch) in enumerate(steps):
                        act.wait_ge(s_pj, b * len(steps) + n + 1)
                        bk = bank[1 + n % 4]
                        if ch[0] == "v":
                            act.activation(V[:, 0, (2 if ch == "v" else 0) + t, :], bk[:, :], ACT.Copy).then_inc(s_vhi, 1)
                            continue
                        h0 = head0[ch]
                        for h in range(4):
                            ins = act.activation(junk[:, h, :], bk[:, h * HD1:(h + 1) * HD1], ACT.Square, accum_out=ssq[:, t, h0 + h:h0 + h + 1])
                        ins.then_inc(s_sq, 1)
                        act.wait_ge(s_sq, b * NR + r + 1)
                        if ch[0] == "k":
                            act.activation(rms[:, t, h0:h0 + 4], ssq[:, t, h0:h0 + 4], ACT.Sqrt, bias=p.eps[:, 2:3], scale=1.0 / HD1).then_inc(s_rt, 1)
                        else:
                            act.activation(rms[:, t, h0:h0 + 4], ssq[:, t, h0:h0 + 4], ACT.Sqrt, bias=p.eps[:, 1:2]).then_inc(s_rt, 1)
                        r += 1
                        if r >= 3:
                            hi_of(r - 3)
                    hi_of(NR - 2)
                    hi_of(NR - 1)

                def attend(b, nxt):
                    def exps(u, s):
                        g, t = u // TB, u % TB
                        w = 2 * u + s
                        nk = KTS[u] * P
                        act.wait_ge(s_nb, b * 2 * NU + w + 1)
                        for i in range(2):
                            h = 2 * s + i
                            ins = act.activation(Pr[:, u % 2, h, 0:nk], bank[2 * s + i][:, 0:nk], ACT.Exp, bias=bias[:, u % 2, h:h + 1],
                                                 scale=rk[:, t, 2 * KV1 + REP1 * g + h:2 * KV1 + REP1 * g + h + 1], accum_out=sm[:, u % 2, h:h + 1])
                        ins.then_inc(s_e, 1)

                    def evac(u, k):
                        i = FIRST[u] + k
                        if k < KTS[u]:
                            act.wait_ge(s_kT, b * EV + i + 1)
                            act.wait_ge(s_pvk, b * EV + i + 1)
                            act.activation(PTs[:, 0, i % 4, :], bank[4 + i % 2][:, :], ACT.Copy).then_inc(s_evA, 1)

                    exps(0, 0)
                    exps(0, 1)
                    for u in range(NU):
                        evac(u, 0)
                        evac(u, 1)
                        if u + 1 < NU:
                            exps(u + 1, 0)
                        if u == NU - 1 and nxt is not None:
                            turned(nxt)
                        evac(u, 2)
                        if u + 1 < NU:
                            exps(u + 1, 1)
                        evac(u, 3)
                        g, t = u // TB, u % TB
                        act.wait_ge(s_pvk, b * EV + FIRST[u] + KTS[u] + 4)
                        act.activation(OT[:, 0, REP1 * g:REP1 * g + REP1, t * P:(t + 1) * P],
                                       bank[6 + u % 2][:, :].rearrange("p (h n) -> p h n", h=4), ACT.Copy).then_inc(s_ohi, 1)
                        if u == NU - 2 and nxt is not None:
                            normed(nxt)

                def body(b, nxt):
                    attend(b, nxt)
                    if nxt is not None:
                        project(nxt)

                act.sem_inc(s_e, 2)
                normed(0)
                turned(0)
                project(0)
                rounds(act, body)

            @block.vector
            def _(v):
                xt = lambda b, t: p.X[:, ds(2 * b + t, 1), :].rearrange("p o n -> p (o n)")

                def normed(b, ch_):
                    layernorm(v, lambda t: xt(b, t), p.ln_stats, p.ln_mv, p.xn, p.ln_rs, s_var, s_sd, ch_, s_xn, b)

                def turned(b):
                    v.wait_ge(s_hhi, b + 1)
                    v.tensor_tensor(hT[:, 1, :, :], bank[0][:, :].rearrange("p (k n) -> p k n", k=KD), hT[:, 0, :, :], ALU.subtract).then_inc(s_hlo, 1)

                def add_result(b):
                    v.wait_ge(s_y, b + 1)
                    x = p.X[:, ds(2 * b, TB), :]
                    v.tensor_tensor(x, bank[7][:, :].rearrange("p (t d) -> p t d", t=TB), x, ALU.add).then_inc(s_x, 1)

                def project(b, prev, ch_):
                    def lo_of(n):
                        t, ch = rsteps[n]
                        v.wait_ge(s_rhi, b * NR + n + 1)
                        v.tensor_tensor(place(t, ch, 1), bank[5 + n % 2][:, :].rearrange("p (h n) -> p h n", h=4), place(t, ch, 0), ALU.subtract).then_inc(s_rlo, 1)

                    r = nv = 0
                    for n, (t, ch) in enumerate(steps):
                        if ch[0] == "v":
                            nv += 1
                            row = (2 if ch == "v" else 0) + t
                            v.wait_ge(s_vhi, b * 2 * TB + nv)
                            v.tensor_tensor(V[:, 1, row, :], bank[1 + n % 4][:, :], V[:, 0, row, :], ALU.subtract).then_inc(s_vev, 1)
                            continue
                        bk = bank[1 + n % 4][:, :].rearrange("p (h a n) -> p h a n", h=4, a=2)
                        bf = bank[1 + n % 4][:, :].rearrange("p (h n) -> p h n", h=4)
                        h0 = head0[ch]
                        Rf = R[:, r % 3, :].rearrange("p (h n) -> p h n", h=4)
                        R2h = R2[:, :].rearrange("p (h a n) -> p h a n", h=4, a=2)
                        v.wait_ge(s_sq, b * NR + r + 1)
                        full = lambda tab: tab.rearrange("p (o n) -> p o n", o=1).broadcast_to([P, 4, tab.shape[-1]])
                        if ch == "kc":
                            ch_.add(v.tensor_tensor(Rf, bf, full(WR[:, 1, :]), ALU.mult))
                        else:
                            C_, S_ = (CK, SK) if ch == "k" else (CQ, SQ)
                            ch_.add(v.tensor_tensor(Rf, bf, full(C_[:, t, :]), ALU.mult))
                            ch_.add(v.tensor_tensor(R2h[:, :, 0, :], bk[:, :, 1, :], full(S_[:, t, 0:64]), ALU.mult))
                            ch_.add(v.tensor_tensor(R2h[:, :, 1, :], bk[:, :, 0, :], full(S_[:, t, 64:128]), ALU.mult))
                        v.wait_ge(s_rt, b * NR + r + 1)
                        ins = v.reciprocal(rk[:, t, h0:h0 + 4], rms[:, t, h0:h0 + 4])
                        ins.then_inc(s_pf, 1)
                        ch_.wait()
                        if ch == "k":
                            ch_.link(v.tensor_tensor(R[:, r % 3, :], R[:, r % 3, :], R2[:, :], ALU.add))
                        if ch[0] == "k":
                            v.wait_ge(s_pf, b * NR + r + 1)
                            v.tensor_tensor(Rf, Rf, rk[:, t, h0:h0 + 4].rearrange("p (h o) -> p h o", o=1).broadcast_to([P, 4, HD1]), ALU.mult).then_inc(s_ro, 1)
                        else:
                            v.tensor_tensor(R[:, r % 3, :], R[:, r % 3, :], R2[:, :], ALU.add).then_inc(s_ro, 1)
                        r += 1
                        if r >= 3:
                            lo_of(r - 3)
                        v.wait_ge(s_ro, b * NR + r)
                    lo_of(NR - 2)
                    lo_of(NR - 1)
                    if prev is not None:
                        add_result(prev)

                def attend(b, nxt, ch_):
                    def maxima(u, s):
                        g, t = u // TB, u % TB
                        w = 2 * u + s
                        nk = KTS[u] * P
                        v.wait_ge(s_s, b * 2 * NU + w + 1)
                        for i in range(2):
                            ch_.add(v.tensor_reduce(nm[:, u % 2, 2 * s + i:2 * s + i + 1], bank[2 * s + i][:, 0:nk], AX.X, ALU.max, negate=True))
                        ch_.wait()
                        h = 2 * KV1 + REP1 * g + 2 * s
                        v.tensor_tensor(bias[:, u % 2, 2 * s:2 * s + 2], nm[:, u % 2, 2 * s:2 * s + 2], rk[:, t, h:h + 2], ALU.mult).then_inc(s_nb, 1)

                    def norms(u, s):
                        nk = KTS[u] * P
                        v.wait_ge(s_e, b * 2 * NU + 2 * u + s + 3)
                        ch_.link(v.reciprocal(rs[:, u % 2, 2 * s:2 * s + 2], sm[:, u % 2, 2 * s:2 * s + 2]))
                        for h in (2 * s, 2 * s + 1):
                            v.tensor_scalar(Pr[:, u % 2, h, 0:nk], Pr[:, u % 2, h, 0:nk], rs[:, u % 2, h:h + 1], None, ALU.mult).then_inc(s_p, 1)

                    def evac(u, k):
                        i = FIRST[u] + k
                        if k < KTS[u]:
                            v.wait_ge(s_evA, b * EV + i + 1)
                            v.tensor_tensor(PTs[:, 1, i % 4, :], bank[4 + i % 2][:, :], PTs[:, 0, i % 4, :], ALU.subtract).then_inc(s_evD, 1)

                    maxima(0, 0)
                    maxima(0, 1)
                    norms(0, 0)
                    norms(0, 1)
                    for u in range(NU):
                        g, t = u // TB, u % TB
                        if u + 1 < NU:
                            maxima(u + 1, 0)
                        evac(u, 0)
                        if u + 1 < NU:
                            maxima(u + 1, 1)
                        evac(u, 1)
                        if u + 1 < NU:
                            norms(u + 1, 0)
                        if u == NU - 1 and nxt is not None:
                            turned(nxt)
                        evac(u, 2)
                        evac(u, 3)
                        if u + 1 < NU:
                            norms(u + 1, 1)
                        v.wait_ge(s_ohi, b * NU + u + 1)
                        hd = slice(REP1 * g, REP1 * g + REP1)
                        v.tensor_tensor(OT[:, 1, hd, t * P:(t + 1) * P], bank[6 + u % 2][:, :].rearrange("p (h n) -> p h n", h=4),
                                        OT[:, 0, hd, t * P:(t + 1) * P], ALU.subtract).then_inc(s_olo, 1)
                        if u == NU - 2 and nxt is not None:
                            normed(nxt, ch_)

                def body(b, nxt):
                    ch_ = Chain(v, s_dch, b, LINKS_C, LINKS_C0)
                    attend(b, nxt, ch_)
                    if nxt is not None:
                        project(nxt, b, ch_)
                        ch_.done()
                    else:
                        add_result(b)

                v.sem_inc(s_evD, 2)
                v.sem_inc(s_x, 1)
                first = Chain(v, s_dch, 0, LINKS_C0)
                normed(0, first)
                turned(0)
                project(0, None, first)
                first.done()
                rounds(v, body)

            @block.tensor
            def _(pe):
                def turned(b):
                    pe.wait_ge(s_xn, b + 1)
                    for k in range(KD):
                        for t in range(TB):
                            mm = pe.transpose(bank[0][:, k * S + t * P:k * S + (t + 1) * P], p.xn[:, t, k * P:(k + 1) * P], p.identf[:, :])
                    mm.then_inc(s_tr, 1)

                WO_TERMS = [(t, x, w, h) for t in range(TB) for x, w in ((0, 0), (0, 1), (1, 0)) for h in range(H1)]

                def output(b, n0, n1):
                    half = len(WO_TERMS) // TB
                    for n in range(n0, n1):
                        t, x, w, h = WO_TERMS[n]
                        mm = pe.matmul(bank[7][:, t * D:(t + 1) * D], OT[:, x, h, t * P:(t + 1) * P], p.WO[:, w, h, :],
                                       start=(n % half == 0), stop=(n % half == half - 1))
                        if n == len(WO_TERMS) - 1:
                            mm.then_inc(s_y, 1)

                def project(b, prev):
                    def turn(n):
                        pe.wait_ge(s_ro, b * NR + n + 1)
                        if n >= 2:
                            pe.wait_ge(s_rlo, b * NR + n - 1)
                        for h in range(4):
                            mm = pe.transpose(bank[5 + n % 2][:, h * P:(h + 1) * P], R[:, n % 3, h * HD1:(h + 1) * HD1], p.identf[:, :])
                        mm.then_inc(s_rT, 1)

                    r = nv = 0
                    used = {}
                    for n, (t, ch) in enumerate(steps):
                        if n == 0:
                            pe.wait_ge(s_hlo, b + 1)
                        if n % 4 in used:
                            sem, per, cnt = used[n % 4]
                            pe.wait_ge(sem, b * per + cnt)
                        if ch[-1] == "c":
                            act_ = lambda part, k: p.CTS[:, part, k, ds(b * S + t * P, P)]
                        else:
                            act_ = lambda part, k: hT[:, part, k, t * P:(t + 1) * P]
                        if ch[0] == "q":
                            w_ = lambda part, k: p.WQ[:, part, k, int(ch[1]) * CH:(int(ch[1]) + 1) * CH]
                        else:
                            w_ = lambda part, k: p.WKV[:, part, k, int(ch[-1] == "c"), (CH if ch[0] == "v" else 0):(2 * CH if ch[0] == "v" else CH)]
                        terms = [(x, w, k) for x, w in ((0, 0), (0, 1), (1, 0)) for k in range(KD)]
                        for i, (x, w, k) in enumerate(terms):
                            mm = pe.matmul(bank[1 + n % 4][:, :], act_(x, k), w_(w, k), start=(i == 0), stop=(i == len(terms) - 1))
                        mm.then_inc(s_pj, 1)
                        if prev is not None:
                            if n == 0:
                                pe.wait_ge(s_olo, prev * NU + NU)
                            each = len(WO_TERMS) // len(steps)
                            output(prev, n * each, (n + 1) * each)
                        if ch[0] == "v":
                            nv += 1
                            used[n % 4] = (s_vev, 2 * TB, nv)
                        else:
                            r += 1
                            used[n % 4] = (s_pf, NR, r)
                            if r >= 3:
                                turn(r - 3)
                    turn(NR - 2)
                    turn(NR - 1)

                def attend(b, nxt):
                    pe.wait_ge(s_rlo, b * NR + NR)
                    pe.wait_ge(s_vev, b * 2 * TB + 2 * TB)

                    def scores(u, s):
                        g, t = u // TB, u % TB
                        nk = KTS[u] * P
                        pe.wait_ge(s_e, b * 2 * NU + 2 * u + s + 1)
                        for i in range(2):
                            h = REP1 * g + 2 * s + i
                            o = bank[2 * s + i]
                            for n, (x, y) in enumerate(((0, 0), (0, 1), (1, 0))):
                                pe.matmul(o[:, 0:nk], qT[:, x, h, t * P:(t + 1) * P], kT[:, y, g, 0:nk], start=(n == 0), stop=False)
                            mm = pe.matmul(o[:, nk - P:nk], p.identb[:, :], mask[:, :], start=False, stop=True)
                        mm.then_inc(s_s, 1)

                    def spread(u, k):
                        i = FIRST[u] + k
                        pe.wait_ge(s_evD, b * EV + i + 1)
                        for h in range(REP1):
                            if k == 0 and h % 2 == 0:
                                pe.wait_ge(s_p, b * 4 * NU + 4 * u + h + 2)
                            mm = pe.transpose(bank[4 + i % 2][:, h * P:(h + 1) * P], Pr[:, u % 2, h, k * P:(k + 1) * P], p.identf[:, :])
                        mm.then_inc(s_kT, 1)

                    def product(u, k):
                        i = FIRST[u] + k
                        if k == 0 and u >= 2:
                            pe.wait_ge(s_olo, b * NU + u - 1)
                        if k == 0 and u == 1:
                            pe.wait_ge(s_x, b + 1)
                        pe.wait_ge(s_evD, b * EV + i + 3)
                        g = u // TB
                        for n, (x, y) in enumerate(((0, 0), (0, 1), (1, 0))):
                            mm = pe.matmul(bank[6 + u % 2][:, :], V[:, x, k, g * HD1:(g + 1) * HD1], PTs[:, y, i % 4, :],
                                           start=(k == 0 and n == 0), stop=(k == KTS[u] - 1 and n == 2))
                        mm.then_inc(s_pvk, 1)

                    scores(0, 0)
                    scores(0, 1)
                    for u in range(NU):
                        spread(u, 0)
                        if u + 1 < NU:
                            scores(u + 1, 0)
                        spread(u, 1)
                        if u + 1 < NU:
                            scores(u + 1, 1)
                        if u == NU - 1 and nxt is not None:
                            turned(nxt)
                        for k in range(KTS[u]):
                            product(u, k)
                            if k + 2 < KTS[u]:
                                spread(u, k + 2)

                def body(b, nxt):
                    attend(b, nxt)
                    if nxt is not None:
                        project(nxt, b)
                    else:
                        pe.wait_ge(s_olo, b * NU + NU)
                        output(b, 0, len(WO_TERMS))

                pe.sem_inc(s_pvk, 4)
                turned(0)
                project(0, None)
                rounds(pe, body)


def expert_weights(p):
    p.WG = p.sb("WG", [P, 2, KD, 2, HID1], BF16)
    p.WB = p.sb("WB", [P, 2, 2, ET1, HID1], BF16)


def second_ffn(p):
    nc, a = p.nc, p.a
    with ExitStack() as c:
        sb = lambda n, s, dt=F32: p.sb(n, s, dt, c)
        p.used = 0
        WA = sb("WA", [P, 2, KD, 2, E1 * R1], BF16)
        WG, WB = p.WG, p.WB
        WDA = p.carve([2, MT1, E1 * R1])
        WD = p.carve([2, MT1, D])
        WDB = p.carve([2, ET1, D])
        raw = sb("rawD", [P, 2, 2048])
        confT = sb("confT", [P, KD, E1])
        confb = sb("confb", [1, E1])
        wealth = sb("wealth", [1, E1])
        worth = sb("worth", [P, E1])
        order = sb("order", [P, E1])
        pick = sb("pick", [18, ET1, 2, P], BF16)
        pickw = sb("pickw", [18, 2, P])
        hf = sb("hf", [P, KD, S])
        hT = sb("hTd", [P, 2, KD, S], BF16)
        conf = sb("conf", [P, TB, E1])
        eq = sb("eq", [P, TB, E1])
        best = sb("best", [P, 4, TB])
        RT = sb("RT", [P, TB, 18])
        RTf = sb("RTf", [18, S])
        RTb = sb("RTb", [18, S], BF16)
        MK = sb("MK", [P, ET1, 2, S], BF16)
        wrep = sb("wrep", [P, 2, S])
        z = p.carve([2, 2, ET1, S])
        zm = p.carve([2, 2, ET1, 2 * S])
        BS = sb("BS", [P, 2, 2, S])
        gl = sb("gl", [P, 2, 2 * S])
        ul = sb("ul", [P, 2, 2 * S])
        sil = sb("silD", [P, 2, 2 * S])
        hw = sb("hw", [P, 2, 2, S])
        hs = sb("hs", [P, 2, S])
        HW = sb("HW", [P, 2, MT1, 2 * S], BF16)
        HS = sb("HS", [P, 2, MT1, S], BF16)
        yt = sb("yt", [P, ET1, 2, S])
        ys = sb("ys", [P, ET1, S])
        YS = p.carve([2, ET1, S])
        bank = [p.ps(f"d{i}", [P, 512], c) for i in range(8)]
        (s_c, s_sel, s_wl, s_wt) = p.sems(c, "c8 sel8 wl8 wt8")
        with nc.Block() as block:
            @block.sync
            def _(sp):
                sp.dma_start(confT[:, :, :], a["confT"].rearrange("(k p) e -> p k e", p=P)).then_inc(s_c, 16)
                sp.dma_start(confb[:, :], a["confb"]).then_inc(s_c, 16)
                sp.dma_start(wealth[:, :], a["wealth"]).then_inc(s_c, 16)
                sp.wait_ge(s_c, 48)

            @block.gpsimd
            def _(g):
                g.memset(pick[:, :, :, :], 0.0).then_inc(s_sel, 1)
                g.memset(pickw[:, :, :], 0.0).then_inc(s_sel, 1)
                g.wait_ge(s_sel, 2)
                for s in range(2):
                    for t in range(ET1):
                        v = pick[:, t, s, :].rearrange("k (h n) -> k h n", h=2)
                        g.affine_select(out=v, in_=v, compare_op=ALU.not_equal, fill=SCALING, base=-(E1 * s + 2 * t),
                                        pattern=[[-1, 2], [0, R1]], channel_multiplier=1).then_inc(s_sel, 1)
                    g.affine_select(out=pickw[:, s, :], in_=pickw[:, s, :], compare_op=ALU.not_equal, fill=1.0, base=-(2 * E1 + s),
                                    pattern=[[0, P]], channel_multiplier=1).then_inc(s_sel, 1)

            @block.vector
            def _(v):
                for e in range(E1):
                    v.memset(order[:, e:e + 1], e - 99.0).then_inc(s_wt, 1)
                v.wait_ge(s_wl, 1)
                v.tensor_copy(worth[:, :], bank[0][:, 0:E1]).then_inc(s_wt, 1)

            @block.tensor
            def _(pe):
                pe.wait_ge(s_c, 48)
                pe.matmul(bank[0][:, 0:E1], p.ones1[:, :], wealth[:, :], start=True, stop=True).then_inc(s_wl, 1)

        (s_var, s_sd, s_xn, s_dch, s_tr, s_hf, s_hhi, s_hlo, s_lg, s_conf, s_diff, s_ex, s_rt, s_rtT, s_rtc, s_zp, s_zhi, s_zlo,
         s_mkp, s_mk, s_wp, s_wrep, s_zm, s_bs, s_bev, s_lo, s_gl, s_ul, s_sil, s_hw, s_hs, s_hwhi, s_hshi, s_hwlo, s_hslo,
         s_yp, s_ys, s_yhi, s_ylo, s_y, s_x, s_out) = \
            p.sems(c, "var9 sd9 xn9 dch9 tr9 hf9 hhi9 hlo9 lg9 conf9 diff9 ex9 rt9 rtT9 rtc9 zp9 zhi9 zlo9 mkp9 mk9 wp9 wrep9 zm9 "
                      "bs9 bev9 lo9 gl9 ul9 sil9 hw9 hs9 hwhi9 hshi9 hwlo9 hslo9 yp9 ys9 yhi9 ylo9 y9 x9 out9")
        HAVE_A, HAVE_D, HAVE_DA, HAVE_DB = (p.split + n for n in (1, 2, 4, 5))
        TERMS = ((0, 0), (0, 1), (1, 0))

        with nc.Block() as block:
            @block.gpsimd
            def _(g):
                some = lambda m, n: lambda r: r[:, 0:m * n].rearrange("p (m n) -> p m n", m=m)
                rows = lambda t, m0, m: t[m0 * P:(m0 + m) * P, :].rearrange("(m p) n -> p m n", p=P)
                fl = lambda w: w.rearrange("p k a n -> p k (a n)")
                chunks = [(rows(a["gu_A"], 0, KD), fl(WA[:, 0]), fl(WA[:, 1]), some(KD, 1024))]
                chunks.append((rows(a["base_d"], 0, MT1), WD[:, 0], WD[:, 1], some(MT1, D)))
                for m0, m in ((0, 4), (4, 3)):
                    chunks.append((rows(a["d_A"], m0, m), WDA[:, 0, m0:m0 + m, :], WDA[:, 1, m0:m0 + m, :], some(m, E1 * R1)))
                chunks.append((rows(a["d_B"], 0, ET1), WDB[:, 0], WDB[:, 1], some(ET1, D)))
                split_weights(p, g, chunks, raw)

            @block.sync
            def _(sp):
                with sp.Fori(0, B) as b:
                    sp.wait_ge(s_x, b * TB + TB + 1)
                    sp.dma_start(a["out"].rearrange("(t p) d -> p t d", p=P)[:, ds(b * TB, TB), :], p.X[:, ds(b * TB, TB), :]).then_inc(s_out, 16)
                sp.wait_ge(s_out, 16 * B)

            @block.scalar
            def _(act):
                def normed(b):
                    act.wait_ge(s_var, b + 1)
                    act.activation(p.ln_rs[:, 0:TB], p.ln_mv[:, :, 1], ACT.Sqrt, bias=p.eps[:, 0:1]).then_inc(s_sd, 1)

                def route(b):
                    act.wait_ge(s_tr, b + 1)
                    hp = bank[6][:, :].rearrange("p (k n) -> p k n", k=KD)
                    act.activation(hf[:, :, :], hp, ACT.Copy).then_inc(s_hf, 1)
                    act.activation(hT[:, 0, :, :], hp, ACT.Copy).then_inc(s_hhi, 1)
                    act.wait_ge(s_lg, b + 1)
                    act.activation(conf[:, :, :], bank[7][:, 0:TB * E1].rearrange("p (t e) -> p t e", t=TB), ACT.Sigmoid).then_inc(s_conf, 1)
                    act.wait_ge(s_diff, b + 1)
                    act.activation(best[:, 2, :], best[:, 2, :], ACT.Exp).then_inc(s_ex, 1)
                    act.wait_ge(s_rtT, b + 1)
                    act.activation(RTf[:, :], bank[6][0:18, 0:S], ACT.Copy).then_inc(s_rtc, 1)
                    act.activation(RTb[:, :], bank[6][0:18, 0:S], ACT.Copy).then_inc(s_rtc, 1)

                def body(b, nxt):
                    for t in range(ET1):
                        act.wait_ge(s_mkp, b * ET1 + t + 1)
                        act.activation(MK[:, t, :, :], bank[2 + t][:, :].rearrange("p (s n) -> p s n", s=2), ACT.Copy).then_inc(s_mk, 1)
                    for i in range(4):
                        act.wait_ge(s_zp, b * 4 + i + 1)
                        act.activation(z[:, 0, i // 2, 2 * (i % 2):2 * (i % 2) + 2, :], bank[2 + i][:, :].rearrange("p (t n) -> p t n", t=2),
                                       ACT.Copy).then_inc(s_zhi, 1)
                    act.wait_ge(s_wp, b + 1)
                    act.activation(wrep[:, :, :], bank[1][:, :].rearrange("p (s n) -> p s n", s=2), ACT.Copy).then_inc(s_wrep, 1)

                    def base_out(m):
                        act.wait_ge(s_bs, b * MT1 + m + 1)
                        if m >= 2:
                            act.wait_ge(s_ul, b * MT1 + m - 1)
                        act.activation(BS[:, m % 2, :, :], bank[6 + m % 2][:, :].rearrange("p (w n) -> p w n", w=2), ACT.Copy).then_inc(s_bev, 1)

                    def high(m):
                        act.wait_ge(s_hw, b * MT1 + m + 1)
                        act.activation(HW[:, 0, m, :], hw[:, m % 2, :, :].rearrange("p s n -> p (s n)"), ACT.Copy).then_inc(s_hwhi, 1)
                        act.wait_ge(s_hs, b * MT1 + m + 1)
                        act.activation(HS[:, 0, m, :], hs[:, m % 2, :], ACT.Copy).then_inc(s_hshi, 1)

                    base_out(0)
                    for m in range(MT1):
                        if m + 1 < MT1:
                            base_out(m + 1)
                        act.wait_ge(s_gl, b * MT1 + m + 1)
                        act.activation(sil[:, m % 2, :], gl[:, m % 2, :], ACT.Silu).then_inc(s_sil, 1)
                        if m >= 1:
                            high(m - 1)
                        if m == MT1 - 2 and nxt is not None:
                            normed(nxt)
                    high(MT1 - 1)
                    if nxt is not None:
                        route(nxt)
                    for t in range(ET1):
                        act.wait_ge(s_ys, b * ET1 + t + 1)
                        act.activation(YS[:, 0, t, :], ys[:, t, :], ACT.Copy).then_inc(s_yhi, 1)

                normed(0)
                route(0)
                rounds(act, body)

            @block.vector
            def _(v):
                def normed(b, ch):
                    xt = lambda t: p.X[:, ds(2 * b + t, 1), :].rearrange("p o n -> p (o n)")
                    layernorm(v, xt, p.ln_stats, p.ln_mv, p.xn, p.ln_rs, s_var, s_sd, ch, s_xn, b)

                def route(b, ch):
                    v.wait_ge(s_hhi, b + 1)
                    v.tensor_tensor(hT[:, 1, :, :], bank[6][:, :].rearrange("p (k n) -> p k n", k=KD), hT[:, 0, :, :], ALU.subtract).then_inc(s_hlo, 1)
                    v.wait_ge(s_conf, b + 1)
                    row = lambda r: r.rearrange("p (o e) -> p o e", o=1).broadcast_to([P, TB, E1])
                    col = lambda r: r.rearrange("p (t o) -> p t o", o=1).broadcast_to([P, TB, E1])
                    ch.link(v.tensor_tensor(conf[:, :, :], conf[:, :, :], row(worth[:, :]), ALU.mult))
                    for s in range(2):
                        mask = RT[:, :, s * E1:(s + 1) * E1]
                        ch.link(v.tensor_reduce(best[:, s, :], conf[:, :, :], AX.X, ALU.max))
                        ch.link(v.tensor_tensor(eq[:, :, :], conf[:, :, :], col(best[:, s, :]), ALU.is_equal))
                        ch.link(v.tensor_tensor(eq[:, :, :], eq[:, :, :], row(order[:, :]), ALU.mult))
                        ch.link(v.tensor_reduce(best[:, 3, :], eq[:, :, :], AX.X, ALU.min))
                        ch.link(v.tensor_tensor(mask, row(order[:, :]), col(best[:, 3, :]), ALU.is_equal))
                        if s == 0:
                            ch.link(v.scalar_tensor_tensor(conf[:, :, :], mask, -1e38, conf[:, :, :], ALU.mult, ALU.add))
                    v.tensor_tensor(best[:, 2, :], best[:, 1, :], best[:, 0, :], ALU.subtract).then_inc(s_diff, 1)
                    v.wait_ge(s_ex, b + 1)
                    ch.link(v.tensor_scalar(best[:, 3, :], best[:, 2, :], 1.0, None, ALU.add))
                    ch.link(v.reciprocal(RT[:, :, 16], best[:, 3, :]))
                    v.tensor_tensor(RT[:, :, 17], RT[:, :, 16], best[:, 2, :], ALU.mult).then_inc(s_rt, 1)

                def body(b, nxt):
                    ch = Chain(v, s_dch, b, LINKS_D, LINKS_D0)
                    xt = lambda t: p.X[:, ds(2 * b + t, 1), :].rearrange("p o n -> p (o n)")
                    v.wait_ge(s_mk, b * ET1 + ET1)
                    for w in range(2):
                        for i in (2 * w, 2 * w + 1):
                            v.wait_ge(s_zhi, b * 4 + i + 1)
                            tt = slice(2 * (i % 2), 2 * (i % 2) + 2)
                            v.tensor_tensor(z[:, 1, w, tt, :], bank[2 + i][:, :].rearrange("p (t n) -> p t n", t=2), z[:, 0, w, tt, :],
                                            ALU.subtract).then_inc(s_zlo, 1)
                        v.wait_ge(s_zlo, b * 4 + 2 * w + 2)
                        for x in range(2):
                            v.tensor_tensor(zm[:, x, w, :, :].rearrange("p t (s n) -> p t s n", s=2),
                                            z[:, x, w, :, :].rearrange("p t (o n) -> p t o n", o=1).broadcast_to([P, ET1, 2, S]),
                                            MK[:, :, :, :], ALU.mult).then_inc(s_zm, 1)
                    v.wait_ge(s_wrep, b + 1)

                    def adds(m):
                        v.wait_ge(s_bev, b * MT1 + m + 1)
                        for w, dst, s_done in ((0, gl, s_gl), (1, ul, s_ul)):
                            v.wait_ge(s_lo, b * 2 * MT1 + 2 * m + w + 1)
                            v.tensor_tensor(dst[:, m % 2, :].rearrange("p (s n) -> p s n", s=2),
                                            bank[2 + 2 * (m % 2) + w][:, :].rearrange("p (s n) -> p s n", s=2),
                                            BS[:, m % 2, w:w + 1, :].broadcast_to([P, 2, S]), ALU.add).then_inc(s_done, 1)

                    def finish(m):
                        v.wait_ge(s_sil, b * MT1 + m + 1)
                        v.wait_ge(s_ul, b * MT1 + m + 1)
                        hm = hw[:, m % 2, :, :]
                        ch.link(v.tensor_tensor(hm.rearrange("p s n -> p (s n)"), sil[:, m % 2, :], ul[:, m % 2, :], ALU.mult))
                        v.tensor_tensor(hm, hm, wrep[:, :, :], ALU.mult).then_inc(s_hw, 1)
                        v.wait_ge(s_hw, b * MT1 + m + 1)
                        v.tensor_tensor(hs[:, m % 2, :], hm[:, 0, :], hm[:, 1, :], ALU.add).then_inc(s_hs, 1)
                        v.wait_ge(s_hwhi, b * MT1 + m + 1)
                        v.tensor_tensor(HW[:, 1, m, :], hm.rearrange("p s n -> p (s n)"), HW[:, 0, m, :], ALU.subtract).then_inc(s_hwlo, 1)
                        v.wait_ge(s_hshi, b * MT1 + m + 1)
                        v.tensor_tensor(HS[:, 1, m, :], hs[:, m % 2, :], HS[:, 0, m, :], ALU.subtract).then_inc(s_hslo, 1)
                        v.wait_ge(s_hslo, b * MT1 + m + 1)

                    for m in range(MT1):
                        adds(m)
                        if m >= 1:
                            finish(m - 1)
                        if m == MT1 - 2 and nxt is not None:
                            normed(nxt, ch)
                    finish(MT1 - 1)
                    if nxt is not None:
                        route(nxt, ch)
                    for t in range(ET1):
                        v.wait_ge(s_yp, b * ET1 + t + 1)
                        ch.link(v.tensor_tensor(yt[:, t, :, :], bank[2 + t][:, :].rearrange("p (s n) -> p s n", s=2), MK[:, t, :, :], ALU.mult))
                        v.tensor_tensor(ys[:, t, :], yt[:, t, 0, :], yt[:, t, 1, :], ALU.add).then_inc(s_ys, 1)
                        v.wait_ge(s_yhi, b * ET1 + t + 1)
                        v.tensor_tensor(YS[:, 1, t, :], ys[:, t, :], YS[:, 0, t, :], ALU.subtract).then_inc(s_ylo, 1)
                    for t in range(TB):
                        v.wait_ge(s_y, b * TB + t + 1)
                        v.tensor_tensor(xt(t), bank[t][:, 0:D], xt(t), ALU.add).then_inc(s_x, 1)
                    if nxt is not None:
                        ch.done()

                v.sem_inc(s_x, 1)
                first = Chain(v, s_dch, 0, LINKS_D0)
                normed(0, first)
                route(0, first)
                first.done()
                rounds(v, body)

            @block.tensor
            def _(pe):
                def turn(b):
                    pe.wait_ge(s_xn, b + 1)
                    for k in range(KD):
                        for t in range(TB):
                            mm = pe.transpose(bank[6][:, k * S + t * P:k * S + (t + 1) * P], p.xn[:, t, k * P:(k + 1) * P], p.identf[:, :])
                    mm.then_inc(s_tr, 1)

                def logits(b):
                    pe.wait_ge(s_hf, b + 1)
                    for t in range(TB):
                        o = bank[7][:, t * E1:(t + 1) * E1]
                        pe.matmul(o, p.ones1[:, :], confb[:, :], start=True, stop=False)
                        for k in range(KD):
                            mm = pe.matmul(o, hf[:, k, t * P:(t + 1) * P], confT[:, k, :], start=False, stop=(k == KD - 1))
                    mm.then_inc(s_lg, 1)

                def turn_routes(b):
                    pe.wait_ge(s_hlo, b + 1)
                    pe.wait_ge(s_rt, b + 1)
                    for t in range(TB):
                        mm = pe.transpose(bank[6][0:18, t * P:(t + 1) * P], RT[:, t, :], p.identf[:, :])
                    mm.then_inc(s_rtT, 1)

                def rank(b):
                    for i in range(4):
                        pe.wait_ge(s_mk, b * ET1 + i + 1)
                        for j in range(2):
                            n = 2 * i + j
                            w, t = n // ET1, n % ET1
                            for q, (x, y, k) in enumerate([(x, y, k) for x, y in TERMS for k in range(KD)]):
                                mm = pe.matmul(bank[2 + i][:, j * S:(j + 1) * S], WA[:, x, k, w, t * P:(t + 1) * P], hT[:, y, k, :],
                                               start=(q == 0), stop=(q == 5))
                        mm.then_inc(s_zp, 1)

                def base(b, m):
                    if m >= 2:
                        pe.wait_ge(s_bev, b * MT1 + m - 1)
                    for w in range(2):
                        for q, (x, y, k) in enumerate([(x, y, k) for x, y in TERMS for k in range(KD)]):
                            mm = pe.matmul(bank[6 + m % 2][:, w * S:(w + 1) * S], WG[:, x, k, w, m * P:(m + 1) * P], hT[:, y, k, :],
                                           start=(q == 0), stop=(q == 5))
                    mm.then_inc(s_bs, 1)

                def experts(b, m):
                    for w in range(2):
                        if m >= 2:
                            pe.wait_ge((s_gl, s_ul)[w], b * MT1 + m - 1)
                        elif m == 0:
                            pe.wait_ge(s_zm, b * 4 + 2 * w + 2)
                        for q, (x, y, t) in enumerate([(x, y, t) for x, y in TERMS for t in range(ET1)]):
                            mm = pe.matmul(bank[2 + 2 * (m % 2) + w][:, :], WB[:, x, w, t, m * P:(m + 1) * P], zm[:, y, w, t, :],
                                           start=(q == 0), stop=(q == 3 * ET1 - 1))
                        mm.then_inc(s_lo, 1)

                def body(b, nxt):
                    pe.wait_ge(s_rtc, b * 2 + 2)
                    for t in range(ET1):
                        for s in range(2):
                            mm = pe.matmul(bank[2 + t][:, s * S:(s + 1) * S], pick[:, t, s, :], RTb[:, :], start=True, stop=True)
                        mm.then_inc(s_mkp, 1)
                    pe.wait_ge(s_hlo, b + 1)
                    pe.wait_ge(p.weight_split, HAVE_A)
                    rank(b)
                    pe.wait_ge(s_x, b * TB + 1)
                    for s in range(2):
                        mm = pe.matmul(bank[1][:, s * S:(s + 1) * S], pickw[:, s, :], RTf[:, :], start=True, stop=True)
                    mm.then_inc(s_wp, 1)
                    base(b, 0)
                    base(b, 1)
                    for m in range(MT1):
                        experts(b, m)
                        if m + 2 < MT1:
                            base(b, m + 2)
                    if nxt is not None:
                        pe.wait_ge(s_bev, b * MT1 + MT1)
                        turn(nxt)
                    pe.wait_ge(p.weight_split, HAVE_D)
                    pe.wait_ge(s_wrep, b + 1)
                    for m in range(MT1):
                        pe.wait_ge(s_hslo, b * MT1 + m + 1)
                        for t in range(TB):
                            for q, (x, y) in enumerate(TERMS):
                                pe.matmul(bank[t][:, 0:D], HS[:, x, m, t * P:(t + 1) * P], WD[:, y, m, :], start=(m == 0 and q == 0), stop=False)
                    if nxt is not None:
                        logits(nxt)
                    pe.wait_ge(p.weight_split, HAVE_DA)
                    for t in range(ET1):
                        for m in range(MT1):
                            for q, (x, y) in enumerate(TERMS):
                                mm = pe.matmul(bank[2 + t][:, :], WDA[:, x, m, t * P:(t + 1) * P], HW[:, y, m, :],
                                               start=(m == 0 and q == 0), stop=(m == MT1 - 1 and q == 2))
                        mm.then_inc(s_yp, 1)
                        if t == 1 and nxt is not None:
                            turn_routes(nxt)
                    pe.wait_ge(p.weight_split, HAVE_DB)
                    for t in range(TB):
                        for e in range(ET1):
                            pe.wait_ge(s_ylo, b * ET1 + e + 1)
                            for q, (x, y) in enumerate(TERMS):
                                mm = pe.matmul(bank[t][:, 0:D], YS[:, x, e, t * P:(t + 1) * P], WDB[:, y, e, :], start=False,
                                               stop=(e == ET1 - 1 and q == 2))
                        mm.then_inc(s_y, 1)

                turn(0)
                logits(0)
                turn_routes(0)
                rounds(pe, body)


def build(nc, args):
    p = Program(nc, args)
    with p.top:
        setup(p)
        with ExitStack() as c:
            raw_weights(p, c)
            first_attention(p)
            first_ffn(p)
        expert_weights(p)
        second_attention(p)
        second_ffn(p)


def kernel(**inputs):
    import numpy as np
    import concourse.bacc as bacc
    from concourse import mybir
    from concourse.bass_utils import run_bass_kernel_spmd

    f = {k: np.ascontiguousarray(v) for k, v in inputs.items()}
    T = lambda v: np.ascontiguousarray(v.T)
    L = {}
    L["x"] = f["x"].reshape(1024, 256)
    L["ctxT"] = T(f["ctx_2048"].reshape(1024, 256))
    L["mask_tok"] = T(f["mask_BxS2_if1"].reshape(8, 128))
    L["mask_row"] = f["mask_BxS2_if1"].reshape(1, 1024)
    wq = f["L0_xattn_w_q"].reshape(2, 4, 2, 2, 8, 256)
    L["wq0T"] = T(wq.transpose(0, 3, 4, 1, 2, 5).reshape(256, 256))
    L["wk0T"] = T(f["L0_xattn_w_k"].reshape(2, 4, 8, 256).transpose(2, 0, 1, 3).reshape(64, 256))
    L["wv0T"] = T(f["L0_xattn_w_v"])
    L["wo0T"] = np.ascontiguousarray(T(f["L0_xattn_w_o"]).reshape(2, 4, 2, 2, 8, 256).transpose(0, 3, 2, 1, 4, 5).reshape(256, 256))
    L["bo0"] = f["L0_xattn_b_o"].reshape(1, 256)
    L["w12T"] = np.concatenate([T(f["L0_ffn_w1"]), T(f["L0_ffn_w2"])], 1)
    L["w3T"] = np.concatenate([T(f["L0_ffn_w3"]), np.zeros((64, 256), np.float32)], 0)
    L["wq1"] = f["L1_xattn_wq"]
    L["wkv1"] = np.concatenate([f["L1_xattn_wk"], f["L1_xattn_wv"], f["L1_xattn_wk_ctx"], f["L1_xattn_wv_ctx"]], 1)
    L["wo1"] = f["L1_xattn_wo"]
    L["qkw"] = np.concatenate([f["L1_xattn_q_norm_w"], f["L1_xattn_k_norm_w"]]).reshape(1, 256)
    inv = (1.0 / np.float32(10000.0) ** (np.arange(0, 128, 2, dtype=np.float32) / np.float32(128))).astype(np.float32)
    ang = np.outer(np.arange(256, dtype=np.float32), inv).astype(np.float32)
    rope = np.stack([np.cos(ang), np.cos(ang), -np.sin(ang), np.sin(ang)], 1).astype(np.float32)
    L["rope"] = np.ascontiguousarray(rope.reshape(2, 128, 4, 64).transpose(1, 0, 2, 3))
    L["confT"] = T(f["L1_ffn_conf_W"])
    L["confb"] = f["L1_ffn_conf_b"].reshape(1, 8)
    L["wealth"] = f["L1_ffn_expert_wealth"].reshape(1, 8)
    L["base_gu"] = np.concatenate([f["L1_ffn_base_gate"], f["L1_ffn_base_up"]], 1)
    A = lambda n: f[n].transpose(1, 0, 2).reshape(f[n].shape[1], 512)
    L["gu_A"] = np.concatenate([A("L1_ffn_gate_A"), A("L1_ffn_up_A")], 1)
    L["gu_B"] = np.concatenate([f["L1_ffn_gate_B"].reshape(512, 896), f["L1_ffn_up_B"].reshape(512, 896)], 0)
    L["d_A"] = A("L1_ffn_down_A")
    L["base_d"] = f["L1_ffn_base_down"]
    L["d_B"] = f["L1_ffn_down_B"].reshape(512, 256)

    nc = bacc.Bacc("TRN2", target_bir_lowering=False, num_devices=1)
    arrays, args = {}, {}
    for name, v in L.items():
        v = np.ascontiguousarray(v)
        arrays[name + "_in"] = v
        args[name] = nc.dram_tensor(name + "_in", v.shape, mybir.dt.from_np(v.dtype), kind="ExternalInput").ap()
    args["out"] = nc.dram_tensor("out", (1024, 256), mybir.dt.float32, kind="ExternalOutput").ap()
    build(nc, args)
    r = run_bass_kernel_spmd(nc, [arrays], core_ids=[0])
    return r.results[0]["out"].reshape(4, 256, 256)
```

```python
import numpy as np
import concourse.bass as bass
from concourse import mybir
from contextlib import ExitStack

F32 = mybir.dt.float32
BF16 = mybir.dt.bfloat16
I32 = mybir.dt.int32
ALU = mybir.AluOpType
ACT = mybir.ActivationFunctionType
AX = mybir.AxisListType
ds = bass.ds

P = 128
B, S, D = 4, 256, 256
NT = B * S // P
TB = S // P
KD = D // P
NEG = -1e30
MAGIC = 12582912.0

G0, HG0, HD0 = 8, 4, 8
HALF = G0 // 2
NPART = 3
Q_TERM = (0, 0, 1, 1, 0, 2)
K_TERM = (0, 1, 0, 1, 2, 0)
ONES2 = float(np.array([0x3F803F80], np.uint32).view(np.float32)[0])
ROW_M, ROW_PAD = 48, 49
HID0 = 704
HT0 = 6

H1, KV1, HD1 = 16, 4, 128
REP1 = H1 // KV1
T1 = 256
CH = 512
E1, R1, HID1 = 8, 64, 896
MT1 = HID1 // P
ET1 = E1 * R1 // P
SCALING = 0.25
ROOM = 57344


class Chain:

    def __init__(self, eng, sem, i, per, start=0):
        self.eng, self.sem, self.i, self.per, self.start, self.k = eng, sem, i, per, start, 0

    def add(self, ins):
        ins.then_inc(self.sem, 1)
        self.k += 1

    def wait(self):
        self.eng.wait_ge(self.sem, self.i * self.per + self.start + self.k)

    def link(self, ins):
        self.add(ins)
        self.wait()

    def pause(self):
        self.wait()
        self.eng.sem_inc(self.sem, 1)
        self.k += 1

    def done(self, n=None):
        assert self.k == (self.per if n is None else n), f"{self.sem}: the body adds {self.k}"


def rounds(eng, body):
    with eng.Fori(0, B - 1) as b:
        body(b, b + 1)
    body(B - 1, None)


class Program:
    def __init__(self, nc, args):
        self.nc, self.a = nc, args
        self.top = ExitStack()

    def sb(self, name, shape, dt=F32, ctx=None):
        return (ctx or self.top).enter_context(self.nc.sbuf_tensor(name, shape, dt))

    def carve(self, shape, dt=BF16):
        n = int(np.prod(shape)) // (2 if dt == BF16 else 1)
        v = self.room[:, self.used:self.used + n]
        self.used += n
        assert self.used * 4 <= ROOM
        if dt == BF16:
            v = v.bitcast(BF16)
        names = "abcd"[:len(shape)]
        return v.rearrange(f"p ({' '.join(names)}) -> p {' '.join(names)}", **dict(zip(names, shape)))

    def ps(self, name, shape, ctx, dt=F32):
        return ctx.enter_context(self.nc.psum_tensor(name, shape, dt))

    def sems(self, ctx, names):
        return [ctx.enter_context(self.nc.semaphore(n)) for n in names.split()]


def norm_stats(p, v, chain, ln_var, ln_sd):
    for t in range(NT):
        chain.add(v.bn_stats(p.ln_stats[:, t, :], p.X[:, t, :]))
    chain.pause()
    for t in range(NT):
        last = v.bn_aggr(p.ln_mv[:, t, :], p.ln_stats[:, t, :])
        if t == NT - 1:
            last.then_inc(ln_var, 1)
        else:
            chain.add(last)
    v.wait_ge(ln_sd, 1)
    chain.link(v.reciprocal(p.ln_rs[:, 1, :], p.ln_rs[:, 0, :]))


def norm_roots(p, act, ln_var, ln_sd):
    act.wait_ge(ln_var, 1)
    act.activation(p.ln_rs[:, 0, :], p.ln_mv[:, :, 1], ACT.Sqrt, bias=p.eps[:, 0:1]).then_inc(ln_sd, 1)


def normalise(p, v, b, chain, ready):
    for t in range(TB):
        tile = ds(TB * b + t, 1)
        flat = lambda r: r.rearrange("p o n -> p (o n)")
        ins = v.tensor_scalar(p.xn[:, t, :], flat(p.X[:, tile, :]), flat(p.ln_mv[:, tile, 0:1]), p.ln_rs[:, 1, tile], ALU.subtract, ALU.mult)
        if t == TB - 1:
            ins.then_inc(ready, 1)
        else:
            chain.add(ins)


def split_weights(p, g, chunks, raw):
    def load(n):
        src, hi, lo, view = chunks[n - first]
        g.dma_start(view(raw[:, n % 2, :]), src).then_inc(p.weight_in[n % 2], 16)
        g.dma_start(hi, src).then_inc(p.weight_in[n % 2], 16)

    first, last = p.split, p.split + len(chunks)
    load(first)
    for n in range(first, last):
        src, hi, lo, view = chunks[n - first]
        if n + 1 < last:
            if n >= 1:
                g.wait_ge(p.weight_split, n)
            load(n + 1)
        g.wait_ge(p.weight_in[n % 2], 32 * (n // 2 + 1))
        g.tensor_tensor(lo, view(raw[:, n % 2, :]), hi, ALU.subtract).then_inc(p.weight_split, 1)
    g.wait_ge(p.weight_split, last)
    p.split = last


def setup(p):
    nc, a = p.nc, p.a
    p.X = p.sb("X", [P, NT, D])
    p.identf = p.sb("identf", [P, P])
    p.identb = p.sb("identb", [P, P], BF16)
    p.eps = p.sb("eps", [P, 3])
    p.ones1 = p.sb("ones1", [1, P])
    p.ln_stats = p.sb("ln_stats", [P, NT, 6])
    p.ln_mv = p.sb("ln_mv", [P, NT, 2])
    p.ln_rs = p.sb("ln_rs", [P, 2, NT])
    p.xn = p.sb("xn", [P, TB, D])
    p.weight_in = p.sems(p.top, "weight_in0 weight_in1")
    (p.weight_split,) = p.sems(p.top, "weight_split")
    p.split = 0
    p.room = p.sb("room", [P, ROOM // 4])
    p.used = 0
    p.CTS = p.carve([2, KD, B * S])
    p.WQ = p.carve([2, KD, H1 * HD1])
    p.WKV = p.carve([2, KD, 2, 2 * KV1 * HD1])
    p.WO = p.carve([2, H1, D])


def raw_weights(p, c):
    w12, w3 = KD * 2 * HID0, HT0 * D
    p.raw = p.sb("raw", [P, w12 + w3], F32, c)
    p.w12 = p.raw[:, 0:w12].rearrange("p (k n) -> p k n", k=KD)
    p.w3 = p.raw[:, w12:w12 + w3].rearrange("p (k n) -> p k n", k=HT0)
    p.W12 = p.sb("W12", [P, KD, 2 * HID0], BF16, c)
    p.W3 = p.sb("W3", [P, HT0, D], BF16, c)
    p.mean = p.sb("mean", [P, 3], F32, c)
    p.inv = p.sb("inv", [P, 3], F32, c)
    p.asum = p.sb("asum", [P, 3], F32, c)
    p.ones = p.sb("ones", [P, P], F32, c)


def ternary(p, v, raw, out, m, chain):
    chain.link(v.tensor_scalar(raw, raw, p.inv[:, m:m + 1], 1.0, ALU.mult, ALU.min))
    chain.link(v.tensor_scalar(raw, raw, -1.0, MAGIC, ALU.max, ALU.add))
    chain.link(v.tensor_scalar(out, raw, MAGIC, None, ALU.subtract))


def first_attention(p):
    nc, a = p.nc, p.a
    with ExitStack() as c:
        sb = lambda n, s, dt=F32: p.sb(n, s, dt, c)
        wq = sb("wq0", [P, KD, D])
        wo = sb("wo0", [P, KD, D])
        bo = sb("bo0", [1, D])
        Vaug = sb("Vaug", [P, NT, G0, 32])
        Qst = sb("Qst", [P, 2, 8, B, S], BF16)
        Kst = sb("Kst", [P, 2, 2, HALF, B, S], BF16)
        triA = sb("triA", [P, 2, S], BF16)
        triB = sb("triB", [P, 2, S], BF16)
        k_scr = nc.dram_tensor("k_scr", [NPART, G0 * HD0, B * S], BF16).ap()
        q_scr = nc.dram_tensor("q_scr", [NPART, 2, P, B * S], BF16).ap()
        bank = [p.ps(f"a{i}", [P, 512], c) for i in range(8)]

        with ExitStack() as c1:
            CT = p.raw[:, 0:KD * B * S].rearrange("p (k n) -> p k n", k=KD)
            wk = p.sb("wk0", [P, KD, G0 * HD0], F32, c1)
            wv = p.sb("wv0", [P, KD, G0 * HD0], F32, c1)
            mask_i = p.sb("mask_i", [P, NT], I32, c1)
            mask_r = p.sb("mask_r", [1, B * S], I32, c1)
            valid = p.sb("valid", [P, NT], F32, c1)
            pad_row = p.sb("pad_row", [1, B * S], BF16, c1)
            one_row = p.sb("one_row", [1, B * S], BF16, c1)
            kp = p.sb("kp", [G0 * HD0, NPART, B * S], BF16, c1)
            kr = p.sb("kr", [G0 * HD0, 2, 512], F32, c1)
            stats, mv, rstd = p.ln_stats, p.ln_mv, p.ln_rs
            xT = p.sb("xT", [P, KD, S], F32, c1)
            qp = p.sb("qp", [P, NPART, 2, B, S], BF16, c1)
            qr = p.sb("qr", [P, 2, S], F32, c1)
            (s_x, s_wq, s_wo, s_ct, s_wk, s_m, s_eng, s_v, s_k, s_khi, s_kr, s_kout, s_kin, s_rows, s_zero,
             s_valid, s_va, s_dch, s_cts, s_var, s_sd, s_rstd, s_xn, s_tr, s_xT, s_q, s_qhi, s_qr, s_qp, s_qout, s_qinA, s_qinB, s_qinC) = \
                p.sems(c1, "x0 wq0 wo0 ct0 wk0 m0 eng0 v0 k0 khi0 kr0 kout0 kin0 rows0 zero0 valid0 va0 dch0 cts0 "
                           "var0 sd0 rstd0 xn0 tr0 xT0 q0 qhi0 qr0 qp0 qout0 qinA0 qinB0 qinC0")

            def stack_q(eng, e, terms, sem):
                for t in terms:
                    r = 64 * e + 8 * t
                    eng.dma_start(Qst[r:r + 8, :, :, :, :].rearrange("p h j b n -> p h (j b n)"),
                                  q_scr[Q_TERM[t], :, 64 * e:64 * e + 64, :].rearrange("h (d j) m -> d h (j m)", j=8)).then_inc(sem, 16)

            with nc.Block() as block:
                @block.sync
                def _(sp):
                    sp.dma_start(CT[:, :, :], a["ctxT"].rearrange("(k p) n -> p k n", p=P)).then_inc(s_ct, 16)
                    sp.dma_start(wk[:, :, :], a["wk0T"].rearrange("(k p) n -> p k n", p=P)).then_inc(s_wk, 16)
                    sp.dma_start(wv[:, :, :], a["wv0T"].rearrange("(k p) n -> p k n", p=P)).then_inc(s_wk, 16)
                    sp.dma_start(mask_i[:, :], a["mask_tok"]).then_inc(s_m, 16)
                    sp.dma_start(mask_r[:, :], a["mask_row"]).then_inc(s_m, 16)
                    sp.wait_ge(s_kr, 6)
                    sp.dma_start(k_scr.rearrange("a p m -> p a m"), kp[:, :, :]).then_inc(s_kout, 16)
                    sp.wait_ge(s_kout, 16)
                    sp.wait_ge(s_zero, 2)
                    for e in range(2):
                        for t in range(6):
                            sp.dma_start(Kst[64 * e + 8 * t:64 * e + 8 * t + 8, e, :, :, :, :].rearrange("p h j b n -> p (h j b n)"),
                                         k_scr[K_TERM[t], :, :].rearrange("(d g) m -> d (g m)", d=HD0)).then_inc(s_kin, 16)
                    with sp.Fori(0, B) as b:
                        sp.wait_ge(s_qp, b * 2 + 2)
                        sp.dma_start(q_scr[:, :, :, ds(b * S, S)].rearrange("a h p t -> p (a h) t"),
                                     qp[:, :, :, ds(b, 1), :].rearrange("p a h o t -> p (a h) (o t)")).then_inc(s_qout, 16)
                    sp.wait_ge(s_qout, B * 16)
                    stack_q(sp, 0, range(6), s_qinA)
                    sp.wait_ge(s_kin, 16 * 12)
                    sp.wait_ge(s_qinA, 16 * 6)

                @block.scalar
                def _(act):
                    act.dma_start(p.X[:, :, :], a["x"].rearrange("(t p) d -> p t d", p=P)).then_inc(s_x, 16)
                    act.dma_start(wq[:, :, :], a["wq0T"].rearrange("(k p) n -> p k n", p=P)).then_inc(s_wq, 16)
                    act.dma_start(wo[:, :, :], a["wo0T"].rearrange("(k p) n -> p k n", p=P)).then_inc(s_wo, 16)
                    act.dma_start(bo[:, :], a["bo0"]).then_inc(s_wo, 16)
                    act.wait_ge(s_eng, 1)
                    act.wait_ge(s_var, 1)
                    act.activation(rstd[:, 0, :], mv[:, :, 1], ACT.Sqrt, bias=p.eps[:, 0:1]).then_inc(s_sd, 1)
                    for n in range(2):
                        act.wait_ge(s_k, n + 1)
                        act.activation(kp[:, 0, n * 512:(n + 1) * 512], bank[2 + n][0:64, :], ACT.Copy).then_inc(s_khi, 1)

                    def turned(b):
                        act.wait_ge(s_tr, b + 1)
                        act.activation(xT[:, :, :], bank[4][:, :].rearrange("p (k n) -> p k n", k=KD), ACT.Copy).then_inc(s_xT, 1)

                    def body(b, nxt):
                        act.wait_ge(s_q, b + 1)
                        act.activation(qp[:, 0, :, ds(b, 1), :].rearrange("p h o n -> p h (o n)"), bank[5][:, :].rearrange("p (h n) -> p h n", h=2),
                                       ACT.Copy, scale=HD0 ** -0.5).then_inc(s_qhi, 1)
                        if nxt is not None:
                            turned(nxt)

                    turned(0)
                    rounds(act, body)
                    act.wait_ge(s_qout, B * 16)
                    stack_q(act, 1, range(3, 6), s_qinC)
                    act.wait_ge(s_qinC, 16 * 3)
                    act.wait_ge(s_wo, 32)

                @block.gpsimd
                def _(g):
                    g.memset(p.eps[:, 0:1], 1e-5).then_inc(s_eng, 1)
                    g.memset(p.eps[:, 1:2], HD1 * 1e-6).then_inc(s_eng, 1)
                    g.memset(p.eps[:, 2:3], 1e-6).then_inc(s_eng, 1)
                    g.memset(p.ones1[:, :], 1.0).then_inc(s_eng, 1)
                    g.memset(p.identf[:, :], 0.0).then_inc(s_eng, 1)
                    g.memset(p.identb[:, :], 0.0).then_inc(s_eng, 1)
                    g.memset(triA[:, :, :], 0.0).then_inc(s_eng, 1)
                    g.memset(triB[:, :, :], 0.0).then_inc(s_eng, 1)
                    g.wait_ge(s_eng, 8)
                    for m in (p.identf, p.identb):
                        g.affine_select(out=m[:, :], in_=m[:, :], compare_op=ALU.not_equal, fill=1.0, base=0,
                                        pattern=[[-1, P]], channel_multiplier=1).then_inc(s_eng, 1)
                    g.affine_select(out=triA[:, :, P:S], in_=triA[:, :, P:S], compare_op=ALU.is_ge, fill=NEG, base=0,
                                    pattern=[[0, 2], [-1, P]], channel_multiplier=1).then_inc(s_eng, 1)
                    g.affine_select(out=triB[:, :, 0:P], in_=triB[:, :, 0:P], compare_op=ALU.is_ge, fill=NEG, base=0,
                                    pattern=[[0, 2], [1, P]], channel_multiplier=-1).then_inc(s_eng, 1)
                    g.memset(Kst[:, :, :, :, :, :].rearrange("p e h j b n -> p (e h j b n)").bitcast(F32), 0.0).then_inc(s_zero, 1)
                    g.wait_ge(s_zero, 2)
                    g.wait_ge(s_valid, 2)
                    for e in range(2):
                        for r, row in ((ROW_M, one_row), (ROW_PAD, pad_row)):
                            g.dma_start(Kst[64 * e + r:64 * e + r + 1, e, :, :, :, :].rearrange("p h j b n -> p (h j) (b n)"),
                                        row[:, :].rearrange("p (o m) -> p o m", o=1).broadcast_to([1, 8, B * S])).then_inc(s_rows, 16)
                    g.wait_ge(s_rows, 16 * 4)
                    g.wait_ge(s_qout, B * 16)
                    stack_q(g, 1, range(3), s_qinB)
                    g.wait_ge(s_qinB, 16 * 3)

                @block.vector
                def _(v):
                    v.memset(one_row[:, :], 1.0).then_inc(s_valid, 1)
                    v.memset(Qst[:, :, :, :, :].rearrange("p h j b n -> p (h j b n)").bitcast(F32), ONES2).then_inc(s_zero, 1)
                    v.wait_ge(s_x, 16)
                    for t in range(NT):
                        v.bn_stats(stats[:, t, :], p.X[:, t, :]).then_inc(s_dch, 1)
                    v.wait_ge(s_dch, NT)
                    for t in range(NT):
                        v.bn_aggr(mv[:, t, :], stats[:, t, :]).then_inc(s_var if t == NT - 1 else s_dch, 1)
                    v.memset(Vaug[:, :, :, :], 0.0).then_inc(s_dch, 1)
                    v.wait_ge(s_m, 32)
                    v.tensor_scalar(pad_row[:, :], mask_r[:, :], 0.0, NEG, ALU.is_equal, ALU.mult).then_inc(s_valid, 1)
                    v.tensor_scalar(valid[:, :], mask_i[:, :], 0.0, None, ALU.not_equal).then_inc(s_dch, 1)
                    v.wait_ge(s_sd, 1)
                    v.reciprocal(rstd[:, 1, :], rstd[:, 0, :]).then_inc(s_rstd, 1)
                    v.wait_ge(s_rstd, 1)

                    def normed(b):
                        for t in range(TB):
                            one = lambda r: r[:, ds(2 * b + t, 1), :].rearrange("p o n -> p (o n)")
                            v.tensor_scalar(p.xn[:, t, :], one(p.X), mv[:, ds(2 * b + t, 1), 0:1].rearrange("p a o -> p (a o)"),
                                            rstd[:, 1, ds(2 * b + t, 1)], ALU.subtract, ALU.mult).then_inc(s_xn, 1)

                    normed(0)
                    for n in range(2):
                        cols = slice(n * 512, (n + 1) * 512)
                        v.wait_ge(s_khi, n + 1)
                        v.tensor_tensor(kr[:, n, :], bank[2 + n][0:64, :], kp[:, 0, cols], ALU.subtract).then_inc(s_kr, 1)
                        v.wait_ge(s_kr, 3 * n + 1)
                        v.tensor_copy(kp[:, 1, cols], kr[:, n, :]).then_inc(s_kr, 1)
                        v.wait_ge(s_kr, 3 * n + 2)
                        v.tensor_tensor(kp[:, 2, cols], kr[:, n, :], kp[:, 1, cols], ALU.subtract).then_inc(s_kr, 1)

                    def body(b, nxt):
                        if nxt is not None:
                            v.wait_ge(s_tr, b + 1)
                            normed(nxt)
                        v.wait_ge(s_qhi, b + 1)
                        psq = bank[5][:, :].rearrange("p (h n) -> p h n", h=2)
                        part = lambda i: qp[:, i, :, ds(b, 1), :].rearrange("p h o n -> p h (o n)")
                        v.scalar_tensor_tensor(qr[:, :, :], psq, HD0 ** -0.5, part(0), ALU.mult, ALU.subtract).then_inc(s_qr, 1)
                        v.wait_ge(s_qr, b + 2)
                        v.tensor_copy(part(1), qr[:, :, :]).then_inc(s_qp, 1)
                        v.wait_ge(s_qp, b * 2 + 1)
                        v.tensor_tensor(part(2), qr[:, :, :], part(1), ALU.subtract).then_inc(s_qp, 1)
                        v.wait_ge(s_qp, b * 2 + 2)

                    v.sem_inc(s_qr, 1)
                    rounds(v, body)
                    v.wait_ge(s_dch, 2 * NT + 1)
                    v.wait_ge(s_v, 1)
                    v.tensor_tensor(Vaug[:, :, :, 0:8], bank[0][:, :].rearrange("p (t g d) -> p t g d", t=NT, g=G0),
                                    valid[:, :].rearrange("p (t a b) -> p t a b", a=1, b=1).broadcast_to([P, NT, G0, 8]),
                                    ALU.mult).then_inc(s_va, 1)
                    v.tensor_copy(Vaug[:, :, :, 8:9], valid[:, :].rearrange("p (t a b) -> p t a b", a=1, b=1).broadcast_to([P, NT, G0, 1])).then_inc(s_va, 1)
                    v.tensor_copy(p.CTS[:, 0, :, :], CT[:, :, :]).then_inc(s_cts, 1)
                    v.wait_ge(s_cts, 1)
                    v.tensor_tensor(p.CTS[:, 1, :, :], CT[:, :, :], p.CTS[:, 0, :, :], ALU.subtract).then_inc(s_cts, 1)

                @block.tensor
                def _(pe):
                    pe.wait_ge(s_ct, 16)
                    pe.wait_ge(s_wk, 32)
                    for n in range(2):
                        for k in range(KD):
                            mm = pe.matmul(bank[2 + n][0:64, :], wk[:, k, :], CT[:, k, n * 512:(n + 1) * 512],
                                           start=(k == 0), stop=(k == KD - 1))
                        mm.then_inc(s_k, 1)
                    pe.wait_ge(s_eng, 10)
                    pe.wait_ge(s_wq, 16)

                    def turn(b):
                        pe.wait_ge(s_xn, b * TB + TB)
                        for k in range(KD):
                            for t in range(TB):
                                mm = pe.transpose(bank[4][:, k * S + t * P:k * S + (t + 1) * P], p.xn[:, t, k * P:(k + 1) * P], p.identf[:, :])
                        mm.then_inc(s_tr, 1)

                    def body(b, nxt):
                        pe.wait_ge(s_xT, b + 1)
                        pe.wait_ge(s_qr, b + 1)
                        for h in range(2):
                            for k in range(KD):
                                mm = pe.matmul(bank[5][:, h * S:(h + 1) * S], wq[:, k, h * P:(h + 1) * P], xT[:, k, :],
                                               start=(k == 0), stop=(k == KD - 1))
                        mm.then_inc(s_q, 1)
                        if nxt is not None:
                            turn(nxt)

                    turn(0)
                    rounds(pe, body)
                    for t in range(NT):
                        for k in range(KD):
                            mm = pe.matmul(bank[0][:, t * 64:(t + 1) * 64], CT[:, k, t * P:(t + 1) * P], wv[:, k, :],
                                           start=(k == 0), stop=(k == KD - 1))
                    mm.then_inc(s_v, 1)

        with ExitStack() as c2:
            NM = p.sb("NM", [P, 2, 2, 2, HALF, 2], F32, c2)
            nmT = p.sb("nmT", [64, P], BF16, c2)
            PT = p.sb("PT", [P, HALF, 1536], F32, c2)
            VS = p.sb("VS", [P, 2, 2, HALF, 32], F32, c2)
            OT = p.sb("OT", [P, 2, 1024], F32, c2)
            rinv = p.sb("rinv", [P, 2, 16], F32, c2)
            AO, AOT = p.xn, wq
            (s_a, s_fa, s_held, s_nt, s_nmT, s_ndma, s_s, s_e, s_pv, s_vs, s_ot, s_t, s_dch, s_ao, s_aot, s_aoT, s_y, s_xr, s_w, s_tern, s_sum, s_tot) = \
                p.sems(c2, "a2 fa2 held2 nt2 nmT2 ndma2 s3 e3 pv3 vs3 ot3 t3 dch3 ao3 aot3 aoT3 y3 xr3 w3 tern3 sum3 tot3")
            NG = 2 * HALF
            with nc.Block() as block:
                @block.gpsimd
                def _(g):
                    chunks = []
                    for k in range(KD):
                        rows = slice(k * P, (k + 1) * P)
                        chunks.append((a["wq1"][rows, :], p.WQ[:, 0, k, :], p.WQ[:, 1, k, :], lambda r: r))
                        chunks.append((a["wkv1"][rows, :], p.WKV[:, 0, k, :, :].rearrange("p w n -> p (w n)"),
                                       p.WKV[:, 1, k, :, :].rearrange("p w n -> p (w n)"), lambda r: r))
                    for m in range(0, H1, 8):
                        chunks.append((a["wo1"][m * P:(m + 8) * P, :].rearrange("(m p) n -> p m n", p=P),
                                       p.WO[:, 0, m:m + 8, :], p.WO[:, 1, m:m + 8, :], lambda r: r.rearrange("p (m n) -> p m n", m=8)))
                    split_weights(p, g, chunks, p.raw[:, 0:4096].rearrange("p (s n) -> p s n", s=2))
                    g.dma_start(p.w12, a["w12T"].rearrange("(k p) n -> p k n", p=P)).then_inc(s_w, 16)
                    g.dma_start(p.w3, a["w3T"].rearrange("(k p) n -> p k n", p=P)).then_inc(s_w, 16)
                    g.wait_ge(s_w, 32)

                @block.sync
                def _(sp):
                    with sp.Fori(0, B) as b:
                        sp.wait_ge(s_nmT, b + 1)
                        for e in range(2):
                            for qb in range(2):
                                r = 64 * e + ROW_M
                                sp.dma_start(Qst[r:r + 1, :, :, ds(b, 1), qb * P:(qb + 1) * P].rearrange("p h j o n -> p (h j o) n"),
                                             nmT[(2 * e + qb) * 16:(2 * e + qb) * 16 + 16, :]).then_inc(s_ndma, 16)
                    sp.wait_ge(s_ndma, B * 64)

                @block.scalar
                def _(act):
                    def maxima_out(b, first=False):
                        act.wait_ge(s_nt, b + 1)
                        if not first:
                            act.wait_ge(s_ndma, b * 64)
                        act.activation(nmT[:, :], bank[3][0:64, 0:P], ACT.Copy).then_inc(s_nmT, 1)

                    def body(b, nxt):
                        for n in range(NG):
                            h, j = n // HALF, n % HALF
                            act.wait_ge(s_pv, b * 2 + h + 1)
                            for i in range(3):
                                act.wait_ge(s_s, b * 3 * NG + 3 * n + i + 1)
                                act.activation(PT[:, j, i * 512:(i + 1) * 512], bank[i][:, :], ACT.Exp).then_inc(s_e, 1)
                            if j == HALF - 1:
                                act.wait_ge(s_pv, b * 2 + h + 2)
                                act.activation(OT[:, h, 0:512], bank[6][:, :], ACT.Copy)
                                act.activation(OT[:, h, 512:1024], bank[7][:, :], ACT.Copy).then_inc(s_ot, 1)
                        if nxt is not None:
                            maxima_out(nxt)
                        act.wait_ge(s_aoT, b + 1)
                        act.activation(AOT[:, :, :], bank[6][:, :].rearrange("p (k n) -> p k n", k=KD), ACT.Copy).then_inc(s_aot, 1)

                    maxima_out(0, first=True)
                    rounds(act, body)

                @block.vector
                def _(v):
                    def maxima(b, n):
                        h, j = n // HALF, n % HALF
                        for i in range(3):
                            v.wait_ge(s_a, b * 3 * NG + 3 * n + i + 1)
                            if i == 0:
                                v.tensor_reduce(NM[:, :, 0, h, j, :].rearrange("p e q -> p q e"),
                                                bank[3][:, :].rearrange("p (q e n) -> p q e n", q=2, e=2), AX.X, ALU.max, negate=True).then_inc(s_fa, 1)
                            else:
                                v.tensor_reduce(NM[:, :, 1, h, j, i - 1], bank[3 + i][:, :].rearrange("p (e n) -> p e n", e=2),
                                                AX.X, ALU.max, negate=True).then_inc(s_fa, 1)

                    def attended(b, h, ch):
                        v.wait_ge(s_t, b * 2 + h + 1)
                        for qb in range(TB):
                            T = bank[6 + qb][:, :].rearrange("p (m d) -> p m d", d=32)
                            ch.link(v.reciprocal(rinv[:, qb, :], T[:, :, 8]))
                            v.tensor_tensor(AO[:, qb, h * P:(h + 1) * P].rearrange("p (m d) -> p m d", d=8), T[:, :, 0:8],
                                            rinv[:, qb, :].rearrange("p (m o) -> p m o", o=1).broadcast_to([P, 16, 8]), ALU.mult).then_inc(s_ao, 1)

                    def body(b, nxt):
                        ch = Chain(v, s_dch, b, 4)
                        v.tensor_copy(VS[:, :, :, :, :].rearrange("p h k j d -> p k h (j d)"),
                                      Vaug[:, ds(2 * b, 2), :, :].rearrange("p k (h j) d -> p k h (j d)", h=2)).then_inc(s_vs, 1)
                        if nxt is None:
                            ternary_gate_up()
                        for n in range(NG):
                            if nxt is not None:
                                maxima(nxt, n)
                            if n % HALF == HALF - 1:
                                attended(b, n // HALF, ch)
                                if n < HALF and nxt is None:
                                    ternary(p, v, p.w3, p.W3[:, :, :], 2, tern)
                        v.wait_ge(s_y, b + 1)
                        x = p.X[:, ds(2 * b, TB), :]
                        v.tensor_tensor(x, bank[7][:, :].rearrange("p (t d) -> p t d", t=TB), x, ALU.add).then_inc(s_xr, 1)
                        ch.done()

                    tern = Chain(v, s_tern, 0, 0)

                    def ternary_gate_up():
                        v.wait_ge(s_w, 32)
                        for m in range(2):
                            tern.add(v.tensor_reduce(p.asum[:, m:m + 1], p.w12[:, :, m * HID0:(m + 1) * HID0], AX.XY, ALU.add, apply_absolute_value=True))
                        tern.add(v.tensor_reduce(p.asum[:, 2:3], p.w3, AX.XY, ALU.add, apply_absolute_value=True))
                        tern.wait()
                        v.memset(p.ones[:, :], 1.0).then_inc(s_sum, 1)
                        v.wait_ge(s_tot, 1)
                        tern.link(v.tensor_scalar(p.mean[:, :], bank[3][:, 0:3], 1.0 / (D * HID0), 1e-5, ALU.mult, ALU.max))
                        tern.link(v.reciprocal(p.inv[:, :], p.mean[:, :]))
                        for m in range(2):
                            cols = slice(m * HID0, (m + 1) * HID0)
                            ternary(p, v, p.w12[:, :, cols], p.W12[:, :, cols], m, tern)

                    for n in range(NG):
                        maxima(0, n)
                    v.sem_inc(s_xr, 1)
                    rounds(v, body)

                @block.tensor
                def _(pe):
                    def maxima(b, n):
                        h, j = n // HALF, n % HALF
                        if n >= 1:
                            pe.wait_ge(s_fa, b * 3 * NG + 3 * n - 2)
                        elif not isinstance(b, int):
                            pe.wait_ge(s_nmT, b)
                        pe.matmul(bank[3][:, :], p.identb[:, :], triA[:, 0:1, P:S].broadcast_to([P, 4, P]), start=True, stop=False)
                        for pp in range(2):
                            q = Qst[:, h, 2 * j + pp, ds(b, 1), 0:P].rearrange("p o n -> p (o n)")
                            mm = pe.matmul(bank[3][:, pp * S:(pp + 1) * S], q, Kst[:, :, h, j, ds(b, 1), 0:P].rearrange("p e o n -> p (e o) n"),
                                           start=False, stop=(pp == 1))
                        mm.then_inc(s_a, 1)
                        for pp in range(2):
                            if n >= 1:
                                pe.wait_ge(s_fa, b * 3 * NG + 3 * n - 1 + pp)
                            elif not isinstance(b, int):
                                pe.wait_ge(s_fa, b * 3 * NG)
                            o = bank[4 + pp]
                            q = Qst[:, h, 2 * j + pp, ds(b, 1), P:S].rearrange("p o n -> p (o n)")
                            pe.matmul(o[:, :], q, Kst[:, :, h, j, ds(b, 1), :].rearrange("p e o n -> p (e o) n"), start=True, stop=False)
                            pe.matmul(o[:, :].rearrange("p (e n) -> p e n", e=2)[:, :, P:S], p.identb[:, :], triA[:, :, P:S],
                                      start=False, stop=True).then_inc(s_a, 1)

                    def turn_maxima(b):
                        pe.wait_ge(s_fa, b * 3 * NG + 3 * NG)
                        pe.sem_inc(s_held, 1)
                        pe.transpose(bank[3][0:64, 0:P], NM[:, :, :, :, :, :].rearrange("p e q h j r -> p (e q h j r)"), p.identf[:, :]).then_inc(s_nt, 1)

                    def scores(b, n):
                        h, j = n // HALF, n % HALF
                        qs = Qst[:, h, 2 * j:2 * j + 2, ds(b, 1), :].rearrange("p j o n -> p (j o) n")
                        for e in range(2):
                            if n >= 1:
                                pe.wait_ge(s_e, b * 3 * NG + 3 * n - 2 + e)
                            pe.matmul(bank[e][:, :], Kst[:, e, h, j, ds(b, 1), 0:P].rearrange("p o n -> p (o n)"), qs, start=True, stop=False)
                            pe.matmul(bank[e][:, :].rearrange("p (j n) -> p j n", j=2)[:, :, 0:P], p.identb[:, :], triB[:, :, 0:P],
                                      start=False, stop=True).then_inc(s_s, 1)
                        if n >= 1:
                            pe.wait_ge(s_e, b * 3 * NG + 3 * n)
                        pe.matmul(bank[2][:, :], p.identb[:, :], triB[:, 0:1, 0:P].broadcast_to([P, 4, P]), start=True, stop=False)
                        for e in range(2):
                            mm = pe.matmul(bank[2][:, e * S:(e + 1) * S], Kst[:, e, h, j, ds(b, 1), P:S].rearrange("p o n -> p (o n)"),
                                           qs[:, :, P:S], start=False, stop=(e == 1))
                        mm.then_inc(s_s, 1)

                    def products(b, h):
                        pe.wait_ge(s_e, b * 3 * NG + (h + 1) * 3 * HALF)
                        pe.wait_ge(s_vs, b + 1)
                        if h == 1:
                            pe.wait_ge(s_ao, b * 4 + 2)
                        else:
                            pe.wait_ge(s_xr, b + 1)
                        for e in range(2):
                            for j in range(HALF):
                                pe.matmul(bank[6 + e][32 * j:32 * j + 32, :], VS[:, h, 0, j, :], PT[:, j, e * 512:(e + 1) * 512],
                                          start=True, stop=False)
                            for j in range(HALF):
                                mm = pe.matmul(bank[6 + e][32 * j:32 * j + 32, :].rearrange("p (r q) -> p r q", r=2)[:, :, P:S], VS[:, h, 1, j, :],
                                               PT[:, j, 1024 + e * S:1024 + (e + 1) * S], start=False, stop=True)
                        mm.then_inc(s_pv, 1)

                    def turn(b, h):
                        pe.wait_ge(s_ot, b * 2 + h + 1)
                        for qb in range(TB):
                            for m in range(4):
                                mm = pe.transpose(bank[6 + qb][:, m * P:(m + 1) * P], OT[:, h, m * S + qb * P:m * S + (qb + 1) * P], p.identf[:, :])
                        mm.then_inc(s_t, 1)

                    def output(b):
                        pe.wait_ge(s_ao, b * 4 + 4)
                        for k in range(KD):
                            for t in range(TB):
                                mm = pe.transpose(bank[6][:, k * S + t * P:k * S + (t + 1) * P], AO[:, t, k * P:(k + 1) * P], p.identf[:, :])
                        mm.then_inc(s_aoT, 1)
                        pe.wait_ge(s_aot, b + 1)
                        for t in range(TB):
                            o = bank[7][:, t * D:(t + 1) * D]
                            pe.matmul(o, p.ones1[:, :], bo[:, :], start=True, stop=False)
                            for k in range(KD):
                                mm = pe.matmul(o, AOT[:, k, t * P:(t + 1) * P], wo[:, k, :], start=False, stop=(k == KD - 1))
                        mm.then_inc(s_y, 1)

                    def body(b, nxt):
                        fill = iter(range(NG))

                        def between():
                            if nxt is not None:
                                maxima(nxt, next(fill))

                        between()
                        pe.wait_ge(s_ndma, b * 64 + 64)
                        for h in range(2):
                            for j in range(HALF):
                                if h == 0 and j == HALF - 1 and nxt is None:
                                    pe.wait_ge(s_sum, 1)
                                    pe.matmul(bank[3][:, 0:3], p.ones[:, :], p.asum[:, :], start=True, stop=True).then_inc(s_tot, 1)
                                if (h, j) != (1, 0):
                                    scores(b, h * HALF + j)
                                if j >= 1:
                                    between()
                            products(b, h)
                            if h == 0:
                                scores(b, HALF)
                            else:
                                between()
                            turn(b, h)
                        if nxt is not None:
                            turn_maxima(nxt)
                        output(b)

                    for n in range(NG):
                        maxima(0, n)
                    turn_maxima(0)
                    pe.sem_inc(s_pv, 1)
                    rounds(pe, body)


LINKS_B0, LINKS_B = 35, 26


def first_ffn(p):
    nc, a = p.nc, p.a
    with ExitStack() as c:
        sb = lambda n, s, dt=F32: p.sb(n, s, dt, c)
        W12, W3, mean = p.W12, p.W3, p.mean
        am = sb("am", [P, TB])
        qs = sb("qs", [P, 2 * TB])
        sa = sb("sa", [P, 2 * TB])
        q = sb("q", [P, TB, D])
        hq = sb("hq", [P, TB, D], BF16)
        hqT = sb("hqT", [P, KD, S], BF16)
        sil = sb("sil", [P, TB, HID0])
        h = sb("h", [P, TB, HID0])
        hm = sb("hm", [P, TB, 4])
        h2 = sb("h2", [P, TB, HID0], BF16)
        h2T = sb("h2T", [P, TB, HT0, P], BF16)
        G = [p.ps(f"G{t}", [P, 1024], c) for t in range(TB)]
        U = [p.ps(f"U{t}", [P, 1024], c) for t in range(TB)]
        (s_var, s_sd, s_xn, s_dch, s_hq, s_tr, s_hqT, s_a, s_sa, s_sil, s_h2, s_ht, s_h2T, s_y, s_x) = \
            p.sems(c, "var5 sd5 xn5 dch5 hq5 tr5 hqT5 a5 sa5 sil5 h25 ht5 h2T5 y5 x5")
        with nc.Block() as block:
            @block.scalar
            def _(act):
                def turned(b):
                    act.wait_ge(s_tr, b + 1)
                    act.activation(hqT[:, :, :], G[1][:, 512:768].bitcast(BF16).rearrange("p (k n) -> p k n", k=KD), ACT.Copy).then_inc(s_hqT, 1)

                def silu(b, t):
                    act.wait_ge(s_sa, b + 1)
                    act.wait_ge(s_a, b * TB + t + 1)
                    act.activation(sil[:, t, :], G[t][:, 0:HID0], ACT.Silu, scale=sa[:, 2 * t:2 * t + 1]).then_inc(s_sil, 1)

                def hidden_turned(b, t):
                    act.wait_ge(s_ht, b * TB + t + 1)
                    src = G[t][:, 0:HT0 * 64].bitcast(BF16).rearrange("p (k n) -> p k n", n=P)
                    act.activation(h2T[:, t, 0:HT0 - 1, :], src[:, 0:HT0 - 1, :], ACT.Copy)
                    act.activation(h2T[0:64, t, HT0 - 1, :], src[0:64, HT0 - 1, :], ACT.Copy).then_inc(s_h2T, 1)

                def body(b, nxt):
                    hidden_turned(b, 0)
                    if nxt is not None:
                        turned(nxt)
                        silu(nxt, 0)
                    hidden_turned(b, 1)
                    if nxt is not None:
                        silu(nxt, 1)

                norm_roots(p, act, s_var, s_sd)
                turned(0)
                silu(0, 0)
                silu(0, 1)
                rounds(act, body)

            @block.vector
            def _(v):
                xt = lambda b, t: p.X[:, ds(2 * b + t, 1), :].rearrange("p o n -> p (o n)")

                def front(b, ch):
                    normalise(p, v, b, ch, s_xn)
                    v.wait_ge(s_xn, b + 1)
                    ch.wait()
                    ch.link(v.tensor_reduce(am[:, :], p.xn[:, :, :], AX.X, ALU.max, apply_absolute_value=True))
                    ch.link(v.tensor_scalar(am[:, :], am[:, :], 1e-5, None, ALU.max))
                    ch.link(v.reciprocal(qs[:, 0:TB], am[:, :]))
                    ch.link(v.tensor_scalar(qs[:, 0:TB], qs[:, 0:TB], 127.0, None, ALU.mult))
                    ch.link(v.tensor_scalar(qs[:, TB:2 * TB], am[:, :], 1.0 / 127.0, None, ALU.mult))

                def integers(b, ch):
                    for t in range(TB):
                        ch.add(v.tensor_scalar(q[:, t, :], p.xn[:, t, :], qs[:, t:t + 1], -128.0, ALU.mult, ALU.max))
                    ch.wait()
                    ch.link(v.tensor_scalar(q[:, :, :], q[:, :, :], 127.0, MAGIC, ALU.min, ALU.add))
                    v.tensor_scalar(hq[:, :, :], q[:, :, :], MAGIC, None, ALU.subtract).then_inc(s_hq, 1)

                def scales(b, ch):
                    ch.add(v.tensor_scalar(sa[:, 0:2 * TB:2], qs[:, TB:2 * TB], mean[:, 0:1], None, ALU.mult))
                    v.tensor_scalar(sa[:, 1:2 * TB:2], qs[:, TB:2 * TB], mean[:, 1:2], None, ALU.mult).then_inc(s_sa, 1)
                    v.wait_ge(s_sa, b + 1)

                def hidden(b, t, nxt, ch):
                    v.wait_ge(s_sil, b * TB + t + 1)
                    ch.link(v.scalar_tensor_tensor(h[:, t, :], U[t][:, 0:HID0], sa[:, 2 * t + 1:2 * t + 2], sil[:, t, :], ALU.mult, ALU.mult))
                    if t == TB - 1 and nxt is not None:
                        scales(nxt, ch)
                    ch.link(v.tensor_reduce(hm[:, t, 0:1], h[:, t, :], AX.X, ALU.max, apply_absolute_value=True))
                    ch.link(v.tensor_scalar(hm[:, t, 0:1], hm[:, t, 0:1], 1e-5, None, ALU.max))
                    ch.link(v.reciprocal(hm[:, t, 1:2], hm[:, t, 0:1]))
                    ch.add(v.tensor_scalar(hm[:, t, 2:3], hm[:, t, 1:2], 127.0, None, ALU.mult))
                    ch.link(v.tensor_scalar(hm[:, t, 3:4], hm[:, t, 0:1], 1.0 / 127.0, mean[:, 2:3], ALU.mult, ALU.mult))
                    ch.link(v.tensor_scalar(h[:, t, :], h[:, t, :], hm[:, t, 2:3], -128.0, ALU.mult, ALU.max))
                    ch.link(v.tensor_scalar(h[:, t, :], h[:, t, :], 127.0, MAGIC, ALU.min, ALU.add))
                    v.tensor_scalar(h2[:, t, :], h[:, t, :], MAGIC, None, ALU.subtract).then_inc(s_h2, 1)

                def add_result(b, t):
                    v.wait_ge(s_y, b * TB + t + 1)
                    v.scalar_tensor_tensor(xt(b, t), U[t][:, 0:D], hm[:, t, 3:4], xt(b, t), ALU.mult, ALU.add).then_inc(s_x, 1)

                def body(b, nxt):
                    ch = Chain(v, s_dch, b, LINKS_B, LINKS_B0)
                    if nxt is not None:
                        front(nxt, ch)
                        v.wait_ge(s_tr, b + 1)
                        integers(nxt, ch)
                    add_result(b, 0)
                    hidden(b, 1, nxt, ch)
                    if nxt is not None:
                        hidden(nxt, 0, None, ch)
                        ch.done()
                    add_result(b, 1)

                first = Chain(v, s_dch, 0, LINKS_B0)
                norm_stats(p, v, first, s_var, s_sd)
                front(0, first)
                integers(0, first)
                scales(0, first)
                hidden(0, 0, None, first)
                first.done()
                rounds(v, body)

            @block.tensor
            def _(pe):
                def turn(b):
                    pe.wait_ge(s_hq, b + 1)
                    gb = G[1][:, 512:768].bitcast(BF16)
                    for k in range(KD):
                        for t in range(TB):
                            mm = pe.transpose(gb[:, k * S + t * P:k * S + (t + 1) * P], hq[:, t, k * P:(k + 1) * P], p.identb[:, :])
                    mm.then_inc(s_tr, 1)

                def up(b, t):
                    for o, dst in ((0, G[t]), (HID0, U[t])):
                        for n0, n1 in ((0, 512), (512, HID0)):
                            for k in range(KD):
                                mm = pe.matmul(dst[:, n0:n1], hqT[:, k, t * P:(t + 1) * P], W12[:, k, o + n0:o + n1],
                                               start=(k == 0), stop=(k == KD - 1))
                    mm.then_inc(s_a, 1)

                def down(b, t):
                    pe.wait_ge(s_h2, b * TB + t + 1)
                    gb = G[t][:, 0:HT0 * 64].bitcast(BF16)
                    for k in range(HT0):
                        n = min(P, HID0 - k * P)
                        mm = pe.transpose(gb[0:n, k * P:(k + 1) * P], h2[:, t, k * P:k * P + n], p.identb[:, :])
                    mm.then_inc(s_ht, 1)
                    pe.wait_ge(s_h2T, b * TB + t + 1)
                    for k in range(HT0):
                        n = min(P, HID0 - k * P)
                        mm = pe.matmul(U[t][:, 0:D], h2T[0:n, t, k, :], W3[0:n, k, :], start=(k == 0), stop=(k == HT0 - 1))
                    mm.then_inc(s_y, 1)

                def body(b, nxt):
                    down(b, 0)
                    if nxt is not None:
                        pe.wait_ge(s_sil, b * TB + TB)
                        turn(nxt)
                        pe.wait_ge(s_hqT, nxt + 1)
                        pe.wait_ge(s_x, b * TB + 1)
                        up(nxt, 0)
                    down(b, 1)
                    if nxt is not None:
                        pe.wait_ge(s_x, b * TB + 2)
                        up(nxt, 1)

                turn(0)
                pe.wait_ge(s_hqT, 1)
                up(0, 0)
                up(0, 1)
                rounds(pe, body)


LINKS_C0, LINKS_C = 35, 83
LINKS_D0, LINKS_D = 15, 26


def second_attention(p):
    nc, a = p.nc, p.a
    NH = H1 + 2 * KV1
    CHUNKS = ("k", "kc", "v", "vc", "q0", "q1", "q2", "q3")
    with ExitStack() as c:
        sb = lambda n, s, dt=F32: p.sb(n, s, dt, c)
        CQ = sb("CQ", [P, TB, HD1])
        SQ = sb("SQ", [P, TB, HD1])
        CK = sb("CK", [P, TB, HD1])
        SK = sb("SK", [P, TB, HD1])
        WR = sb("WR", [P, 2, HD1])
        hT = sb("hT", [P, 2, KD, S], BF16)
        R = sb("R", [P, 3, CH])
        R2 = sb("R2", [P, CH])
        ssq = sb("ssq", [P, TB, NH])
        rms = sb("rms", [P, TB, NH])
        rk = sb("rk", [P, TB, NH])
        qT = sb("qT", [P, 2, H1, S], BF16)
        kT = sb("kT", [P, 2, KV1, T1 + S], BF16)
        V = sb("V", [P, 2, 4, KV1 * HD1], BF16)
        nm = sb("nm", [P, 2, 4])
        bias = sb("bias", [P, 2, 4])
        sm = sb("sm", [P, 2, 4])
        rs = sb("rs", [P, 2, 4])
        Pr = sb("Pr", [P, 2, REP1, 512])
        junk = Pr[:, 0, :, 0:HD1]
        raw = sb("rawC", [P, 2, HID1])
        PTs = sb("PTs", [P, 2, 4, 512], BF16)
        OT = sb("OT1", [P, 2, H1, S], BF16)
        bank = [p.ps(f"c{i}", [P, 512], c) for i in range(8)]
        mask = sb("mask1", [P, P], BF16)

        rope = p.sb("rope", [P, TB, 4, 64], F32, c)
        qkw = p.sb("qkw", [1, 2 * HD1], F32, c)
        (s_w, s_wr, s_r, s_t, s_m, s_var, s_sd, s_ln) = p.sems(c, "w6 wr6 r6 t6 m6 var6 sd6 ln6")
        NU = KV1 * TB
        KTS = [2 + 1 + u % TB for u in range(NU)]
        EV = sum(KTS)
        FIRST = [sum(KTS[:u]) for u in range(NU)]
        (s_xn, s_dch, s_tr, s_hhi, s_hlo, s_pj, s_sq, s_vhi, s_vev, s_pf, s_rt, s_ro, s_rT, s_rhi, s_rlo,
         s_s, s_nb, s_e, s_p, s_kT, s_evA, s_evD, s_pvk, s_ohi, s_olo, s_y, s_x) = \
            p.sems(c, "xn7 dch7 tr7 hhi7 hlo7 pj7 sq7 vhi7 vev7 pf7 rt7 ro7 rT7 rhi7 rlo7 "
                      "s7 nb7 e7 p7 kT7 evA7 evD7 pvk7 ohi7 olo7 y7 x7")
        ROT = [ch for ch in CHUNKS if ch[0] != "v"]
        NR = len(ROT) * TB
        head0 = {"k": 0, "kc": KV1, "q0": 2 * KV1, "q1": 3 * KV1, "q2": 4 * KV1, "q3": 5 * KV1}
        steps = [(t, ch) for t in range(TB) for ch in CHUNKS]
        rsteps = [(t, ch) for t, ch in steps if ch[0] != "v"]

        def place(t, ch, part):
            if ch == "k":
                return kT[:, part, :, T1 + t * P:T1 + (t + 1) * P]
            if ch == "kc":
                return kT[:, part, :, t * P:(t + 1) * P]
            h = REP1 * int(ch[1])
            return qT[:, part, h:h + REP1, t * P:(t + 1) * P]

        with nc.Block() as block:
            @block.sync
            def _(sp):
                sp.dma_start(rope[:, :, :, :], a["rope"]).then_inc(s_w, 16)
                sp.dma_start(qkw[:, :], a["qkw"]).then_inc(s_w, 16)

            @block.gpsimd
            def _(g):
                g.memset(mask[:, :], 0.0).then_inc(s_m, 1)
                g.wait_ge(s_m, 1)
                g.affine_select(out=mask[:, :], in_=mask[:, :], compare_op=ALU.is_ge, fill=NEG, base=0,
                                pattern=[[-1, P]], channel_multiplier=1).then_inc(s_m, 1)
                chunks = []
                for k in range(KD):
                    for w in range(2):
                        chunks.append((a["base_gu"][k * P:(k + 1) * P, w * HID1:(w + 1) * HID1], p.WG[:, 0, k, w, :], p.WG[:, 1, k, w, :],
                                       lambda r: r[:, 0:HID1]))
                for w in range(2):
                    for t in range(ET1):
                        r0 = (w * ET1 + t) * P
                        chunks.append((a["gu_B"][r0:r0 + P, :], p.WB[:, 0, w, t, :], p.WB[:, 1, w, t, :], lambda r: r[:, 0:HID1]))
                split_weights(p, g, chunks, raw)


            @block.scalar
            def _(act):
                def turned(b):
                    act.wait_ge(s_tr, b + 1)
                    act.activation(hT[:, 0, :, :], bank[0][:, :].rearrange("p (k n) -> p k n", k=KD), ACT.Copy).then_inc(s_hhi, 1)

                def project(b):
                    def hi_of(n):
                        t, ch = rsteps[n]
                        act.wait_ge(s_rT, b * NR + n + 1)
                        act.activation(place(t, ch, 0), bank[5 + n % 2][:, :].rearrange("p (h n) -> p h n", h=4), ACT.Copy).then_inc(s_rhi, 1)

                    r = 0
                    for n, (t, ch) in enumerate(steps):
                        act.wait_ge(s_pj, b * len(steps) + n + 1)
                        bk = bank[1 + n % 4]
                        if ch[0] == "v":
                            act.activation(V[:, 0, (2 if ch == "v" else 0) + t, :], bk[:, :], ACT.Copy).then_inc(s_vhi, 1)
                            continue
                        h0 = head0[ch]
                        for h in range(4):
                            ins = act.activation(junk[:, h, :], bk[:, h * HD1:(h + 1) * HD1], ACT.Square, accum_out=ssq[:, t, h0 + h:h0 + h + 1])
                        ins.then_inc(s_sq, 1)
                        act.wait_ge(s_sq, b * NR + r + 1)
                        if ch[0] == "k":
                            act.activation(rms[:, t, h0:h0 + 4], ssq[:, t, h0:h0 + 4], ACT.Sqrt, bias=p.eps[:, 2:3], scale=1.0 / HD1).then_inc(s_rt, 1)
                        else:
                            act.activation(rms[:, t, h0:h0 + 4], ssq[:, t, h0:h0 + 4], ACT.Sqrt, bias=p.eps[:, 1:2]).then_inc(s_rt, 1)
                        r += 1
                        if r >= 3:
                            hi_of(r - 3)
                    hi_of(NR - 2)
                    hi_of(NR - 1)

                def attend(b, nxt):
                    def exps(u, s):
                        g, t = u // TB, u % TB
                        w = 2 * u + s
                        nk = KTS[u] * P
                        act.wait_ge(s_nb, b * 2 * NU + w + 1)
                        for i in range(2):
                            h = 2 * s + i
                            ins = act.activation(Pr[:, u % 2, h, 0:nk], bank[2 * s + i][:, 0:nk], ACT.Exp, bias=bias[:, u % 2, h:h + 1],
                                                 scale=rk[:, t, 2 * KV1 + REP1 * g + h:2 * KV1 + REP1 * g + h + 1], accum_out=sm[:, u % 2, h:h + 1])
                        ins.then_inc(s_e, 1)

                    def evac(u, k):
                        i = FIRST[u] + k
                        if k < KTS[u]:
                            act.wait_ge(s_kT, b * EV + i + 1)
                            act.wait_ge(s_pvk, b * EV + i + 1)
                            act.activation(PTs[:, 0, i % 4, :], bank[4 + i % 3][:, :], ACT.Copy).then_inc(s_evA, 1)

                    exps(0, 0)
                    exps(0, 1)
                    for u in range(NU):
                        evac(u, 0)
                        evac(u, 1)
                        if u + 1 < NU:
                            exps(u + 1, 0)
                        if u == NU - 1 and nxt is not None:
                            turned(nxt)
                        evac(u, 2)
                        evac(u, 3)
                        if u + 1 < NU:
                            exps(u + 1, 1)
                        g, t = u // TB, u % TB
                        act.wait_ge(s_pvk, b * EV + FIRST[u] + KTS[u] + 4)
                        act.activation(OT[:, 0, REP1 * g:REP1 * g + REP1, t * P:(t + 1) * P],
                                       bank[7][:, :].rearrange("p (h n) -> p h n", h=4), ACT.Copy).then_inc(s_ohi, 1)

                def body(b, nxt):
                    attend(b, nxt)
                    if nxt is not None:
                        project(nxt)

                act.sem_inc(s_e, 2)
                norm_roots(p, act, s_var, s_sd)
                turned(0)
                project(0)
                rounds(act, body)

            @block.vector
            def _(v):
                def turned(b):
                    v.wait_ge(s_hhi, b + 1)
                    v.tensor_tensor(hT[:, 1, :, :], bank[0][:, :].rearrange("p (k n) -> p k n", k=KD), hT[:, 0, :, :], ALU.subtract).then_inc(s_hlo, 1)

                def add_result(b):
                    v.wait_ge(s_y, b + 1)
                    x = p.X[:, ds(2 * b, TB), :]
                    v.tensor_tensor(x, bank[7][:, :].rearrange("p (t d) -> p t d", t=TB), x, ALU.add).then_inc(s_x, 1)

                def project(b, prev, ch_):
                    def lo_of(n):
                        t, ch = rsteps[n]
                        v.wait_ge(s_rhi, b * NR + n + 1)
                        v.tensor_tensor(place(t, ch, 1), bank[5 + n % 2][:, :].rearrange("p (h n) -> p h n", h=4), place(t, ch, 0), ALU.subtract).then_inc(s_rlo, 1)

                    r = nv = 0
                    for n, (t, ch) in enumerate(steps):
                        if ch[0] == "v":
                            nv += 1
                            row = (2 if ch == "v" else 0) + t
                            v.wait_ge(s_vhi, b * 2 * TB + nv)
                            v.tensor_tensor(V[:, 1, row, :], bank[1 + n % 4][:, :], V[:, 0, row, :], ALU.subtract).then_inc(s_vev, 1)
                            continue
                        bk = bank[1 + n % 4][:, :].rearrange("p (h a n) -> p h a n", h=4, a=2)
                        bf = bank[1 + n % 4][:, :].rearrange("p (h n) -> p h n", h=4)
                        h0 = head0[ch]
                        Rf = R[:, r % 3, :].rearrange("p (h n) -> p h n", h=4)
                        R2h = R2[:, :].rearrange("p (h a n) -> p h a n", h=4, a=2)
                        v.wait_ge(s_sq, b * NR + r + 1)
                        full = lambda tab: tab.rearrange("p (o n) -> p o n", o=1).broadcast_to([P, 4, tab.shape[-1]])
                        if ch == "kc":
                            ch_.add(v.tensor_tensor(Rf, bf, full(WR[:, 1, :]), ALU.mult))
                        else:
                            C_, S_ = (CK, SK) if ch == "k" else (CQ, SQ)
                            ch_.add(v.tensor_tensor(Rf, bf, full(C_[:, t, :]), ALU.mult))
                            ch_.add(v.tensor_tensor(R2h[:, :, 0, :], bk[:, :, 1, :], full(S_[:, t, 0:64]), ALU.mult))
                            ch_.add(v.tensor_tensor(R2h[:, :, 1, :], bk[:, :, 0, :], full(S_[:, t, 64:128]), ALU.mult))
                        v.wait_ge(s_rt, b * NR + r + 1)
                        ins = v.reciprocal(rk[:, t, h0:h0 + 4], rms[:, t, h0:h0 + 4])
                        ins.then_inc(s_pf, 1)
                        ch_.wait()
                        if ch == "k":
                            ch_.link(v.tensor_tensor(R[:, r % 3, :], R[:, r % 3, :], R2[:, :], ALU.add))
                        if ch[0] == "k":
                            v.wait_ge(s_pf, b * NR + r + 1)
                            v.tensor_tensor(Rf, Rf, rk[:, t, h0:h0 + 4].rearrange("p (h o) -> p h o", o=1).broadcast_to([P, 4, HD1]), ALU.mult).then_inc(s_ro, 1)
                        else:
                            v.tensor_tensor(R[:, r % 3, :], R[:, r % 3, :], R2[:, :], ALU.add).then_inc(s_ro, 1)
                        r += 1
                        if r >= 3:
                            lo_of(r - 3)
                        v.wait_ge(s_ro, b * NR + r)
                    lo_of(NR - 2)
                    lo_of(NR - 1)
                    if prev is not None:
                        add_result(prev)

                def attend(b, nxt, ch_):
                    def maxima(u, s):
                        g, t = u // TB, u % TB
                        w = 2 * u + s
                        nk = KTS[u] * P
                        v.wait_ge(s_s, b * 2 * NU + w + 1)
                        for i in range(2):
                            ch_.add(v.tensor_reduce(nm[:, u % 2, 2 * s + i:2 * s + i + 1], bank[2 * s + i][:, 0:nk], AX.X, ALU.max, negate=True))
                        ch_.wait()
                        h = 2 * KV1 + REP1 * g + 2 * s
                        v.tensor_tensor(bias[:, u % 2, 2 * s:2 * s + 2], nm[:, u % 2, 2 * s:2 * s + 2], rk[:, t, h:h + 2], ALU.mult).then_inc(s_nb, 1)

                    def norms(u, s):
                        nk = KTS[u] * P
                        v.wait_ge(s_e, b * 2 * NU + 2 * u + s + 3)
                        ch_.link(v.reciprocal(rs[:, u % 2, 2 * s:2 * s + 2], sm[:, u % 2, 2 * s:2 * s + 2]))
                        for h in (2 * s, 2 * s + 1):
                            v.tensor_scalar(Pr[:, u % 2, h, 0:nk], Pr[:, u % 2, h, 0:nk], rs[:, u % 2, h:h + 1], None, ALU.mult).then_inc(s_p, 1)

                    def evac(u, k):
                        i = FIRST[u] + k
                        if k < KTS[u]:
                            v.wait_ge(s_evA, b * EV + i + 1)
                            v.tensor_tensor(PTs[:, 1, i % 4, :], bank[4 + i % 3][:, :], PTs[:, 0, i % 4, :], ALU.subtract).then_inc(s_evD, 1)

                    maxima(0, 0)
                    maxima(0, 1)
                    norms(0, 0)
                    norms(0, 1)
                    for u in range(NU):
                        g, t = u // TB, u % TB
                        evac(u, 0)
                        if u + 1 < NU:
                            maxima(u + 1, 0)
                        evac(u, 1)
                        if u + 1 < NU:
                            maxima(u + 1, 1)
                        if u + 1 < NU:
                            norms(u + 1, 0)
                        if u == NU - 1 and nxt is not None:
                            turned(nxt)
                        evac(u, 2)
                        evac(u, 3)
                        if u + 1 < NU:
                            norms(u + 1, 1)
                        v.wait_ge(s_ohi, b * NU + u + 1)
                        hd = slice(REP1 * g, REP1 * g + REP1)
                        v.tensor_tensor(OT[:, 1, hd, t * P:(t + 1) * P], bank[7][:, :].rearrange("p (h n) -> p h n", h=4),
                                        OT[:, 0, hd, t * P:(t + 1) * P], ALU.subtract).then_inc(s_olo, 1)
                        if u == NU - 2 and nxt is not None:
                            normalise(p, v, nxt, ch_, s_xn)

                def body(b, nxt):
                    ch_ = Chain(v, s_dch, b, LINKS_C, LINKS_C0)
                    attend(b, nxt, ch_)
                    if nxt is not None:
                        project(nxt, b, ch_)
                        ch_.done()
                    else:
                        add_result(b)

                v.sem_inc(s_evD, 3)
                v.sem_inc(s_x, 1)
                first = Chain(v, s_dch, 0, LINKS_C0)
                norm_stats(p, v, Chain(v, s_ln, 0, 0), s_var, s_sd)
                normalise(p, v, 0, first, s_xn)
                turned(0)
                v.wait_ge(s_wr, 1)
                v.tensor_copy(WR[:, :, :], bank[7][:, :].rearrange("p (w n) -> p w n", w=4)[:, 0:2, :]).then_inc(s_r, 1)
                v.wait_ge(s_r, 1)
                for w, C_, S_ in ((1, CK, SK), (0, CQ, SQ)):
                    for t in range(TB):
                        v.tensor_tensor(C_[:, t, :], rope[:, t, 0:2, :].rearrange("p a n -> p (a n)"), WR[:, w, :], ALU.mult).then_inc(s_t, 1)
                        v.tensor_tensor(S_[:, t, 0:64], rope[:, t, 2, :], WR[:, w, 64:128], ALU.mult).then_inc(s_t, 1)
                        v.tensor_tensor(S_[:, t, 64:128], rope[:, t, 3, :], WR[:, w, 0:64], ALU.mult).then_inc(s_t, 1)
                v.wait_ge(s_t, 6 * TB)
                project(0, None, first)
                first.done()
                rounds(v, body)

            @block.tensor
            def _(pe):
                def turned(b):
                    pe.wait_ge(s_xn, b + 1)
                    for k in range(KD):
                        for t in range(TB):
                            mm = pe.transpose(bank[0][:, k * S + t * P:k * S + (t + 1) * P], p.xn[:, t, k * P:(k + 1) * P], p.identf[:, :])
                    mm.then_inc(s_tr, 1)

                WO_TERMS = [(t, x, w, h) for t in range(TB) for x, w in ((0, 0), (0, 1), (1, 0)) for h in range(H1)]

                def output(b, n0, n1):
                    half = len(WO_TERMS) // TB
                    for n in range(n0, n1):
                        t, x, w, h = WO_TERMS[n]
                        mm = pe.matmul(bank[7][:, t * D:(t + 1) * D], OT[:, x, h, t * P:(t + 1) * P], p.WO[:, w, h, :],
                                       start=(n % half == 0), stop=(n % half == half - 1))
                        if n == len(WO_TERMS) - 1:
                            mm.then_inc(s_y, 1)

                def project(b, prev):
                    def turn(n):
                        pe.wait_ge(s_ro, b * NR + n + 1)
                        if n >= 2:
                            pe.wait_ge(s_rlo, b * NR + n - 1)
                        for h in range(4):
                            mm = pe.transpose(bank[5 + n % 2][:, h * P:(h + 1) * P], R[:, n % 3, h * HD1:(h + 1) * HD1], p.identf[:, :])
                        mm.then_inc(s_rT, 1)

                    r = nv = 0
                    used = {}
                    for n, (t, ch) in enumerate(steps):
                        if n == 0:
                            pe.wait_ge(s_hlo, b + 1)
                        if n % 4 in used:
                            sem, per, cnt = used[n % 4]
                            pe.wait_ge(sem, b * per + cnt)
                        if ch[-1] == "c":
                            act_ = lambda part, k: p.CTS[:, part, k, ds(b * S + t * P, P)]
                        else:
                            act_ = lambda part, k: hT[:, part, k, t * P:(t + 1) * P]
                        if ch[0] == "q":
                            w_ = lambda part, k: p.WQ[:, part, k, int(ch[1]) * CH:(int(ch[1]) + 1) * CH]
                        else:
                            w_ = lambda part, k: p.WKV[:, part, k, int(ch[-1] == "c"), (CH if ch[0] == "v" else 0):(2 * CH if ch[0] == "v" else CH)]
                        terms = [(x, w, k) for x, w in ((0, 0), (0, 1), (1, 0)) for k in range(KD)]
                        for i, (x, w, k) in enumerate(terms):
                            mm = pe.matmul(bank[1 + n % 4][:, :], act_(x, k), w_(w, k), start=(i == 0), stop=(i == len(terms) - 1))
                        mm.then_inc(s_pj, 1)
                        if prev is not None:
                            if n == 0:
                                pe.wait_ge(s_olo, prev * NU + NU)
                            each = len(WO_TERMS) // len(steps)
                            output(prev, n * each, (n + 1) * each)
                        if ch[0] == "v":
                            nv += 1
                            used[n % 4] = (s_vev, 2 * TB, nv)
                        else:
                            r += 1
                            used[n % 4] = (s_pf, NR, r)
                            if r >= 3:
                                turn(r - 3)
                    turn(NR - 2)
                    turn(NR - 1)

                def attend(b, nxt):
                    pe.wait_ge(s_rlo, b * NR + NR)
                    pe.wait_ge(s_vev, b * 2 * TB + 2 * TB)

                    def scores(u, s):
                        g, t = u // TB, u % TB
                        nk = KTS[u] * P
                        pe.wait_ge(s_e, b * 2 * NU + 2 * u + s + 1)
                        for i in range(2):
                            h = REP1 * g + 2 * s + i
                            o = bank[2 * s + i]
                            for n, (x, y) in enumerate(((0, 0), (0, 1), (1, 0))):
                                pe.matmul(o[:, 0:nk], qT[:, x, h, t * P:(t + 1) * P], kT[:, y, g, 0:nk], start=(n == 0), stop=False)
                            mm = pe.matmul(o[:, nk - P:nk], p.identb[:, :], mask[:, :], start=False, stop=True)
                        mm.then_inc(s_s, 1)

                    def spread(u, k):
                        i = FIRST[u] + k
                        pe.wait_ge(s_evD, b * EV + i + 1)
                        for h in range(REP1):
                            if k == 0 and h % 2 == 0:
                                pe.wait_ge(s_p, b * 4 * NU + 4 * u + h + 2)
                            mm = pe.transpose(bank[4 + i % 3][:, h * P:(h + 1) * P], Pr[:, u % 2, h, k * P:(k + 1) * P], p.identf[:, :])
                        mm.then_inc(s_kT, 1)

                    def product(u, k):
                        i = FIRST[u] + k
                        if k == 0 and u >= 1:
                            pe.wait_ge(s_olo, b * NU + u)
                        if k == 0 and u == 0:
                            pe.wait_ge(s_x, b + 1)
                        pe.wait_ge(s_evD, b * EV + i + 4)
                        g = u // TB
                        for n, (x, y) in enumerate(((0, 0), (0, 1), (1, 0))):
                            mm = pe.matmul(bank[7][:, :], V[:, x, k, g * HD1:(g + 1) * HD1], PTs[:, y, i % 4, :],
                                           start=(k == 0 and n == 0), stop=(k == KTS[u] - 1 and n == 2))
                        mm.then_inc(s_pvk, 1)

                    scores(0, 0)
                    scores(0, 1)
                    for u in range(NU):
                        spread(u, 0)
                        if u + 1 < NU:
                            scores(u + 1, 0)
                        spread(u, 1)
                        if u + 1 < NU:
                            scores(u + 1, 1)
                        spread(u, 2)
                        if u == NU - 1 and nxt is not None:
                            turned(nxt)
                        product(u, 0)
                        if 3 < KTS[u]:
                            spread(u, 3)
                        product(u, 1)
                        product(u, 2)
                        if 3 < KTS[u]:
                            product(u, 3)

                def body(b, nxt):
                    attend(b, nxt)
                    if nxt is not None:
                        project(nxt, b)
                    else:
                        pe.wait_ge(s_olo, b * NU + NU)
                        output(b, 0, len(WO_TERMS))

                pe.sem_inc(s_pvk, 4)
                turned(0)
                pe.wait_ge(s_w, 32)
                pe.matmul(bank[7][:, 0:2 * HD1], p.ones1[:, :], qkw[:, :], start=True, stop=True).then_inc(s_wr, 1)
                project(0, None)
                pe.wait_ge(s_m, 2)
                rounds(pe, body)


def expert_weights(p):
    p.WG = p.sb("WG", [P, 2, KD, 2, HID1], BF16)
    p.WB = p.sb("WB", [P, 2, 2, ET1, HID1], BF16)


def second_ffn(p):
    nc, a = p.nc, p.a
    with ExitStack() as c:
        sb = lambda n, s, dt=F32: p.sb(n, s, dt, c)
        p.used = 0
        WA = sb("WA", [P, 2, KD, 2, E1 * R1], BF16)
        WG, WB = p.WG, p.WB
        WDA = p.carve([2, MT1, E1 * R1])
        WD = p.carve([2, MT1, D])
        WDB = p.carve([2, ET1, D])
        raw = sb("rawD", [P, 2, 2048])
        confT = sb("confT", [P, KD, E1])
        confb = sb("confb", [1, E1])
        wealth = sb("wealth", [1, E1])
        worth = sb("worth", [P, E1])
        order = sb("order", [P, E1])
        pick = sb("pick", [18, ET1, 2, P], BF16)
        pickw = sb("pickw", [18, 2, P])
        hf = sb("hf", [P, KD, S])
        hT = sb("hTd", [P, 2, KD, S], BF16)
        conf = sb("conf", [P, TB, E1])
        eq = sb("eq", [P, TB, E1])
        best = sb("best", [P, 4, TB])
        RT = sb("RT", [P, TB, 18])
        RTf = sb("RTf", [18, S])
        RTb = sb("RTb", [18, S], BF16)
        MK = sb("MK", [P, ET1, 2, S], BF16)
        wrep = sb("wrep", [P, 2, S])
        z = p.carve([2, 2, ET1, S])
        zm = p.carve([2, 2, ET1, 2 * S])
        BS = sb("BS", [P, 2, 2, S])
        gl = sb("gl", [P, 2, 2 * S])
        ul = sb("ul", [P, 2, 2 * S])
        sil = sb("silD", [P, 2, 2 * S])
        hw = sb("hw", [P, 2, 2, S])
        hs = sb("hs", [P, 2, S])
        HW = sb("HW", [P, 2, MT1, 2 * S], BF16)
        HS = sb("HS", [P, 2, MT1, S], BF16)
        yt = sb("yt", [P, ET1, 2, S])
        ys = sb("ys", [P, ET1, S])
        YS = p.carve([2, ET1, S])
        bank = [p.ps(f"d{i}", [P, 512], c) for i in range(8)]
        (s_c, s_sel, s_wl, s_wt, s_var, s_sd, s_ln) = p.sems(c, "c8 sel8 wl8 wt8 var8 sd8 ln8")

        (s_xn, s_dch, s_tr, s_hf, s_hhi, s_hlo, s_lg, s_conf, s_diff, s_ex, s_rt, s_rtT, s_rtc, s_zp, s_zhi, s_zlo,
         s_mkp, s_mk, s_wp, s_wrep, s_zm, s_bs, s_bev, s_lo, s_gl, s_ul, s_sil, s_hw, s_hs, s_hwhi, s_hshi, s_hwlo, s_hslo,
         s_yp, s_ys, s_yhi, s_ylo, s_y, s_x, s_out) = \
            p.sems(c, "xn9 dch9 tr9 hf9 hhi9 hlo9 lg9 conf9 diff9 ex9 rt9 rtT9 rtc9 zp9 zhi9 zlo9 mkp9 mk9 wp9 wrep9 zm9 "
                      "bs9 bev9 lo9 gl9 ul9 sil9 hw9 hs9 hwhi9 hshi9 hwlo9 hslo9 yp9 ys9 yhi9 ylo9 y9 x9 out9")
        HAVE_A, HAVE_D, HAVE_DA, HAVE_DB = (p.split + n for n in (1, 3, 5, 6))
        TERMS = ((0, 0), (0, 1), (1, 0))

        with nc.Block() as block:
            @block.gpsimd
            def _(g):
                g.memset(pick[:, :, :, :], 0.0).then_inc(s_sel, 1)
                g.memset(pickw[:, :, :], 0.0).then_inc(s_sel, 1)
                g.wait_ge(s_sel, 2)
                for s in range(2):
                    for t in range(ET1):
                        v = pick[:, t, s, :].rearrange("k (h n) -> k h n", h=2)
                        g.affine_select(out=v, in_=v, compare_op=ALU.not_equal, fill=SCALING, base=-(E1 * s + 2 * t),
                                        pattern=[[-1, 2], [0, R1]], channel_multiplier=1).then_inc(s_sel, 1)
                    g.affine_select(out=pickw[:, s, :], in_=pickw[:, s, :], compare_op=ALU.not_equal, fill=1.0, base=-(2 * E1 + s),
                                    pattern=[[0, P]], channel_multiplier=1).then_inc(s_sel, 1)
                some = lambda m, n: lambda r: r[:, 0:m * n].rearrange("p (m n) -> p m n", m=m)
                rows = lambda t, m0, m: t[m0 * P:(m0 + m) * P, :].rearrange("(m p) n -> p m n", p=P)
                chunks = []
                for w in range(2):
                    chunks.append((rows(a["gu_A"], 0, KD)[:, :, w * E1 * R1:(w + 1) * E1 * R1], WA[:, 0, :, w, :], WA[:, 1, :, w, :], some(KD, E1 * R1)))
                chunks.append((rows(a["base_d"], 0, MT1), WD[:, 0], WD[:, 1], some(MT1, D)))
                for m0, m in ((0, 4), (4, 3)):
                    chunks.append((rows(a["d_A"], m0, m), WDA[:, 0, m0:m0 + m, :], WDA[:, 1, m0:m0 + m, :], some(m, E1 * R1)))
                chunks.append((rows(a["d_B"], 0, ET1), WDB[:, 0], WDB[:, 1], some(ET1, D)))
                split_weights(p, g, chunks, raw)

            @block.sync
            def _(sp):
                sp.dma_start(confT[:, :, :], a["confT"].rearrange("(k p) e -> p k e", p=P)).then_inc(s_c, 16)
                sp.dma_start(confb[:, :], a["confb"]).then_inc(s_c, 16)
                sp.dma_start(wealth[:, :], a["wealth"]).then_inc(s_c, 16)
                with sp.Fori(0, B) as b:
                    sp.wait_ge(s_x, b * TB + TB + 1)
                    sp.dma_start(a["out"].rearrange("(t p) d -> p t d", p=P)[:, ds(b * TB, TB), :], p.X[:, ds(b * TB, TB), :]).then_inc(s_out, 16)
                sp.wait_ge(s_out, 16 * B)

            @block.scalar
            def _(act):
                def route(b):
                    act.wait_ge(s_tr, b + 1)
                    hp = bank[6][:, :].rearrange("p (k n) -> p k n", k=KD)
                    act.activation(hf[:, :, :], hp, ACT.Copy).then_inc(s_hf, 1)
                    act.activation(hT[:, 0, :, :], hp, ACT.Copy).then_inc(s_hhi, 1)
                    act.wait_ge(s_lg, b + 1)
                    act.activation(conf[:, :, :], bank[7][:, 0:TB * E1].rearrange("p (t e) -> p t e", t=TB), ACT.Sigmoid).then_inc(s_conf, 1)
                    act.wait_ge(s_diff, b + 1)
                    act.activation(best[:, 2, :], best[:, 2, :], ACT.Exp).then_inc(s_ex, 1)
                    act.wait_ge(s_rtT, b + 1)
                    act.activation(RTf[:, :], bank[6][0:18, 0:S], ACT.Copy).then_inc(s_rtc, 1)
                    act.activation(RTb[:, :], bank[6][0:18, 0:S], ACT.Copy).then_inc(s_rtc, 1)

                def body(b, nxt):
                    for t in range(ET1):
                        act.wait_ge(s_mkp, b * ET1 + t + 1)
                        act.activation(MK[:, t, :, :], bank[2 + t][:, :].rearrange("p (s n) -> p s n", s=2), ACT.Copy).then_inc(s_mk, 1)
                    for i in range(4):
                        act.wait_ge(s_zp, b * 4 + i + 1)
                        act.activation(z[:, 0, i // 2, 2 * (i % 2):2 * (i % 2) + 2, :], bank[2 + i][:, :].rearrange("p (t n) -> p t n", t=2),
                                       ACT.Copy).then_inc(s_zhi, 1)
                    act.wait_ge(s_wp, b + 1)
                    act.activation(wrep[:, :, :], bank[1][:, :].rearrange("p (s n) -> p s n", s=2), ACT.Copy).then_inc(s_wrep, 1)

                    def base_out(m):
                        act.wait_ge(s_bs, b * MT1 + m + 1)
                        if m >= 2:
                            act.wait_ge(s_ul, b * MT1 + m - 1)
                        act.activation(BS[:, m % 2, :, :], bank[6 + m % 2][:, :].rearrange("p (w n) -> p w n", w=2), ACT.Copy).then_inc(s_bev, 1)

                    def high(m):
                        act.wait_ge(s_hw, b * MT1 + m + 1)
                        act.activation(HW[:, 0, m, :], hw[:, m % 2, :, :].rearrange("p s n -> p (s n)"), ACT.Copy).then_inc(s_hwhi, 1)
                        act.wait_ge(s_hs, b * MT1 + m + 1)
                        act.activation(HS[:, 0, m, :], hs[:, m % 2, :], ACT.Copy).then_inc(s_hshi, 1)

                    base_out(0)
                    for m in range(MT1):
                        if m + 1 < MT1:
                            base_out(m + 1)
                        act.wait_ge(s_gl, b * MT1 + m + 1)
                        act.activation(sil[:, m % 2, :], gl[:, m % 2, :], ACT.Silu).then_inc(s_sil, 1)
                        if m >= 1:
                            high(m - 1)
                    high(MT1 - 1)
                    if nxt is not None:
                        route(nxt)
                    for t in range(ET1):
                        act.wait_ge(s_ys, b * ET1 + t + 1)
                        act.activation(YS[:, 0, t, :], ys[:, t, :], ACT.Copy).then_inc(s_yhi, 1)

                norm_roots(p, act, s_var, s_sd)
                route(0)
                rounds(act, body)

            @block.vector
            def _(v):
                def route(b, ch):
                    v.wait_ge(s_hhi, b + 1)
                    v.tensor_tensor(hT[:, 1, :, :], bank[6][:, :].rearrange("p (k n) -> p k n", k=KD), hT[:, 0, :, :], ALU.subtract).then_inc(s_hlo, 1)
                    v.wait_ge(s_conf, b + 1)
                    row = lambda r: r.rearrange("p (o e) -> p o e", o=1).broadcast_to([P, TB, E1])
                    col = lambda r: r.rearrange("p (t o) -> p t o", o=1).broadcast_to([P, TB, E1])
                    ch.link(v.tensor_tensor(conf[:, :, :], conf[:, :, :], row(worth[:, :]), ALU.mult))
                    for s in range(2):
                        mask = RT[:, :, s * E1:(s + 1) * E1]
                        ch.link(v.tensor_reduce(best[:, s, :], conf[:, :, :], AX.X, ALU.max))
                        ch.link(v.tensor_tensor(eq[:, :, :], conf[:, :, :], col(best[:, s, :]), ALU.is_equal))
                        ch.link(v.tensor_tensor(eq[:, :, :], eq[:, :, :], row(order[:, :]), ALU.mult))
                        ch.link(v.tensor_reduce(best[:, 3, :], eq[:, :, :], AX.X, ALU.min))
                        ch.link(v.tensor_tensor(mask, row(order[:, :]), col(best[:, 3, :]), ALU.is_equal))
                        if s == 0:
                            ch.link(v.scalar_tensor_tensor(conf[:, :, :], mask, -1e38, conf[:, :, :], ALU.mult, ALU.add))
                    v.tensor_tensor(best[:, 2, :], best[:, 1, :], best[:, 0, :], ALU.subtract).then_inc(s_diff, 1)
                    v.wait_ge(s_ex, b + 1)
                    ch.link(v.tensor_scalar(best[:, 3, :], best[:, 2, :], 1.0, None, ALU.add))
                    ch.link(v.reciprocal(RT[:, :, 16], best[:, 3, :]))
                    v.tensor_tensor(RT[:, :, 17], RT[:, :, 16], best[:, 2, :], ALU.mult).then_inc(s_rt, 1)

                def body(b, nxt):
                    ch = Chain(v, s_dch, b, LINKS_D, LINKS_D0)
                    xt = lambda t: p.X[:, ds(2 * b + t, 1), :].rearrange("p o n -> p (o n)")
                    v.wait_ge(s_mk, b * ET1 + ET1)
                    for w in range(2):
                        for i in (2 * w, 2 * w + 1):
                            v.wait_ge(s_zhi, b * 4 + i + 1)
                            tt = slice(2 * (i % 2), 2 * (i % 2) + 2)
                            v.tensor_tensor(z[:, 1, w, tt, :], bank[2 + i][:, :].rearrange("p (t n) -> p t n", t=2), z[:, 0, w, tt, :],
                                            ALU.subtract).then_inc(s_zlo, 1)
                        v.wait_ge(s_zlo, b * 4 + 2 * w + 2)
                        for x in range(2):
                            v.tensor_tensor(zm[:, x, w, :, :].rearrange("p t (s n) -> p t s n", s=2),
                                            z[:, x, w, :, :].rearrange("p t (o n) -> p t o n", o=1).broadcast_to([P, ET1, 2, S]),
                                            MK[:, :, :, :], ALU.mult).then_inc(s_zm, 1)
                    v.wait_ge(s_wrep, b + 1)

                    def adds(m):
                        v.wait_ge(s_bev, b * MT1 + m + 1)
                        for w, dst, s_done in ((0, gl, s_gl), (1, ul, s_ul)):
                            v.wait_ge(s_lo, b * 2 * MT1 + 2 * m + w + 1)
                            v.tensor_tensor(dst[:, m % 2, :].rearrange("p (s n) -> p s n", s=2),
                                            bank[2 + 2 * (m % 2) + w][:, :].rearrange("p (s n) -> p s n", s=2),
                                            BS[:, m % 2, w:w + 1, :].broadcast_to([P, 2, S]), ALU.add).then_inc(s_done, 1)

                    def finish(m):
                        v.wait_ge(s_sil, b * MT1 + m + 1)
                        v.wait_ge(s_ul, b * MT1 + m + 1)
                        hm = hw[:, m % 2, :, :]
                        ch.link(v.tensor_tensor(hm.rearrange("p s n -> p (s n)"), sil[:, m % 2, :], ul[:, m % 2, :], ALU.mult))
                        v.tensor_tensor(hm, hm, wrep[:, :, :], ALU.mult).then_inc(s_hw, 1)
                        v.wait_ge(s_hw, b * MT1 + m + 1)
                        v.tensor_tensor(hs[:, m % 2, :], hm[:, 0, :], hm[:, 1, :], ALU.add).then_inc(s_hs, 1)
                        v.wait_ge(s_hwhi, b * MT1 + m + 1)
                        v.tensor_tensor(HW[:, 1, m, :], hm.rearrange("p s n -> p (s n)"), HW[:, 0, m, :], ALU.subtract).then_inc(s_hwlo, 1)
                        v.wait_ge(s_hshi, b * MT1 + m + 1)
                        v.tensor_tensor(HS[:, 1, m, :], hs[:, m % 2, :], HS[:, 0, m, :], ALU.subtract).then_inc(s_hslo, 1)
                        v.wait_ge(s_hslo, b * MT1 + m + 1)

                    for m in range(MT1):
                        adds(m)
                        if m >= 1:
                            finish(m - 1)
                        if m == MT1 - 2 and nxt is not None:
                            normalise(p, v, nxt, ch, s_xn)
                    finish(MT1 - 1)
                    if nxt is not None:
                        route(nxt, ch)
                    for t in range(ET1):
                        v.wait_ge(s_yp, b * ET1 + t + 1)
                        ch.link(v.tensor_tensor(yt[:, t, :, :], bank[2 + t][:, :].rearrange("p (s n) -> p s n", s=2), MK[:, t, :, :], ALU.mult))
                        v.tensor_tensor(ys[:, t, :], yt[:, t, 0, :], yt[:, t, 1, :], ALU.add).then_inc(s_ys, 1)
                        v.wait_ge(s_yhi, b * ET1 + t + 1)
                        v.tensor_tensor(YS[:, 1, t, :], ys[:, t, :], YS[:, 0, t, :], ALU.subtract).then_inc(s_ylo, 1)
                    for t in range(TB):
                        v.wait_ge(s_y, b * TB + t + 1)
                        v.tensor_tensor(xt(t), bank[t][:, 0:D], xt(t), ALU.add).then_inc(s_x, 1)
                    if nxt is not None:
                        ch.done()

                v.sem_inc(s_x, 1)
                first = Chain(v, s_dch, 0, LINKS_D0)
                norm_stats(p, v, Chain(v, s_ln, 0, 0), s_var, s_sd)
                normalise(p, v, 0, first, s_xn)
                for e in range(E1):
                    v.memset(order[:, e:e + 1], e - 99.0).then_inc(s_wt, 1)
                v.wait_ge(s_wl, 1)
                v.tensor_copy(worth[:, :], bank[0][:, 0:E1]).then_inc(s_wt, 1)
                v.wait_ge(s_wt, E1 + 1)
                route(0, first)
                first.done()
                rounds(v, body)

            @block.tensor
            def _(pe):
                def turn(b):
                    pe.wait_ge(s_xn, b + 1)
                    for k in range(KD):
                        for t in range(TB):
                            mm = pe.transpose(bank[6][:, k * S + t * P:k * S + (t + 1) * P], p.xn[:, t, k * P:(k + 1) * P], p.identf[:, :])
                    mm.then_inc(s_tr, 1)

                def logits(b):
                    pe.wait_ge(s_hf, b + 1)
                    for t in range(TB):
                        o = bank[7][:, t * E1:(t + 1) * E1]
                        pe.matmul(o, p.ones1[:, :], confb[:, :], start=True, stop=False)
                        for k in range(KD):
                            mm = pe.matmul(o, hf[:, k, t * P:(t + 1) * P], confT[:, k, :], start=False, stop=(k == KD - 1))
                    mm.then_inc(s_lg, 1)

                def turn_routes(b):
                    pe.wait_ge(s_hlo, b + 1)
                    pe.wait_ge(s_rt, b + 1)
                    for t in range(TB):
                        mm = pe.transpose(bank[6][0:18, t * P:(t + 1) * P], RT[:, t, :], p.identf[:, :])
                    mm.then_inc(s_rtT, 1)

                def rank(b):
                    for i in range(4):
                        pe.wait_ge(s_mk, b * ET1 + i + 1)
                        pe.wait_ge(p.weight_split, HAVE_A + i // 2)
                        for j in range(2):
                            n = 2 * i + j
                            w, t = n // ET1, n % ET1
                            for q, (x, y, k) in enumerate([(x, y, k) for x, y in TERMS for k in range(KD)]):
                                mm = pe.matmul(bank[2 + i][:, j * S:(j + 1) * S], WA[:, x, k, w, t * P:(t + 1) * P], hT[:, y, k, :],
                                               start=(q == 0), stop=(q == 5))
                        mm.then_inc(s_zp, 1)

                def base(b, m):
                    if m >= 2:
                        pe.wait_ge(s_bev, b * MT1 + m - 1)
                    for w in range(2):
                        for q, (x, y, k) in enumerate([(x, y, k) for x, y in TERMS for k in range(KD)]):
                            mm = pe.matmul(bank[6 + m % 2][:, w * S:(w + 1) * S], WG[:, x, k, w, m * P:(m + 1) * P], hT[:, y, k, :],
                                           start=(q == 0), stop=(q == 5))
                    mm.then_inc(s_bs, 1)

                def experts(b, m):
                    for w in range(2):
                        if m >= 2:
                            pe.wait_ge((s_gl, s_ul)[w], b * MT1 + m - 1)
                        elif m == 0:
                            pe.wait_ge(s_zm, b * 4 + 2 * w + 2)
                        for q, (x, y, t) in enumerate([(x, y, t) for x, y in TERMS for t in range(ET1)]):
                            mm = pe.matmul(bank[2 + 2 * (m % 2) + w][:, :], WB[:, x, w, t, m * P:(m + 1) * P], zm[:, y, w, t, :],
                                           start=(q == 0), stop=(q == 3 * ET1 - 1))
                        mm.then_inc(s_lo, 1)

                def body(b, nxt):
                    pe.wait_ge(s_rtc, b * 2 + 2)
                    for t in range(ET1):
                        for s in range(2):
                            mm = pe.matmul(bank[2 + t][:, s * S:(s + 1) * S], pick[:, t, s, :], RTb[:, :], start=True, stop=True)
                        mm.then_inc(s_mkp, 1)
                    pe.wait_ge(s_hlo, b + 1)
                    rank(b)
                    pe.wait_ge(s_x, b * TB + 1)
                    for s in range(2):
                        mm = pe.matmul(bank[1][:, s * S:(s + 1) * S], pickw[:, s, :], RTf[:, :], start=True, stop=True)
                    mm.then_inc(s_wp, 1)
                    base(b, 0)
                    base(b, 1)
                    for m in range(MT1):
                        experts(b, m)
                        if m + 2 < MT1:
                            base(b, m + 2)
                    if nxt is not None:
                        pe.wait_ge(s_bev, b * MT1 + MT1)
                        turn(nxt)
                    pe.wait_ge(p.weight_split, HAVE_D)
                    pe.wait_ge(s_wrep, b + 1)
                    for m in range(MT1):
                        pe.wait_ge(s_hslo, b * MT1 + m + 1)
                        for t in range(TB):
                            for q, (x, y) in enumerate(TERMS):
                                pe.matmul(bank[t][:, 0:D], HS[:, x, m, t * P:(t + 1) * P], WD[:, y, m, :], start=(m == 0 and q == 0), stop=False)
                    if nxt is not None:
                        logits(nxt)
                    pe.wait_ge(p.weight_split, HAVE_DA)
                    for t in range(ET1):
                        for m in range(MT1):
                            for q, (x, y) in enumerate(TERMS):
                                mm = pe.matmul(bank[2 + t][:, :], WDA[:, x, m, t * P:(t + 1) * P], HW[:, y, m, :],
                                               start=(m == 0 and q == 0), stop=(m == MT1 - 1 and q == 2))
                        mm.then_inc(s_yp, 1)
                        if t == 1 and nxt is not None:
                            turn_routes(nxt)
                    pe.wait_ge(p.weight_split, HAVE_DB)
                    for t in range(TB):
                        for e in range(ET1):
                            pe.wait_ge(s_ylo, b * ET1 + e + 1)
                            for q, (x, y) in enumerate(TERMS):
                                mm = pe.matmul(bank[t][:, 0:D], YS[:, x, e, t * P:(t + 1) * P], WDB[:, y, e, :], start=False,
                                               stop=(e == ET1 - 1 and q == 2))
                        mm.then_inc(s_y, 1)

                turn(0)
                pe.wait_ge(s_c, 48)
                pe.matmul(bank[0][:, 0:E1], p.ones1[:, :], wealth[:, :], start=True, stop=True).then_inc(s_wl, 1)
                logits(0)
                turn_routes(0)
                pe.wait_ge(s_sel, 2 + 2 * (ET1 + 1))
                rounds(pe, body)


def build(nc, args):
    p = Program(nc, args)
    with p.top:
        setup(p)
        with ExitStack() as c:
            raw_weights(p, c)
            first_attention(p)
            first_ffn(p)
        expert_weights(p)
        second_attention(p)
        second_ffn(p)


def kernel(**inputs):
    import numpy as np
    import concourse.bacc as bacc
    from concourse import mybir
    from concourse.bass_utils import run_bass_kernel_spmd

    f = {k: np.ascontiguousarray(v) for k, v in inputs.items()}
    T = lambda v: np.ascontiguousarray(v.T)
    L = {}
    L["x"] = f["x"].reshape(1024, 256)
    L["ctxT"] = T(f["ctx_2048"].reshape(1024, 256))
    L["mask_tok"] = T(f["mask_BxS2_if1"].reshape(8, 128))
    L["mask_row"] = f["mask_BxS2_if1"].reshape(1, 1024)
    wq = f["L0_xattn_w_q"].reshape(2, 4, 2, 2, 8, 256)
    L["wq0T"] = T(wq.transpose(0, 3, 4, 1, 2, 5).reshape(256, 256))
    L["wk0T"] = T(f["L0_xattn_w_k"].reshape(2, 4, 8, 256).transpose(2, 0, 1, 3).reshape(64, 256))
    L["wv0T"] = T(f["L0_xattn_w_v"])
    L["wo0T"] = np.ascontiguousarray(T(f["L0_xattn_w_o"]).reshape(2, 4, 2, 2, 8, 256).transpose(0, 3, 2, 1, 4, 5).reshape(256, 256))
    L["bo0"] = f["L0_xattn_b_o"].reshape(1, 256)
    L["w12T"] = np.concatenate([T(f["L0_ffn_w1"]), T(f["L0_ffn_w2"])], 1)
    L["w3T"] = np.concatenate([T(f["L0_ffn_w3"]), np.zeros((64, 256), np.float32)], 0)
    L["wq1"] = f["L1_xattn_wq"]
    L["wkv1"] = np.concatenate([f["L1_xattn_wk"], f["L1_xattn_wv"], f["L1_xattn_wk_ctx"], f["L1_xattn_wv_ctx"]], 1)
    L["wo1"] = f["L1_xattn_wo"]
    L["qkw"] = np.concatenate([f["L1_xattn_q_norm_w"], f["L1_xattn_k_norm_w"]]).reshape(1, 256)
    inv = (1.0 / np.float32(10000.0) ** (np.arange(0, 128, 2, dtype=np.float32) / np.float32(128))).astype(np.float32)
    ang = np.outer(np.arange(256, dtype=np.float32), inv).astype(np.float32)
    rope = np.stack([np.cos(ang), np.cos(ang), -np.sin(ang), np.sin(ang)], 1).astype(np.float32)
    L["rope"] = np.ascontiguousarray(rope.reshape(2, 128, 4, 64).transpose(1, 0, 2, 3))
    L["confT"] = T(f["L1_ffn_conf_W"])
    L["confb"] = f["L1_ffn_conf_b"].reshape(1, 8)
    L["wealth"] = f["L1_ffn_expert_wealth"].reshape(1, 8)
    L["base_gu"] = np.concatenate([f["L1_ffn_base_gate"], f["L1_ffn_base_up"]], 1)
    A = lambda n: f[n].transpose(1, 0, 2).reshape(f[n].shape[1], 512)
    L["gu_A"] = np.concatenate([A("L1_ffn_gate_A"), A("L1_ffn_up_A")], 1)
    L["gu_B"] = np.concatenate([f["L1_ffn_gate_B"].reshape(512, 896), f["L1_ffn_up_B"].reshape(512, 896)], 0)
    L["d_A"] = A("L1_ffn_down_A")
    L["base_d"] = f["L1_ffn_base_down"]
    L["d_B"] = f["L1_ffn_down_B"].reshape(512, 256)

    nc = bacc.Bacc("TRN2", target_bir_lowering=False, num_devices=1)
    arrays, args = {}, {}
    for name, v in L.items():
        v = np.ascontiguousarray(v)
        arrays[name + "_in"] = v
        args[name] = nc.dram_tensor(name + "_in", v.shape, mybir.dt.from_np(v.dtype), kind="ExternalInput").ap()
    args["out"] = nc.dram_tensor("out", (1024, 256), mybir.dt.float32, kind="ExternalOutput").ap()
    build(nc, args)
    r = run_bass_kernel_spmd(nc, [arrays], core_ids=[0])
    return r.results[0]["out"].reshape(4, 256, 256)
```
